# Optimizing a Trainium2 kernel written in Bass

```python
import numpy as np
import jax
import jax.numpy as jnp

def _softmax(x, axis=-1):
    return jax.nn.softmax(x, axis=axis)

def _gelu(x):
    return jax.nn.gelu(x, approximate=True)

def _silu(x):
    return jax.nn.silu(x)

def _sigmoid(x):
    return jax.nn.sigmoid(x)

def _layernorm(x, axis=-1, eps=1e-05):
    m = jnp.mean(x, axis=axis, keepdims=True)
    v = jnp.var(x, axis=axis, keepdims=True)
    return (x - m) / jnp.sqrt(v + eps)

def _scatter_add(tgt, idx, src, axis=0):
    return tgt.at[idx].add(src)

def _segment_sum(src, seg, n):
    return jax.ops.segment_sum(src, seg, n)
kernel_name = 'mk_gnn_resnorm_d4_gnn_r8_4f521a'

def setup_inputs(seed: int=0):
    np.random.seed(seed)
    _w = jnp.asarray

    def _rec_inputs():
        import jax
        import jax.numpy as jnp
        _gk = jax.random.key(seed)
        x = -0.000202 + 1 * jax.random.normal(jax.random.fold_in(_gk, 1), (12500, 64), jnp.float32)
        src = jax.random.randint(jax.random.fold_in(_gk, 2), (200000,), 0, 12500, jnp.int32)
        dst = jax.random.randint(jax.random.fold_in(_gk, 3), (200000,), 0, 12500, jnp.int32)
        _o = jnp.argsort(dst, stable=True)
        src = src[_o]
        dst = dst[_o]
        edge_attr_16 = 0.000196303 + 1.00016 * jax.random.normal(jax.random.fold_in(_gk, 11), (200000, 16), jnp.float32)
        edge_attr_64 = -9.77346e-05 + 0.999888 * jax.random.normal(jax.random.fold_in(_gk, 12), (200000, 64), jnp.float32)
        return (x, src, dst, edge_attr_16, edge_attr_64)
    x, src, dst, edge_attr_16, edge_attr_64 = _rec_inputs()

    def _L0_gnn_setup():
        import jax, jax.numpy as jnp
        import numpy as np
        N_NODES = 12500
        N_EDGES = 200000
        D_IN = 64
        D_OUT = 64
        EDGE_DIM = 16
        key = jax.random.key(seed)
        ks = jax.random.split(key, 6)
        x = jax.random.normal(ks[0], (N_NODES, D_IN), dtype=jnp.float32)
        edge_index = jax.random.randint(ks[1], (2, N_EDGES), 0, N_NODES, dtype=jnp.int64)
        edge_feature = jax.random.normal(ks[2], (N_EDGES, EDGE_DIM), dtype=jnp.float32)
        W_edge = jax.random.normal(ks[3], (EDGE_DIM, 1), dtype=jnp.float32) * (1.0 / np.sqrt(EDGE_DIM))
        b_edge = jnp.zeros((1,), dtype=jnp.float32)
        W_node = jax.random.normal(ks[4], (D_OUT, D_IN), dtype=jnp.float32) * (1.0 / np.sqrt(D_IN))
        b_node = jnp.zeros((D_OUT,), dtype=jnp.float32)
        return {'x': x, 'edge_index': edge_index, 'edge_feature': edge_feature, 'W_edge': W_edge, 'b_edge': b_edge, 'W_node': W_node, 'b_node': b_node}
    _L0_gnn_all = _L0_gnn_setup()
    _L0_gnn_in = {k: v for k, v in _L0_gnn_all.items() if k in ('W_edge', 'b_edge', 'W_node', 'b_node')}
    del _L0_gnn_all

    def _L1_gnn_setup():
        import jax, jax.numpy as jnp
        import numpy as np
        N_ATOMS = 6250
        N_EDGES = 100000
        NODE_DIM = 64
        EDGE_DIM = 64
        FULL_DIM = 2 * NODE_DIM + EDGE_DIM
        BN_EPS = 1e-05

        def _batchnorm(x, gamma, beta):
            mean = jnp.mean(x, axis=0)
            var = jnp.mean(jnp.square(x - mean), axis=0)
            return (x - mean) * jax.lax.rsqrt(var + BN_EPS) * gamma + beta
        key = jax.random.key(seed)
        ks = jax.random.split(key, 8)
        atom_features = jax.random.normal(ks[0], (N_ATOMS, NODE_DIM), dtype=jnp.float32)
        edge_features = jax.random.normal(ks[1], (N_EDGES, EDGE_DIM), dtype=jnp.float32)
        edge_indices = jax.random.randint(ks[2], (N_EDGES, 2), 0, N_ATOMS, dtype=jnp.int64)
        lim = 1.0 / np.sqrt(FULL_DIM)
        W_filter = jax.random.uniform(ks[3], (NODE_DIM, FULL_DIM), jnp.float32, -lim, lim)
        b_filter = jax.random.uniform(ks[4], (NODE_DIM,), jnp.float32, -lim, lim)
        W_core = jax.random.uniform(ks[5], (NODE_DIM, FULL_DIM), jnp.float32, -lim, lim)
        b_core = jax.random.uniform(ks[6], (NODE_DIM,), jnp.float32, -lim, lim)
        gamma_filter = jnp.ones((NODE_DIM,), jnp.float32)
        beta_filter = jnp.zeros((NODE_DIM,), jnp.float32)
        gamma_core = jnp.ones((NODE_DIM,), jnp.float32)
        beta_core = jnp.zeros((NODE_DIM,), jnp.float32)
        return {'atom_features': atom_features, 'edge_features': edge_features, 'W_filter': W_filter, 'b_filter': b_filter, 'gamma_filter': gamma_filter, 'beta_filter': beta_filter, 'W_core': W_core, 'b_core': b_core, 'gamma_core': gamma_core, 'beta_core': beta_core, 'edge_indices': edge_indices}
    _L1_gnn_all = _L1_gnn_setup()
    _L1_gnn_in = {k: v for k, v in _L1_gnn_all.items() if k in ('W_filter', 'b_filter', 'gamma_filter', 'beta_filter', 'W_core', 'b_core', 'gamma_core', 'beta_core')}
    del _L1_gnn_all

    def _L2_gnn_setup():
        import jax, jax.numpy as jnp
        import numpy as np
        ALPHA = 0.2
        key = jax.random.key(seed)
        k1, k2, k3, k4 = jax.random.split(key, 4)
        N, E, d_in, d_out = (12500, 200000, 64, 64)
        node_features = jax.random.normal(k1, (N, d_in), dtype=jnp.float32)
        edge_index = jax.random.randint(k2, (2, E), 0, N, dtype=jnp.int64)
        W = jax.random.normal(k3, (d_in, d_out), dtype=jnp.float32) * (1.414 * np.sqrt(2.0 / (d_in + d_out)))
        a = jax.random.normal(k4, (2 * d_out,), dtype=jnp.float32) * (1.414 * np.sqrt(2.0 / (2 * d_out + 1)))
        return {'node_features': node_features, 'edge_index': edge_index, 'W': W, 'a': a}
    _L2_gnn_all = _L2_gnn_setup()
    _L2_gnn_in = {k: v for k, v in _L2_gnn_all.items() if k in ('W', 'a')}
    del _L2_gnn_all

    def _L3_gnn_setup():
        import jax, jax.numpy as jnp
        import numpy as np
        N_NODES = 6250
        N_EDGES = 100000
        HIDDEN = 64

        def gcn_conv(x, src, dst, W, b, n_nodes):
            ones = jnp.ones(src.shape[0], dtype=x.dtype)
            deg = jax.ops.segment_sum(ones, dst, num_segments=n_nodes)
            dinv = jnp.where(deg > 0, jax.lax.rsqrt(jnp.maximum(deg, 1.0)), 0.0)
            norm = dinv[src] * dinv[dst]
            h = x @ W
            msg = h[src] * norm[:, None]
            out = jax.ops.segment_sum(msg, dst, num_segments=n_nodes)
            return out + b
        key = jax.random.key(seed)
        k1, k2, k3, k4 = jax.random.split(key, 4)
        scale = 1.0 / np.sqrt(HIDDEN)
        x = jax.random.normal(k1, (N_NODES, HIDDEN), dtype=jnp.float32)
        edge_index = jax.random.randint(k2, (2, N_EDGES), 0, N_NODES, dtype=jnp.int64)
        W1 = jax.random.normal(k3, (HIDDEN, HIDDEN), dtype=jnp.float32) * scale
        W2 = jax.random.normal(k4, (HIDDEN, HIDDEN), dtype=jnp.float32) * scale
        b1 = jnp.zeros((HIDDEN,), dtype=jnp.float32)
        b2 = jnp.zeros((HIDDEN,), dtype=jnp.float32)
        return {'x': x, 'edge_index': edge_index, 'W1': W1, 'b1': b1, 'W2': W2, 'b2': b2}
    _L3_gnn_all = _L3_gnn_setup()
    _L3_gnn_in = {k: v for k, v in _L3_gnn_all.items() if k in ('W1', 'b1', 'W2', 'b2')}
    del _L3_gnn_all
    return {'x': x, 'src': src, 'dst': dst, 'edge_attr_16': edge_attr_16, 'edge_attr_64': edge_attr_64, 'L0_gnn_W_edge': _L0_gnn_in['W_edge'], 'L0_gnn_b_edge': _L0_gnn_in['b_edge'], 'L0_gnn_W_node': _L0_gnn_in['W_node'], 'L0_gnn_b_node': _L0_gnn_in['b_node'], 'L1_gnn_W_filter': _L1_gnn_in['W_filter'], 'L1_gnn_b_filter': _L1_gnn_in['b_filter'], 'L1_gnn_gamma_filter': _L1_gnn_in['gamma_filter'], 'L1_gnn_beta_filter': _L1_gnn_in['beta_filter'], 'L1_gnn_W_core': _L1_gnn_in['W_core'], 'L1_gnn_b_core': _L1_gnn_in['b_core'], 'L1_gnn_gamma_core': _L1_gnn_in['gamma_core'], 'L1_gnn_beta_core': _L1_gnn_in['beta_core'], 'L2_gnn_W': _L2_gnn_in['W'], 'L2_gnn_a': _L2_gnn_in['a'], 'L3_gnn_W1': _L3_gnn_in['W1'], 'L3_gnn_b1': _L3_gnn_in['b1'], 'L3_gnn_W2': _L3_gnn_in['W2'], 'L3_gnn_b2': _L3_gnn_in['b2']}

def reference(x, src, dst, edge_attr_16, edge_attr_64, L0_gnn_W_edge, L0_gnn_b_edge, L0_gnn_W_node, L0_gnn_b_node, L1_gnn_W_filter, L1_gnn_b_filter, L1_gnn_gamma_filter, L1_gnn_beta_filter, L1_gnn_W_core, L1_gnn_b_core, L1_gnn_gamma_core, L1_gnn_beta_core, L2_gnn_W, L2_gnn_a, L3_gnn_W1, L3_gnn_b1, L3_gnn_W2, L3_gnn_b2):
    import jax
    import jax.numpy as jnp

    def _L0_gnn_ref(x, edge_index, edge_feature, W_edge, b_edge, W_node, b_node):
        import jax, jax.numpy as jnp
        import numpy as np
        N_NODES = 12500
        N_EDGES = 200000
        D_IN = 64
        D_OUT = 64
        EDGE_DIM = 16
        gate = jax.nn.sigmoid(edge_feature @ W_edge + b_edge)[:, 0]
        xp = x @ W_node.T + b_node
        row = edge_index[0]
        col = edge_index[1]
        num_nodes = x.shape[0]
        msg = gate[:, None] * xp[col]
        summed = jax.ops.segment_sum(msg, row, num_segments=num_nodes)
        cnt = jax.ops.segment_sum(jnp.ones((row.shape[0],), dtype=xp.dtype), row, num_segments=num_nodes)
        out = summed / jnp.maximum(cnt, 1.0)[:, None]
        return out

    def _L1_gnn_ref(atom_features, edge_features, W_filter, b_filter, gamma_filter, beta_filter, W_core, b_core, gamma_core, beta_core, edge_indices):
        import jax, jax.numpy as jnp
        import numpy as np
        N_ATOMS = 6250
        N_EDGES = 100000
        NODE_DIM = 64
        EDGE_DIM = 64
        FULL_DIM = 2 * NODE_DIM + EDGE_DIM
        BN_EPS = 1e-05

        def _batchnorm(x, gamma, beta):
            mean = jnp.mean(x, axis=0)
            var = jnp.mean(jnp.square(x - mean), axis=0)
            return (x - mean) * jax.lax.rsqrt(var + BN_EPS) * gamma + beta
        src = edge_indices[:, 0]
        dst = edge_indices[:, 1]
        z = jnp.concatenate([atom_features[dst], atom_features[src], edge_features], axis=1)
        signal = jax.nn.softplus(_batchnorm(z @ W_core.T + b_core, gamma_core, beta_core))
        gate = jax.nn.sigmoid(_batchnorm(z @ W_filter.T + b_filter, gamma_filter, beta_filter))
        message = gate * signal
        nbr_sumed = jax.ops.segment_sum(message, dst, num_segments=atom_features.shape[0])
        return atom_features + nbr_sumed

    def _L2_gnn_ref(node_features, edge_index, W, a):
        import jax, jax.numpy as jnp
        import numpy as np
        ALPHA = 0.2
        N = node_features.shape[0]
        d_out = W.shape[1]
        src, tgt = (edge_index[0], edge_index[1])
        h = node_features @ W
        s_src = h @ a[:d_out]
        s_tgt = h @ a[d_out:]
        e = jax.nn.leaky_relu(s_src[src] + s_tgt[tgt], negative_slope=ALPHA)
        m = jax.ops.segment_max(e, tgt, num_segments=N)
        e_exp = jnp.exp(e - m[tgt])
        denom = jax.ops.segment_sum(e_exp, tgt, num_segments=N)
        attention = e_exp / denom[tgt]
        h_prime = jax.ops.segment_sum(h[src] * attention[:, None], tgt, num_segments=N)
        return jax.nn.elu(h_prime)

    def _L3_gnn_ref(x, edge_index, W1, b1, W2, b2):
        import jax, jax.numpy as jnp
        import numpy as np
        N_NODES = 6250
        N_EDGES = 100000
        HIDDEN = 64

        def gcn_conv(x, src, dst, W, b, n_nodes):
            ones = jnp.ones(src.shape[0], dtype=x.dtype)
            deg = jax.ops.segment_sum(ones, dst, num_segments=n_nodes)
            dinv = jnp.where(deg > 0, jax.lax.rsqrt(jnp.maximum(deg, 1.0)), 0.0)
            norm = dinv[src] * dinv[dst]
            h = x @ W
            msg = h[src] * norm[:, None]
            out = jax.ops.segment_sum(msg, dst, num_segments=n_nodes)
            return out + b
        n = x.shape[0]
        src, dst = (edge_index[0], edge_index[1])
        h = jax.nn.relu(gcn_conv(x, src, dst, W1, b1, n))
        return gcn_conv(h, src, dst, W2, b2, n)
    edge_index = jnp.stack([src, dst])
    edge_index_t = jnp.stack([src, dst], axis=1)
    x = _layernorm(x + _L0_gnn_ref(x, edge_index, edge_attr_16, L0_gnn_W_edge, L0_gnn_b_edge, L0_gnn_W_node, L0_gnn_b_node), axis=-1)
    x = _layernorm(x + _L1_gnn_ref(x, edge_attr_64, L1_gnn_W_filter, L1_gnn_b_filter, L1_gnn_gamma_filter, L1_gnn_beta_filter, L1_gnn_W_core, L1_gnn_b_core, L1_gnn_gamma_core, L1_gnn_beta_core, edge_index_t), axis=-1)
    x = _layernorm(x + _L2_gnn_ref(x, edge_index, L2_gnn_W, L2_gnn_a), axis=-1)
    x = _layernorm(x + _L3_gnn_ref(x, edge_index, L3_gnn_W1, L3_gnn_b1, L3_gnn_W2, L3_gnn_b2), axis=-1)
    return x

_drawn_inputs = setup_inputs


def setup_inputs(seed=0):
    import zlib

    import numpy as np

    out = dict(_drawn_inputs(seed))
    spreads = {'L0_gnn_b_node': (0.0, 0.1),
     'L1_gnn_gamma_filter': (1.0, 0.2),
     'L1_gnn_beta_filter': (0.0, 0.1),
     'L1_gnn_gamma_core': (1.0, 0.2),
     'L1_gnn_beta_core': (0.0, 0.1),
     'L3_gnn_b1': (0.0, 0.1),
     'L3_gnn_b2': (0.0, 0.1)}
    factors = {}
    for name, (base, spread) in spreads.items():
        noise = np.random.default_rng([zlib.crc32(name.encode()), seed]).standard_normal(out[name].shape)
        drawn = base * np.exp(spread * noise) if base else spread * noise
        out[name] = jnp.asarray(drawn.astype(out[name].dtype))
    for name, factor in factors.items():
        out[name] = (out[name] * factor).astype(out[name].dtype)
    return out
```

```python
from collections import namedtuple
from contextlib import ExitStack

import concourse.bass as bass
from concourse import mybir

ALU = mybir.AluOpType
ACT = mybir.ActivationFunctionType
AX = mybir.AxisListType
F32 = mybir.dt.float32
BF16 = mybir.dt.bfloat16
I32 = mybir.dt.int32

P = 128
N = 12500
E = 200000
D = 64
K16 = 16
W = -(-N // P)
NP = W * P
FULL_W = N // P
TAIL_N = N - FULL_W * P
T = -(-E // P)
FULL_T = E // P
HALF = E - FULL_T * P
TB = -(-T // P)
TAIL_T = FULL_T - (TB - 1) * P
G = 8
PAIR = 2 * G
S = -(-(T + W - 1) // P) * P
SB = S // P
ITER = S // PAIR
SPAD = S + PAIR
CH = S // 4
NOWHERE = 1 << 20
TRASH = NP
SROWS = NP + P
LANES = 4
WPC = 7
CHUNKS = W // WPC
D1 = D + 1
D2 = D + 2
BIG = 2.0 ** 100
EPS = 1e-5
assert CHUNKS * WPC == W and CHUNKS % 2 == 0 and ITER * PAIR == S and CH <= 512


def build(nc, x, src, dst, ea16, ea64, w_edge, b_edge, w_node, b_node,
          w_filter, b_filter, gamma_f, beta_f, w_core, b_core, gamma_c, beta_c,
          w_att, a_att, w1, b1, w2, b2, out, debug=None):
    with ExitStack() as ctx:
        def sb(name, shape, dt=F32):
            return ctx.enter_context(nc.sbuf_tensor(name, shape, dt))

        def sem(name):
            return ctx.enter_context(nc.semaphore(name))

        def dram(name, shape, dt=F32):
            return nc.dram_tensor(name, shape, dt, kind="Internal").ap()

        lane_tab = [dram(f"lane_tab{k}", (SROWS, D1)) for k in range(LANES)]
        src_tab = dram("src_tab", (NP, 2 * D))
        att_tab = dram("att_tab", (NP, D2))
        gcn_tab = [dram(f"gcn_tab{k}", (NP, D)) for k in range(2)]
        y_stash = dram("y_stash", (2 * ITER, P, G * 2 * D))
        h_stash = dram("h_stash", (2 * ITER, P, G * D2))

        x_n = sb("x_n", [P, W, D])
        acc = sb("acc", [P, W, D1])
        tab = sb("tab", [P, W, 2 * D])
        aux = sb("aux", [P, W, D1])
        src_s = sb("src_s", [P, SPAD])
        dst_s = sb("dst_s", [P, SPAD])
        gate_s = sb("gate_s", [P, SPAD])
        valid_s = sb("valid_s", [P, SPAD])
        place_s = sb("place_s", [2 * 32, SPAD], I32)
        win_s, row_s = place_s[0:1, :], place_s[32:33, :]
        buf_a = sb("buf_a", [P, 2, G, 2 * D])
        buf_b = sb("buf_b", [P, 2, G, 2 * D])
        buf_c = sb("buf_c", [P, 2, G, 2 * D])
        buf_d = sb("buf_d", [P, 2, G, 2 * D])
        rows = sb("rows", [P, 2, G, D2])
        sums = sb("sums", [P, W, 2])
        mx = sb("mx", [P, W])
        col_a = sb("col_a", [P, W])
        col_b = sb("col_b", [P, W])
        idx = sb("idx", [P, 2, G], I32)
        srcg = sb("srcg", [P, 2, G])
        dup = sb("dup", [P, 2, G])
        tmp_c = sb("tmp_c", [P, 4, G])
        ex = sb("ex", [P, 2, G])
        iota = sb("iota", [P, P])
        ident = sb("ident", [P, P])
        ident_b = sb("ident_b", [P, P], BF16)
        below = sb("below", [P, P])
        ids = sb("ids", [P, TB])
        trash = sb("trash", [P, 1])
        ones = sb("ones", [P, P])
        key = sb("key", [P, TB])
        last_i = sb("last_i", [P, TB], I32)
        t_col = sb("t_col", [P, TB])
        wsm = rows[:, :, :, :].rearrange("p a b c -> p (a b c)")[:, 512:1024]
        wt = sb("wt", [P, 640])
        bias0 = sb("bias0", [P, D])
        bias_d = sb("bias_d", [P, 2 * D])
        bias3 = sb("bias3", [P, 2, D])
        we_bc = sb("we_bc", [P, K16])
        be_c = sb("be_c", [P, 1])
        bn_col = sb("bn_col", [P, 8])
        bn = sb("bn", [P, 2, 2 * D])
        deg = sb("deg", [P, W])

        aux_flat = aux[:, :, :].rearrange("p a b -> p (a b)")
        ob = aux_flat[:, 0:G * P].bitcast(BF16).rearrange("p (b u f) -> p b u f", b=2, u=G)
        sq = aux_flat[:, G * P:3 * G * P].rearrange("p (b u f) -> p b u f", b=2, u=G)
        ea_s = aux_flat[:, 3 * G * P:4 * G * P].rearrange("p (b u f) -> p b u f", b=2, u=G)
        xs = aux_flat[:, 4 * G * P:4 * G * P + WPC * D].rearrange("p (w f) -> p w f", f=D)
        xt = aux_flat[0:D, W * D1 - WPC * P:W * D1]

        ps = ctx.enter_context(nc.psum_tensor("ps", [P, 8, 512], F32))

        def region(k, n):
            return ps[:, k // 4, (k % 4) * P:(k % 4) * P + n]

        def regions(bank, n):
            return ps[:, bank:bank + 2, :].rearrange("p c (k f) -> p (c k) f", f=P)[:, :, 0:n]

        def by_bank(ap):
            return ap.rearrange("p (k c) f -> p c k f", c=2)

        src_t = buf_a[:, :, :, :].rearrange("p a b c -> p (a b) c")[:, 0:TB, :].bitcast(I32)
        dst_t = buf_b[:, :, :, :].rearrange("p a b c -> p (a b) c")[:, 0:TB, :].bitcast(I32)
        src_f = buf_c[:, :, :, :].rearrange("p a b c -> p (a b) c")[:, 0:TB, :]
        dst_f = buf_d[:, :, :, :].rearrange("p a b c -> p (a b) c")[:, 0:TB, :]
        gate_t = aux[:, :, :].rearrange("p a b -> p (a b)")[:, 0:TB * P].rearrange("p (b e) -> p b e", e=P)
        t_row = aux[:, :, :].rearrange("p a b -> p (a b)")[:, TB * P:TB * P + S]
        w_row = aux[:, :, :].rearrange("p a b -> p (a b)")[:, TB * P + S:TB * P + 2 * S]
        scr_i = rows[:, :, :, :].rearrange("p a b c -> p (a b c)").bitcast(I32)
        step_i = acc[:, :, :].rearrange("p a b -> p (a b)")[:, 0:S].bitcast(I32)
        step_f = acc[:, :, :].rearrange("p a b -> p (a b)")[:, S:2 * S]
        junk = acc[:, :, :].rearrange("p a b -> p (a b)")[:, 2 * S:3 * S]
        tab_flat = tab[:, :, :].rearrange("p a b -> p (a b)")
        EB = P * K16
        sel = tab_flat[:, 0:TB * CH].rearrange("p (b s) -> p b s", s=CH)
        x_flat = tab_flat
        tab_d = tab_flat[:, 0:W * D].rearrange("p (w f) -> p w f", f=D)
        scratch = tab_flat[:, W * D:2 * W * D].rearrange("p (w f) -> p w f", f=D)
        stage = buf_a[:, :, :, :].rearrange("p a b c -> p (a b) c")

        NAMES = """consts_made iotas_made tiles_clean tiles_loaded weights_loaded bias_loaded x_clean x_loaded
            ea_loaded0 ea_loaded1 ea_clean dve key_ready keyrow_made tcol_ready trow_made trow_copied sel_made sel_used steps_made gate_lin gate_done
            wt_made wt_copied wa_made fill_ready fill0 fill1 fill2 fill3
            node_in node_xs node_xt node_xtc node_out node_evac stage_full stage_free tab_stored
            l0_src l0_srow l0_og l0_s l0_idx l0_b l0_bc l0_out l0_outc l0_sfree l0_done l0_turn l0_dve lanes_done lane_in0 lane_in1 lane_in2 lane_in3 lane_again
            l1_idx l1_turn l1_gfree l1_o l1_t l1_tc l1_ys l1_y l1_sq l1_stat l1_yfree l1_ybank e_turn e0 e1 ys0 ys1 l1_got0 l1_got1
            stat_done bn_ready bn_made bn_copied
            lb_y0 lb_y1 lb_z lb_zfree lb_o lb_abs lb_exp lb_dve lb_msg lb_out lb_accfree lb_acc lb_clean
            ln_var ln_std
            l2_idx l2_turn l2_got0 l2_got1 l2_nm l2_mask l2_max l2_maskfree l2_mx l2_hst0 l2_hst1 l2_hfree l2_dve
            mx_done l2b_h0 l2b_h1 l2b_hfree l2b_o l2b_t l2b_tc l2b_s l2b_arg l2b_exp l2b_dve l2b_ow l2b_out l2b_accfree l2b_acc
            elu_in elu_out gcn_in0 gcn_in1 gcn_st0 gcn_st1
            g0_idx g0_turn g0_got0 g0_got1 g0_o g0_out g0_accfree g0_gfree g0_acc
            g1_idx g1_turn g1_got0 g1_got1 g1_o g1_out g1_accfree g1_gfree g1_acc
            result_ready result_stored""".split()
        s = namedtuple("Semaphores", NAMES)(*[sem(n) for n in NAMES])
        fill = [s.fill0, s.fill1, s.fill2, s.fill3]
        lane_in = [s.lane_in0, s.lane_in1, s.lane_in2, s.lane_in3]

        def bc(ap, shape):
            return ap.to_broadcast(shape)

        def step_slice(t, g):
            return t[:, bass.ds(g * G, G)]

        def step_col(t, g, u):
            return t[:, bass.ds(g * G + u, 1)]

        def load8(engine, table, g, top):
            _, v = nc.values_load_multi_w_load_instructions(
                table[:, bass.ds(g * G, G)], engines=(engine,), min_val=0, max_val=top,
                skip_runtime_bounds_check_because="the table's entries are clamped to it")
            return v

        def window(t, w, n, start=0):
            return t[:, bass.ds(w, 1), start:start + n].rearrange("p a b -> p (a b)")

        block = ctx.enter_context(nc.Block())

        WN, WC, WF, WA = 0, D, 4 * D, 7 * D
        TN, TS, TE, TA, T1 = 0, D, 5 * D, 7 * D, 7 * D + D2
        a2 = sb("a2", [D, 2])
        w12 = sb("w12", [D, 2, D])

        @block.sync
        def _(sp):
            sp.wait_ge(s.tiles_clean, 2)
            body = (TB - 1) * P * P
            for tile, arr in ((src_t, src), (dst_t, dst)):
                sp.dma_start(tile[:, 0:TB - 1, :], arr[0:body].rearrange("(b t e) -> t b e", t=P, e=P)).then_inc(s.tiles_loaded, 16)
                sp.dma_start(tile[0:TAIL_T, TB - 1, :],
                             arr[body:FULL_T * P].rearrange("(t e) -> t e", e=P)).then_inc(s.tiles_loaded, 16)
                sp.dma_start(tile[TAIL_T:TAIL_T + 1, TB - 1, P - HALF:P],
                             arr[FULL_T * P:E].rearrange("(a e) -> a e", a=1)).then_inc(s.tiles_loaded, 16)
            sp.dma_start(we_bc[:, :], w_edge.rearrange("k a -> (a k)").partition_broadcast(P)).then_inc(s.weights_loaded, 16)
            sp.dma_start(be_c[:, :], b_edge.partition_broadcast(P)).then_inc(s.weights_loaded, 16)

            def load_ea(b, slot, done):
                view = x_flat[:, slot * EB:(slot + 1) * EB]
                if b < TB - 1:
                    sp.dma_start(view, ea16[b * P * P:(b + 1) * P * P, :].rearrange("(t e) k -> t (e k)", e=P)).then_inc(done, 16)
                else:
                    sp.dma_start(view[0:TAIL_T, :], ea16[b * P * P:FULL_T * P, :].rearrange("(t e) k -> t (e k)", e=P)).then_inc(done, 16)
                    sp.dma_start(view[TAIL_T:TAIL_T + 1, (P - HALF) * K16:EB],
                                 ea16[FULL_T * P:E, :].rearrange("(a e) k -> a (e k)", a=1)).then_inc(done, 16)

            for b in range(6):
                load_ea(b, b, s.ea_loaded0)
            sp.dma_start(wsm[0:D, WN:WN + D], w_node).then_inc(s.weights_loaded, 16)
            sp.dma_start(wsm[0:D, WC:WC + 3 * D], w_core).then_inc(s.weights_loaded, 16)
            sp.dma_start(wsm[0:D, WF:WF + 3 * D], w_filter).then_inc(s.weights_loaded, 16)
            sp.dma_start(wsm[0:D, WA:WA + D], w_att).then_inc(s.weights_loaded, 16)
            with nc.allow_non_contiguous_dma(reason="128 single elements, once"):
                sp.dma_start(a2[:, :], a_att.rearrange("(k d) -> d k", k=2)).then_inc(s.weights_loaded, 16)
            sp.dma_start(w12[:, 0, :], w1).then_inc(s.weights_loaded, 16)
            sp.dma_start(w12[:, 1, :], w2).then_inc(s.weights_loaded, 16)
            sp.dma_start(bias0[:, :], b_node.partition_broadcast(P)).then_inc(s.bias_loaded, 16)
            sp.dma_start(bias_d[:, 0:D], b_core.partition_broadcast(P)).then_inc(s.bias_loaded, 16)
            sp.dma_start(bias_d[:, D:2 * D], b_filter.partition_broadcast(P)).then_inc(s.bias_loaded, 16)
            sp.dma_start(bias3[:, 0, :], b1.partition_broadcast(P)).then_inc(s.bias_loaded, 16)
            sp.dma_start(bias3[:, 1, :], b2.partition_broadcast(P)).then_inc(s.bias_loaded, 16)
            for k, (gam, half) in enumerate(((gamma_c, 0), (gamma_f, 1), (beta_c, 0), (beta_f, 1))):
                sp.dma_start(bn_col[half * D:half * D + D, 2 + k // 2:3 + k // 2], gam.rearrange("(d a) -> d a", a=1)).then_inc(s.bias_loaded, 16)
            sp.wait_ge(s.x_clean, 1)
            sp.dma_start(x_n[:, 0:FULL_W, :], x[0:FULL_W * P, :].rearrange("(w p) f -> p w f", p=P)).then_inc(s.x_loaded, 16)
            sp.dma_start(x_n[0:TAIL_N, FULL_W, :], x[FULL_W * P:N, :]).then_inc(s.x_loaded, 16)
            for part, n in ((1, 6), (2, 1)):
                sp.wait_ge(s.ea_clean, part)
                for b in range(n):
                    load_ea(6 * part + b, b, s.ea_loaded1)

            sp.wait_ge(s.lanes_done, 1)

            def lane_rows(k):
                return lane_tab[k][0:NP, :].rearrange("(w p) f -> p w f", p=P)

            tab_l = tab_flat[:, 0:W * D1].rearrange("p (w f) -> p w f", f=D1)
            for k, to in ((0, acc[:, :, :]), (1, aux[:, :, :]), (2, tab_l)):
                sp.dma_start(to, lane_rows(k)).then_inc(lane_in[k], 16)
            sp.wait_ge(s.lane_again, 1)
            sp.dma_start(aux[:, :, :], lane_rows(3)).then_inc(lane_in[3], 16)

            with sp.Fori(0, CHUNKS) as c:
                sp.wait_ge(s.stage_full, c + 1)
                sp.dma_start(src_tab[bass.ds(c * (WPC * P), WPC * P), :].rearrange("(w p) f -> p w f", p=P),
                             stage[:, 0:WPC, :]).then_inc(s.tab_stored, 16)
                sp.wait_ge(s.tab_stored, c * 16 + 16)
                sp.sem_inc(s.stage_free, 1)

            e_in, y_out = [s.e0, s.e1], [s.ys0, s.ys1]

            def load_edges(g, b):
                starts = load8(mybir.EngineType.SP, row_s, g, E - P)
                for u in range(G):
                    sp.dma_start(ea_s[:, b, u, :], ea64[bass.ds(starts[u], P), :]).then_inc(e_in[b], 16)

            sp.wait_ge(s.trow_copied, 1)
            for b in range(2):
                load_edges(b, b)
            with sp.Fori(0, ITER) as i:
                for b in range(2):
                    sp.wait_ge(s.l1_t, i * 2 + b + 1)
                    sp.sem_inc(s.e_turn, 1)
                    load_edges(i * 2 + b + 2, b)
                for b in range(2):
                    sp.wait_ge(s.l1_y, i * 2 + b + 1)
                    sp.dma_start(y_stash[bass.ds(i * 2 + b, 1), :, :].rearrange("a p f -> (a p) f"),
                                 buf_c[:, b, :, :].rearrange("p u f -> p (u f)")).then_inc(y_out[b], 16)
                for b in range(2):
                    sp.wait_ge(y_out[b], i * 16 + 16)
                    sp.sem_inc(s.l1_yfree, 1)
            for b in range(2):
                sp.wait_ge(e_in[b], (ITER + 1) * G * 16)

            y_in = [s.lb_y0, s.lb_y1]
            with sp.Fori(0, ITER) as i:
                for b in range(2):
                    sp.wait_ge(s.lb_zfree, i * 2 + b + 1)
                    sp.dma_start(buf_c[:, b, :, :].rearrange("p u f -> p (u f)"),
                                 y_stash[bass.ds(i * 2 + b, 1), :, :].rearrange("a p f -> (a p) f")).then_inc(y_in[b], 16)

            with sp.Fori(0, CHUNKS) as c:
                sp.wait_ge(s.stage_full, c + CHUNKS + 1)
                sp.dma_start(att_tab[bass.ds(c * (WPC * P), WPC * P), :].rearrange("(w p) f -> p w f", p=P),
                             stage[:, 0:WPC, 0:D2]).then_inc(s.tab_stored, 16)
                sp.wait_ge(s.tab_stored, c * 16 + (CHUNKS + 1) * 16)
                sp.sem_inc(s.stage_free, 1)
            got, h_out = [s.l2_got0, s.l2_got1], [s.l2_hst0, s.l2_hst1]
            with sp.Fori(0, ITER) as i:
                for b in range(2):
                    sp.wait_ge(got[b], i * (G * 16) + G * 16)
                    sp.dma_start(h_stash[bass.ds(i * 2 + b, 1), :, :].rearrange("a p f -> (a p) f"),
                                 rows[:, b, :, :].rearrange("p u f -> p (u f)")).then_inc(h_out[b], 16)
                    sp.wait_ge(h_out[b], i * 16 + 16)
                    sp.sem_inc(s.e_turn, 1)
                    sp.wait_ge(s.l2_mask, i * 2 + b + 1)
                    sp.sem_inc(s.l2_hfree, 1)
            h_in = [s.l2b_h0, s.l2b_h1]
            with sp.Fori(0, ITER) as i:
                for b in range(2):
                    sp.wait_ge(s.l2b_hfree, i * 2 + b + 1)
                    sp.dma_start(rows[:, b, :, :].rearrange("p u f -> p (u f)"),
                                 h_stash[bass.ds(i * 2 + b, 1), :, :].rearrange("a p f -> (a p) f")).then_inc(h_in[b], 16)

            for k, (ready, stored) in enumerate(((s.gcn_in0, s.gcn_st0), (s.gcn_in1, s.gcn_st1))):
                sp.wait_ge(ready, 1)
                sp.dma_start(gcn_tab[k].rearrange("(w p) f -> p w f", p=P), tab_d).then_inc(stored, 16)

            sp.wait_ge(s.result_ready, 1)
            sp.dma_start(out[0:FULL_W * P, :].rearrange("(w p) f -> p w f", p=P), x_n[:, 0:FULL_W, :]).then_inc(s.result_stored, 16)
            sp.dma_start(out[FULL_W * P:N, :], x_n[0:TAIL_N, FULL_W, :]).then_inc(s.result_stored, 16)
            sp.wait_ge(s.result_stored, 32)

        @block.gpsimd
        def _(pool):
            pool.memset(src_t, 0).then_inc(s.tiles_clean, 1)
            pool.memset(dst_t, NOWHERE).then_inc(s.tiles_clean, 1)
            pool.iota(step_i, [[1, S]], base=0, channel_multiplier=0).then_inc(s.iotas_made, 1)
            pool.iota(scr_i[:, 0:TB], [[P, TB]], base=0, channel_multiplier=1).then_inc(s.iotas_made, 1)
            pool.memset(x_n[:, FULL_W, :], 0.0).then_inc(s.x_clean, 1)

            pool.wait_ge(s.fill_ready, 1)
            per = SROWS * D1 // P
            for k in range(LANES):
                pool.dma_start(lane_tab[k].rearrange("(p r) f -> p (r f)", p=P), tab_flat[:, 0:per]).then_inc(fill[k], 16)
            for k in range(LANES):
                pool.wait_ge(fill[k], 16)
            pool.sem_inc(s.fill_ready, 1)
            with pool.Fori(0, ITER) as i:
                for b in range(2):
                    g = i * 2 + b
                    pool.wait_ge(s.l0_idx, g + 1)
                    pool.sem_inc(s.l0_turn, 1)
                    pool.wait_ge(s.l0_outc, g + 2)
                    pool.sem_inc(s.l0_turn, 1)
                    for u in range(G):
                        k = u % LANES
                        pool.wait_ge(fill[k], i * 64 + (16 + 32 * b + 16 * (u // LANES)))
                        pool.sem_inc(s.l0_done if u == LANES - 1 else s.l0_turn, 1)
                        pool.indirect_dma_start(lane_tab[k][:, :], bass.IndirectOffsetOnAxis(ap=idx[:, b, u:u + 1], axis=0),
                                                rows[:, b, u, 0:D1], None, compute_op=ALU.add).then_inc(fill[k], 16)
            for k in range(LANES):
                pool.wait_ge(fill[k], 16 + 64 * ITER)
            pool.sem_inc(s.lanes_done, 1)

            def gathers(table, n, to, idx_ready, turn, free, got):
                with pool.Fori(0, ITER) as i:
                    for b in range(2):
                        pool.wait_ge(idx_ready, i * 2 + b + 1)
                        pool.sem_inc(turn, 1)
                        pool.wait_ge(free, i * 2 + b + 1)
                        pool.sem_inc(turn, 1)
                        for u in range(G):
                            pool.indirect_dma_start(to[:, b, u, 0:n], None, table[:, :],
                                                    bass.IndirectOffsetOnAxis(ap=idx[:, b, u:u + 1], axis=0)).then_inc(got[b], 16)

            pool.wait_ge(s.tab_stored, CHUNKS * 16)
            gathers(src_tab, 2 * D, buf_b, s.l1_idx, s.l1_turn, s.l1_gfree, [s.l1_got0, s.l1_got1])
            pool.wait_ge(s.tab_stored, 2 * CHUNKS * 16)
            gathers(att_tab, D2, rows, s.l2_idx, s.l2_turn, s.l2_hfree, [s.l2_got0, s.l2_got1])
            pool.wait_ge(s.gcn_st0, 16)
            gathers(gcn_tab[0], D, rows, s.g0_idx, s.g0_turn, s.g0_gfree, [s.g0_got0, s.g0_got1])
            pool.wait_ge(s.gcn_st1, 16)
            gathers(gcn_tab[1], D, rows, s.g1_idx, s.g1_turn, s.g1_gfree, [s.g1_got0, s.g1_got1])

        @block.scalar
        def _(act):
            act.wait_ge(s.weights_loaded, 16 * 9)
            act.wait_ge(s.gate_lin, 1)
            act.activation(gate_t, gate_t, ACT.Sigmoid, bias=be_c[:, 0:1]).then_inc(s.gate_done, 1)
            act.wait_ge(s.wt_made, 1)
            act.activation(wt[:, 0:7 * D], ps[:, 6, 0:7 * D], ACT.Copy).then_inc(s.wt_copied, 1)
            act.activation(wt[0:D, TA:TA + D], wsm[0:D, WA:WA + D], ACT.Copy).then_inc(s.wt_copied, 1)
            act.activation(xt[0:D, 0:D], ps[0:D, 7, 0:D], ACT.Copy).then_inc(s.wt_copied, 1)
            act.wait_ge(s.wa_made, 1)
            act.activation(wt[0:D, TA + D:TA + D2], ps[0:D, 7, D:D2], ACT.Copy).then_inc(s.wt_copied, 1)

            def node_copies(base, view):
                with act.Fori(0, CHUNKS) as c:
                    act.activation(xs, view[:, bass.ds(c * WPC, WPC), :], ACT.Copy).then_inc(s.node_xs, 1)
                    act.wait_ge(s.node_xt, c + (base + 1))
                    act.activation(xt[:, :], ps[0:D, 0:2, :].rearrange("p a b -> p (a b)")[:, 0:WPC * P], ACT.Copy).then_inc(s.node_xtc, 1)

            act.wait_ge(s.node_in, 1)
            node_copies(0, x_n)
            with act.Fori(0, ITER) as i:
                for b in range(2):
                    g = i * 2 + b
                    act.wait_ge(s.l0_b, g + 1)
                    act.activation(buf_d[:, 0, :, :], regions(4, P), ACT.Copy).then_inc(s.l0_bc, 1)
                    act.wait_ge(s.l0_out, g + 1)
                    act.wait_ge(s.l0_done, g + 1)
                    act.activation(rows[:, b, :, 0:D1], regions(6, D1), ACT.Copy).then_inc(s.l0_outc, 1)

            def std(n):
                act.wait_ge(s.ln_var, n)
                act.activation(col_b[:, :], col_a[:, :], ACT.Sqrt).then_inc(s.ln_std, 1)

            def indices(ready, got):
                for b in range(2):
                    act.activation(idx[:, b, :], src_s[:, b * G:b * G + G], ACT.Copy).then_inc(ready, 1)

            def next_indices(i, b, ready, got):
                act.wait_ge(got[b], i * (G * 16) + G * 16)
                act.activation(idx[:, b, :], src_s[:, bass.ds(i * PAIR + (PAIR + b * G), G)], ACT.Copy).then_inc(ready, 1)

            std(1)
            act.wait_ge(s.node_in, 3)
            node_copies(CHUNKS, x_n)
            got = [s.l1_got0, s.l1_got1]
            indices(s.l1_idx, got)
            with act.Fori(0, ITER) as i:
                for b in range(2):
                    act.wait_ge(s.l1_t, i * 2 + b + 1)
                    act.activation(buf_d[:, b, :, :].rearrange("p u f -> p (u f)"), ps[:, b, :].bitcast(BF16), ACT.Copy)
                    act.activation(buf_a[:, b, 0:4, :].rearrange("p u f -> p (u f)"), ps[:, 2 + b, :], ACT.Copy).then_inc(s.l1_tc, 1)
                for b in range(2):
                    next_indices(i, b, s.l1_idx, got)
                    act.wait_ge(s.l1_y, i * 2 + b + 1)
                    act.wait_ge(s.l1_stat, i * 2 + b + 1)
                    act.activation(sq[:, b, :, :], buf_c[:, b, :, :], ACT.Square).then_inc(s.l1_sq, 1)
            act.wait_ge(s.bn_ready, 1)
            act.activation(bn_col[:, 7:8], bn_col[:, 6:7], ACT.Sqrt).then_inc(s.bn_made, 1)
            act.preload_act_table_set("natural_log_exp_and_others")
            with act.Fori(0, ITER) as i:
                for b in range(2):
                    z = buf_d[:, b, :, :]
                    act.wait_ge(s.lb_abs, i * 2 + b + 1)
                    act.activation(buf_b[:, b, :, 0:D], buf_b[:, b, :, 0:D], ACT.Exp)
                    act.activation(z[:, :, D:2 * D], z[:, :, D:2 * D], ACT.Exp, scale=-1.0).then_inc(s.lb_exp, 1)
                    act.wait_ge(s.lb_exp, i * 4 + (2 * b + 1))
                    act.activation(buf_b[:, b, :, D:2 * D], buf_b[:, b, :, 0:D], ACT.Ln, bias=1.0).then_inc(s.lb_exp, 1)
            std(2)
            act.wait_ge(s.node_in, 5)
            node_copies(2 * CHUNKS, x_n)
            act.wait_ge(s.l1_idx, 2 * ITER + 2)
            got = [s.l2_got0, s.l2_got1]
            indices(s.l2_idx, got)
            with act.Fori(0, ITER) as i:
                for b in range(2):
                    next_indices(i, b, s.l2_idx, got)
            with act.Fori(0, ITER) as i:
                for b in range(2):
                    act.wait_ge(s.l2b_t, i * 2 + b + 1)
                    act.activation(buf_d[:, b, :, :].rearrange("p u f -> p (u f)"), ps[:, b, :].bitcast(BF16), ACT.Copy).then_inc(s.l2b_tc, 1)
                for b in range(2):
                    act.wait_ge(s.l2b_arg, i * 2 + b + 1)
                    act.activation(ex[:, b, :], tmp_c[:, 2 + b, :], ACT.Exp).then_inc(s.l2b_exp, 1)
            act.wait_ge(s.elu_in, 1)
            act.activation(scratch, scratch, ACT.Exp).then_inc(s.elu_out, 1)
            std(3)
            std(4)
            act.wait_ge(s.l2_idx, 2 * ITER + 2)
            got = [s.g0_got0, s.g0_got1]
            indices(s.g0_idx, got)
            with act.Fori(0, ITER) as i:
                for b in range(2):
                    next_indices(i, b, s.g0_idx, got)
            act.wait_ge(s.node_in, 6)
            node_copies(3 * CHUNKS, tab_d)
            act.wait_ge(s.g0_idx, 2 * ITER + 2)
            got = [s.g1_got0, s.g1_got1]
            indices(s.g1_idx, got)
            with act.Fori(0, ITER) as i:
                for b in range(2):
                    next_indices(i, b, s.g1_idx, got)
            act.wait_ge(s.node_in, 7)
            node_copies(4 * CHUNKS, tab_d)
            std(5)

        @block.tensor
        def _(pe):
            pe.wait_ge(s.consts_made, 1)
            pe.wait_ge(s.key_ready, 1)
            for b in range(TB):
                last = pe.matmul(region(b, P), bc(key[:, b:b + 1], [P, P]), ident[:, :], start=True, stop=True)
            last.then_inc(s.keyrow_made, 1)
            pe.wait_ge(s.weights_loaded, 16 * 9)
            i64 = ident[0:D, 0:D]
            wps = ps[:, 6, :]
            for at, frm in ((TN, WN), (TS, WC + D), (TS + D, WF + D), (TS + 2 * D, WC), (TS + 3 * D, WF),
                            (TE, WC + 2 * D), (TE + D, WF + 2 * D)):
                pe.matmul(wps[0:D, at:at + D], wsm[0:D, frm:frm + D], i64, start=True, stop=True)
            for at, frm in ((TN, WN), (TS, WC + D), (TS + D, WF + D), (TS + 2 * D, WC), (TS + 3 * D, WF),
                            (TE, WC + 2 * D), (TE + D, WF + 2 * D)):
                pe.matmul(wps[D:P, at:at + D], wsm[0:D, frm:frm + D], i64, start=True, stop=True)
            pe.matmul(ps[0:D, 7, 0:D], wsm[0:D, WA:WA + D], i64, start=True, stop=True).then_inc(s.wt_made, 1)
            pe.wait_ge(s.wt_copied, 3)
            pe.matmul(ps[0:D, 7, D:D2], xt[0:D, 0:D], a2[:, :], start=True, stop=True).then_inc(s.wa_made, 1)
            pe.wait_ge(s.wt_copied, 4)
            pe.wait_ge(s.tcol_ready, 1)
            for b in range(SB):
                last = pe.matmul(region(16 + b, P), bc(t_col[:, b:b + 1], [P, P]), ident[:, :], start=True, stop=True)
            last.then_inc(s.trow_made, 1)
            pe.wait_ge(s.trow_copied, 1)
            pe.wait_ge(s.gate_done, 1)
            with pe.Fori(0, 4) as c:
                pe.wait_ge(s.sel_made, c + 1)
                for k, t in enumerate((src_f, dst_f, gate_t)):
                    for b in range(TB):
                        last = pe.matmul(ps[:, k, 0:CH], t[:, b, :], sel[:, b, :], start=(b == 0), stop=(b == TB - 1))
                last.then_inc(s.sel_used, 1)

            def node_product(base, rhs, n, per_bank):
                with pe.Fori(0, CHUNKS) as c:
                    pe.wait_ge(s.node_xs, c + (base + 1))
                    for k in range(WPC):
                        last = pe.matmul(region(k, P)[0:D, :], xs[:, k, :], ident[:, :], start=True, stop=True)
                    last.then_inc(s.node_xt, 1)
                    pe.wait_ge(s.node_xtc, c + (base + 1))
                    pe.wait_ge(s.node_evac, c + (base + 1))
                    for k in range(WPC):
                        o = ps[:, 2 + k // per_bank, (k % per_bank) * (512 // per_bank):(k % per_bank) * (512 // per_bank) + n]
                        last = pe.matmul(o, xt[:, k * P:k * P + P], rhs, start=True, stop=True)
                    last.then_inc(s.node_out, 1)

            pe.wait_ge(s.node_in, 1)
            pe.sem_inc(s.l0_sfree, 2)
            node_product(0, wt[0:D, TN:TN + D], D, 4)

            pe.wait_ge(s.node_in, 2)
            with pe.Fori(0, ITER) as i:
                for b in range(2):
                    pe.wait_ge(s.l0_src, i * 2 + b + 1)
                    for u in range(G):
                        last = pe.matmul(region(8 * b + u, P), bc(srcg[:, b, u:u + 1], [P, P]), ident[:, :], start=True, stop=True)
                    last.then_inc(s.l0_srow, 1)
                for b in range(2):
                    g = i * 2 + b
                    pe.wait_ge(s.l0_og, g + 1)
                    pe.wait_ge(s.l0_s, g + 1)
                    for u in range(G):
                        last = pe.matmul(region(16 + u, P), buf_a[:, b, u, :], buf_b[:, b, u, :], start=True, stop=True)
                    last.then_inc(s.l0_b, 1)
                    ws = load8(mybir.EngineType.PE, win_s, g, W - 1)
                    pe.wait_ge(s.l0_bc, g + 1)
                    pe.wait_ge(s.l0_outc, g + 1)
                    for u in range(G):
                        pe.matmul(region(24 + u, D1)[:, D:D1], buf_b[:, b, u, :], step_col(valid_s, g, u), start=True, stop=True)
                        last = pe.matmul(region(24 + u, D), buf_d[:, 0, u, :], window(tab, ws[u], D), start=True, stop=True)
                    last.then_inc(s.l0_out, 1)
                    pe.sem_inc(s.l0_sfree, 1)

            pe.wait_ge(s.node_in, 3)
            node_product(CHUNKS, wt[0:D, TS:TS + 4 * D], 4 * D, 2)

            pe.wait_ge(s.node_in, 4)
            pe.matmul(ps[:, 7, 0:2], tab[:, 0, :], valid_s[:, S:S + 2], start=True, stop=False, skip_group_check=True)
            e_in = [s.e0, s.e1]
            with pe.Fori(0, ITER) as i:
                for b in range(2):
                    pe.wait_ge(e_in[b], i * (G * 16) + G * 16)
                    pe.wait_ge(s.l1_o, i * 2 + b + 1)
                    ob_ps = ps[:, b, :].bitcast(BF16)
                    for u in range(G):
                        pe.transpose(ob_ps[:, u * P:u * P + P], ob[:, b, u, :], ident_b[:, :])
                    for u in range(G // 2):
                        last = pe.transpose(ps[:, 2 + b, u * P:u * P + P],
                                            ea_s[:, b, 2 * u:2 * u + 2, :].rearrange("p a f -> p (a f)"), ident[:, :])
                    last.then_inc(s.l1_t, 1)
                for b in range(2):
                    g = i * 2 + b
                    ws = load8(mybir.EngineType.PE, win_s, g, W - 1)
                    pe.wait_ge(s.l1_tc, g + 1)
                    pe.wait_ge(s.l1_ybank, g + 1)
                    for u in range(G):
                        h = D * (u % 2)
                        o = region(16 + 4 * (u % 2) + u // 2, P)
                        pe.matmul(o, buf_d[:, b, u, :], window(tab, ws[u], P), start=True, stop=False)
                        last = pe.matmul(o, buf_a[h:h + D, b, u // 2, :], wt[h:h + D, TE:TE + 2 * D], start=False, stop=True)
                    last.then_inc(s.l1_ys, 1)
                for b in range(2):
                    g = i * 2 + b
                    pe.wait_ge(s.l1_y, g + 1)
                    pe.wait_ge(s.l1_sq, g + 1)
                    for u in range(G):
                        v = step_col(valid_s, g, u)
                        pe.matmul(ps[:, 7, 0:1], buf_c[:, b, u, :], v, start=False, stop=False, skip_group_check=True)
                        last = pe.matmul(ps[:, 7, 1:2], sq[:, b, u, :], v, start=False, stop=False, skip_group_check=True)
                    last.then_inc(s.l1_stat, 1)
            pe.matmul(ps[:, 7, 0:2], tab[:, 0, :], valid_s[:, S:S + 2], start=False, stop=True, skip_group_check=True).then_inc(s.stat_done, 1)
            pe.wait_ge(s.bn_made, 2)
            for k in range(2):
                last = pe.matmul(ps[:, 6, 2 * D * k:2 * D * k + 2 * D], bc(bn_col[:, k:k + 1], [P, P]), ident[:, :], start=True, stop=True)
            last.then_inc(s.bn_copied, 1)

            def aggregate(left, right, n, left_ready, right_ready, right_step, free, done):
                with pe.Fori(0, ITER) as i:
                    for b in range(2):
                        g = i * 2 + b
                        pe.wait_ge(left_ready, g + 1)
                        if right_step:
                            pe.wait_ge(right_ready[b], i * right_step + right_step)
                        else:
                            pe.wait_ge(right_ready, g + 1)
                        pe.wait_ge(free, g + 1)
                        for u in range(G):
                            last = pe.matmul(region(8 * b + u, n), left[:, b, u, :], right[:, b, u, 0:n], start=True, stop=True)
                        last.then_inc(done, 1)

            aggregate(buf_a, rows, D1, s.lb_o, s.lb_msg, 0, s.lb_accfree, s.lb_out)

            pe.wait_ge(s.node_in, 5)
            node_product(2 * CHUNKS, wt[0:D, TA:TA + D2], D2, 4)
            got = [s.l2_got0, s.l2_got1]
            with pe.Fori(0, ITER) as i:
                for b in range(2):
                    g = i * 2 + b
                    pe.wait_ge(got[b], i * (G * 16) + G * 16)
                    pe.wait_ge(s.l2_nm, g + 1)
                    pe.wait_ge(s.l2_maskfree, g + 1)
                    for u in range(G):
                        pe.matmul(region(8 * b + u, P), buf_a[:, b, u, :], ident[:, :], start=True, stop=False)
                        last = pe.matmul(region(8 * b + u, P), bc(rows[:, b, u, D1:D2], [P, P]), ident[:, :], start=False, stop=True)
                    last.then_inc(s.l2_mask, 1)
            pe.wait_ge(s.mx_done, 1)
            with pe.Fori(0, ITER) as i:
                for b in range(2):
                    pe.wait_ge(s.l2b_o, i * 2 + b + 1)
                    for u in range(G):
                        last = pe.transpose(ps[:, b, :].bitcast(BF16)[:, u * P:u * P + P], ob[:, b, u, :], ident_b[:, :])
                    last.then_inc(s.l2b_t, 1)
                for b in range(2):
                    g = i * 2 + b
                    ws = load8(mybir.EngineType.PE, win_s, g, W - 1)
                    pe.wait_ge(s.l2b_tc, g + 1)
                    for u in range(G):
                        last = pe.matmul(ps[:, 2 + b, 2 * u:2 * u + 2], buf_d[:, b, u, :], window(sums, ws[u], 2), start=True, stop=True)
                    last.then_inc(s.l2b_s, 1)
                for b in range(2):
                    g = i * 2 + b
                    pe.wait_ge(s.l2b_ow, g + 1)
                    pe.wait_ge(s.l2b_accfree, g + 1)
                    for u in range(G):
                        last = pe.matmul(region(16 + 8 * b + u, D1), buf_a[:, b, u, :], rows[:, b, u, 0:D1], start=True, stop=True)
                    last.then_inc(s.l2b_out, 1)
            aggregate(buf_a, rows, D, s.g0_o, [s.g0_got0, s.g0_got1], G * 16, s.g0_accfree, s.g0_out)
            pe.wait_ge(s.node_in, 6)
            node_product(3 * CHUNKS, w12[:, 0, :], D, 4)
            aggregate(buf_a, rows, D, s.g1_o, [s.g1_got0, s.g1_got1], G * 16, s.g1_accfree, s.g1_out)
            pe.wait_ge(s.node_in, 7)
            node_product(4 * CHUNKS, w12[:, 1, :], D, 4)

        @block.vector
        def _(dve):
            count = [0]

            def link(ins):
                count[0] += 1
                ins.then_inc(s.dve, 1)
                dve.wait_ge(s.dve, count[0])

            dve.wait_ge(s.iotas_made, 2)
            link(dve.tensor_copy(step_f, step_i))
            link(dve.tensor_copy(ids[:, :], scr_i[:, 0:TB]))
            link(dve.tensor_copy(iota[:, :], step_f[:, 0:P]))
            link(dve.tensor_scalar(ident[:, :], iota[:, :], ids[:, 0:1], None, ALU.is_equal))
            link(dve.tensor_copy(ident_b[:, :], ident[:, :]))
            link(dve.tensor_scalar(below[:, :], iota[:, :], ids[:, 0:1], None, ALU.is_lt))
            link(dve.tensor_scalar(trash[:, :], ids[:, 0:1], float(TRASH), None, ALU.add))
            link(dve.memset(ones[:, :], 1.0))
            for t, v in ((src_s, 0.0), (dst_s, -1.0), (gate_s, 0.0), (valid_s, 0.0)):
                link(dve.memset(t[:, S:SPAD], v))
            link(dve.memset(win_s[:, S:SPAD], 0))
            link(dve.memset(row_s[:, S:SPAD], 0))
            dve.sem_inc(s.consts_made, 1)
            dve.wait_ge(s.tiles_loaded, 96)
            link(dve.tensor_copy(src_f, src_t))
            link(dve.tensor_copy(dst_f, dst_t))
            link(dve.tensor_reduce(last_i[:, :], dst_t, AX.X, ALU.max))
            link(dve.tensor_scalar(last_i[:, :], last_i[:, :], 7, None, ALU.arith_shift_right))
            link(dve.tensor_copy(key[:, :], last_i[:, :]))
            dve.tensor_tensor(key[:, :], key[:, :], ids[:, :], ALU.add).then_inc(s.key_ready, 1)
            dve.wait_ge(s.keyrow_made, 1)
            key_row = ps[:, 0:4, :].rearrange("p a b -> p (a b)")[:, 0:TB * P]
            for c in range(SB):
                link(dve.tensor_scalar(junk, key_row, ids[:, c:c + 1], None, ALU.is_lt, ALU.add, accum_out=t_col[:, c:c + 1]))
            dve.sem_inc(s.tcol_ready, 1)
            dve.wait_ge(s.weights_loaded, 16 * 9)

            def gate_block(b, slot):
                v = x_flat[:, slot * EB:(slot + 1) * EB].rearrange("p (e k) -> p e k", k=K16)
                link(dve.tensor_tensor(v, v, bc(we_bc[:, :].unsqueeze(1), [P, P, K16]), ALU.mult))
                link(dve.tensor_reduce(gate_t[:, b, :], v, AX.X, ALU.add))

            dve.wait_ge(s.ea_loaded0, 16 * 6)
            for b in range(6):
                gate_block(b, b)
            dve.sem_inc(s.ea_clean, 1)
            dve.wait_ge(s.ea_loaded1, 16 * 6)
            for b in range(6):
                gate_block(6 + b, b)
            link(dve.memset(x_flat[:, 0:EB], 0.0))
            dve.sem_inc(s.ea_clean, 1)
            dve.wait_ge(s.ea_loaded1, 16 * 8)
            gate_block(12, 0)
            dve.sem_inc(s.gate_lin, 1)
            dve.wait_ge(s.trow_made, 1)
            trow_ps = ps[:, 4:8, :].rearrange("p a b -> p (a b)")[:, 0:S]
            link(dve.tensor_copy(t_row, trow_ps))
            link(dve.tensor_tensor(w_row, step_f, t_row, ALU.subtract))
            link(dve.tensor_scalar(win_s[:, 0:S], w_row[0:1, :], float(W - 1), None, ALU.min))
            link(dve.tensor_scalar(row_s[:, 0:S], t_row[32:33, :], float(P), float(E - P), ALU.mult, ALU.min))
            dve.sem_inc(s.trow_copied, 1)
            dve.sem_inc(s.sel_used, 1)
            with dve.Fori(0, 4) as c:
                at = bass.ds(c * CH, CH)
                for b in range(TB):
                    last = dve.tensor_scalar(sel[:, b, :], t_row[:, at], ids[:, b:b + 1], None, ALU.is_equal)
                last.then_inc(s.sel_made, 1)
                dve.wait_ge(s.sel_used, c + 2)
                dve.tensor_copy(src_s[:, at], ps[:, 0, 0:CH])
                dve.scalar_tensor_tensor(dst_s[:, at], w_row[:, at], -float(P), ps[:, 1, 0:CH], ALU.mult, ALU.add)
                dve.tensor_copy(gate_s[:, at], ps[:, 2, 0:CH]).then_inc(s.steps_made, 1)
                dve.wait_ge(s.steps_made, c + 1)
            link(dve.tensor_scalar(valid_s[:, 0:S], dst_s[:, 0:S], 0.0, None, ALU.is_ge))
            link(dve.scalar_tensor_tensor(valid_s[:, 0:S], dst_s[:, 0:S], float(P), valid_s[:, 0:S], ALU.is_lt, ALU.mult))
            link(dve.memset(tab_flat, 0.0))
            dve.sem_inc(s.fill_ready, 1)
            dve.wait_ge(s.bias_loaded, 16 * 9)
            dve.wait_ge(s.x_loaded, 32)
            dve.wait_ge(s.wt_copied, 4)
            dve.wait_ge(s.fill_ready, 2)
            dve.sem_inc(s.node_in, 1)

            def products(per_bank, k0, k1):
                n = 512 // per_bank
                b0 = 2 + k0 // per_bank
                return ps[:, b0:b0 + 1, 0:(k1 - k0) * n].rearrange("p a (k f) -> p (a k) f", f=n)

            def to_tab0(c):
                for k0, k1 in ((0, 4), (4, 7)):
                    last = dve.tensor_tensor(tab[:, bass.ds(c * WPC + k0, k1 - k0), 0:D], products(4, k0, k1)[:, :, 0:D],
                                             bc(bias0[:, :].unsqueeze(1), [P, k1 - k0, D]), ALU.add)
                last.then_inc(s.node_evac, 1)

            dve.sem_inc(s.node_evac, 1)
            with dve.Fori(0, CHUNKS) as c:
                dve.wait_ge(s.node_out, c + 1)
                to_tab0(c)
            dve.wait_ge(s.node_evac, CHUNKS + 1)
            dve.sem_inc(s.node_in, 1)

            dve.sem_inc(s.l0_outc, 1)
            dve.sem_inc(s.l0_done, 1)
            KL0 = 5
            with dve.Fori(0, ITER) as i:
                for b in range(2):
                    dve.wait_ge(s.l0_sfree, i * 2 + b + 1)
                    dve.tensor_copy(srcg[:, b, :], step_slice(src_s, i * 2 + b)).then_inc(s.l0_src, 1)
                for b in range(2):
                    g = i * 2 + b
                    for u in range(G):
                        last = dve.tensor_scalar(buf_a[:, b, u, :], iota[:, :], step_col(dst_s, g, u), step_col(gate_s, g, u),
                                                 ALU.is_equal, ALU.mult)
                    last.then_inc(s.l0_og, 1)
                for b in range(2):
                    g = i * 2 + b
                    dve.wait_ge(s.l0_srow, g + 1)
                    dve.tensor_tensor(buf_b[:, b, :, :], regions(2 * b, P), bc(srcg[:, b, :].unsqueeze(2), [P, G, P]),
                                      ALU.is_equal).then_inc(s.l0_s, 1)
                    dve.wait_ge(s.l0_s, g + 1)
                    k = 0

                    def chain(ins):
                        nonlocal k
                        k += 1
                        ins.then_inc(s.l0_dve, 1)
                        dve.wait_ge(s.l0_dve, i * (2 * KL0) + (b * KL0 + k))
                    chain(dve.tensor_tensor(buf_c[:, b, :, :], buf_b[:, b, :, :], bc(below[:, :].unsqueeze(1), [P, G, P]), ALU.mult))
                    chain(dve.tensor_reduce(dup[:, b, :], buf_c[:, b, :, :], AX.X, ALU.max))
                    chain(dve.tensor_scalar(tmp_c[:, b, :], srcg[:, b, :], -1.0, trash[:, 0:1], ALU.mult, ALU.add))
                    chain(dve.tensor_tensor(tmp_c[:, b, :], tmp_c[:, b, :], dup[:, b, :], ALU.mult))
                    dve.wait_ge(s.l0_done, g + 1)
                    dve.tensor_tensor(idx[:, b, :], tmp_c[:, b, :], srcg[:, b, :], ALU.add).then_inc(s.l0_idx, 1)
                    dve.wait_ge(s.l0_idx, g + 1)
                    k += 1
                    dve.sem_inc(s.l0_dve, 1)
                    assert k == KL0

            def norm(t, n):
                link(dve.tensor_reduce(col_a[:, :], t, AX.X, ALU.add))
                link(dve.tensor_scalar(col_a[:, :], col_a[:, :], 1.0 / D, None, ALU.mult))
                link(dve.tensor_tensor(t, t, bc(col_a[:, :].unsqueeze(2), [P, W, D]), ALU.subtract))
                link(dve.tensor_tensor(scratch, t, t, ALU.mult))
                link(dve.tensor_reduce(col_a[:, :], scratch, AX.X, ALU.add))
                dve.tensor_scalar(col_a[:, :], col_a[:, :], 1.0 / D, EPS, ALU.mult, ALU.add).then_inc(s.ln_var, 1)
                dve.wait_ge(s.ln_std, n)
                link(dve.reciprocal(col_b[:, :], col_b[:, :]))
                link(dve.tensor_tensor(x_n[:, :, :], t, bc(col_b[:, :].unsqueeze(2), [P, W, D]), ALU.mult))

            tab_l = tab_flat[:, 0:W * D1].rearrange("p (w f) -> p w f", f=D1)
            dve.wait_ge(lane_in[0], 16)
            dve.wait_ge(lane_in[1], 16)
            link(dve.tensor_tensor(acc[:, :, :], acc[:, :, :], aux[:, :, :], ALU.add))
            dve.sem_inc(s.lane_again, 1)
            dve.wait_ge(lane_in[2], 16)
            link(dve.tensor_tensor(acc[:, :, :], acc[:, :, :], tab_l, ALU.add))
            dve.wait_ge(lane_in[3], 16)
            link(dve.tensor_tensor(acc[:, :, :], acc[:, :, :], aux[:, :, :], ALU.add))
            sums_d = acc[:, :, 0:D]
            last_d = acc[:, :, D:D1].rearrange("p w a -> p (w a)")
            link(dve.tensor_scalar(col_a[:, :], last_d, 1.0, None, ALU.max))
            link(dve.reciprocal(col_b[:, :], col_a[:, :]))
            link(dve.tensor_tensor(sums_d, sums_d, bc(col_b[:, :].unsqueeze(2), [P, W, D]), ALU.mult))
            link(dve.tensor_tensor(sums_d, sums_d, x_n[:, :, :], ALU.add))
            norm(sums_d, 1)
            dve.sem_inc(s.node_in, 1)

            dve.sem_inc(s.stage_free, 1)
            with dve.Fori(0, CHUNKS) as c:
                dve.wait_ge(s.node_out, c + (CHUNKS + 1))
                dve.wait_ge(s.stage_free, c + 1)
                for k0 in range(0, WPC, 2):
                    k1 = min(k0 + 2, WPC)
                    pr = products(2, k0, k1)
                    last_stage = dve.tensor_copy(stage[:, k0:k1, :], pr[:, :, 0:2 * D])
                    last = dve.tensor_tensor(tab[:, bass.ds(c * WPC + k0, k1 - k0), :], pr[:, :, 2 * D:4 * D],
                                             bc(bias_d[:, :].unsqueeze(1), [P, k1 - k0, 2 * D]), ALU.add)
                last_stage.then_inc(s.stage_full, 1)
                last.then_inc(s.node_evac, 1)
            dve.wait_ge(s.node_evac, 2 * CHUNKS + 1)
            dve.wait_ge(s.stage_free, CHUNKS + 1)
            dve.sem_inc(s.node_in, 1)

            dve.sem_inc(s.l1_gfree, 2)
            dve.sem_inc(s.l1_yfree, 2)
            dve.sem_inc(s.l1_stat, 2)
            dve.sem_inc(s.l1_ybank, 1)
            got = [s.l1_got0, s.l1_got1]
            with dve.Fori(0, ITER) as i:
                for b in range(2):
                    g = i * 2 + b
                    for u in range(G):
                        last = dve.tensor_scalar(ob[:, b, u, :], iota[:, :], step_col(dst_s, g, u), None, ALU.is_equal)
                    last.then_inc(s.l1_o, 1)
                for b in range(2):
                    g = i * 2 + b
                    dve.wait_ge(s.l1_yfree, g + 1)
                    dve.wait_ge(s.l1_stat, g + 1)
                    dve.wait_ge(s.l1_ys, g + 1)
                    dve.wait_ge(got[b], i * (G * 16) + G * 16)
                    dve.tensor_tensor(by_bank(buf_c[:, b, :, :]), ps[:, 4:6, :].rearrange("p c (k f) -> p c k f", f=P),
                                      by_bank(buf_b[:, b, :, :]), ALU.add).then_inc(s.l1_y, 1)
                    dve.wait_ge(s.l1_y, g + 1)
                    dve.sem_inc(s.l1_gfree, 1)
                    dve.sem_inc(s.l1_ybank, 1)
            dve.wait_ge(s.stat_done, 1)
            scale, shift, gam, bet, mean, var, std = (bn_col[:, k:k + 1] for k in (0, 1, 2, 3, 5, 6, 7))
            link(dve.tensor_scalar(mean, ps[:, 7, 0:1], 1.0 / E, None, ALU.mult))
            link(dve.tensor_scalar(var, ps[:, 7, 1:2], 1.0 / E, None, ALU.mult))
            link(dve.tensor_tensor(scale, mean, mean, ALU.mult))
            link(dve.tensor_tensor(var, var, scale, ALU.subtract))
            dve.tensor_scalar(var, var, 0.0, EPS, ALU.max, ALU.add).then_inc(s.bn_ready, 1)
            dve.wait_ge(s.bn_made, 1)
            link(dve.reciprocal(var, std))
            link(dve.tensor_tensor(scale, var, gam, ALU.mult))
            link(dve.tensor_tensor(mean, mean, scale, ALU.mult))
            dve.tensor_tensor(shift, bet, mean, ALU.subtract).then_inc(s.bn_made, 1)
            dve.wait_ge(s.bn_copied, 1)
            link(dve.tensor_copy(bn[:, :, :].rearrange("p a b -> p (a b)"), ps[:, 6, 0:4 * D]))

            def add_window(g, u, b, bank, ws, n, order):
                a = window(acc, ws[u], n)
                dve.wait_ge(order, g * G + (u + 1))
                return dve.tensor_tensor(a, a, region(4 * bank + 8 * b + u, n), ALU.add).then_inc(order, 1)

            link(dve.memset(rows[:, :, :, D:D2], 1.0))
            dve.memset(acc[:, :, :], 0.0).then_inc(s.lb_acc, 1)
            dve.sem_inc(s.lb_zfree, 2)
            dve.sem_inc(s.lb_accfree, 2)
            y_in = [s.lb_y0, s.lb_y1]
            KLB = 4
            with dve.Fori(0, ITER) as i:
                for b in range(2):
                    g = i * 2 + b
                    k = 0

                    def chain(ins):
                        nonlocal k
                        k += 1
                        ins.then_inc(s.lb_dve, 1)
                        dve.wait_ge(s.lb_dve, i * (2 * KLB) + (b * KLB + k))
                    z = buf_d[:, b, :, :]
                    for u in range(G):
                        last = dve.tensor_scalar(buf_a[:, b, u, :], iota[:, :], step_col(dst_s, g, u), None, ALU.is_equal)
                    last.then_inc(s.lb_o, 1)
                    dve.wait_ge(y_in[b], i * 16 + 16)
                    dve.tensor_tensor(z, buf_c[:, b, :, :], bc(bn[:, 0:1, :], [P, G, 2 * D]), ALU.mult).then_inc(s.lb_z, 1)
                    dve.wait_ge(s.lb_z, g + 1)
                    dve.sem_inc(s.lb_zfree, 1)
                    chain(dve.tensor_tensor(z, z, bc(bn[:, 1:2, :], [P, G, 2 * D]), ALU.add))
                    dve.scalar_tensor_tensor(buf_b[:, b, :, 0:D], z[:, :, 0:D], -1.0, z[:, :, 0:D], ALU.mult, ALU.min).then_inc(s.lb_abs, 1)
                    dve.wait_ge(s.lb_exp, i * 4 + (2 * b + 1))
                    chain(dve.tensor_scalar(z[:, :, D:2 * D], z[:, :, D:2 * D], 1.0, None, ALU.add))
                    chain(dve.reciprocal(z[:, :, D:2 * D], z[:, :, D:2 * D]))
                    dve.wait_ge(s.lb_exp, i * 4 + (2 * b + 2))
                    chain(dve.scalar_tensor_tensor(z[:, :, 0:D], z[:, :, 0:D], 0.0, buf_b[:, b, :, D:2 * D], ALU.max, ALU.add))
                    dve.tensor_tensor(rows[:, b, :, 0:D], z[:, :, 0:D], z[:, :, D:2 * D], ALU.mult).then_inc(s.lb_msg, 1)
                    assert k == KLB
                for b in range(2):
                    g = i * 2 + b
                    ws = load8(mybir.EngineType.DVE, win_s, g, W - 1)
                    dve.wait_ge(s.lb_out, g + 1)
                    for u in range(G):
                        add_window(g, u, b, 0, ws, D1, s.lb_acc)
                    dve.wait_ge(s.lb_acc, g * G + (G + 1))
                    dve.sem_inc(s.lb_accfree, 1)
            link(dve.tensor_copy(deg[:, :], last_d))
            link(dve.scalar_tensor_tensor(sums_d, x_n[:, :, :], 2.0, sums_d, ALU.mult, ALU.add))
            norm(sums_d, 2)
            dve.sem_inc(s.node_in, 1)

            link(dve.memset(stage[:, 0:WPC, D:D1], 1.0))
            with dve.Fori(0, CHUNKS) as c:
                dve.wait_ge(s.node_out, c + (2 * CHUNKS + 1))
                dve.wait_ge(s.stage_free, c + (CHUNKS + 1))
                for k0, k1 in ((0, 4), (4, 7)):
                    pr = products(4, k0, k1)
                    dve.tensor_copy(stage[:, k0:k1, 0:D], pr[:, :, 0:D])
                    last_stage = dve.tensor_copy(stage[:, k0:k1, D1:D2], pr[:, :, D:D1])
                    last = dve.tensor_copy(sums[:, bass.ds(c * WPC + k0, k1 - k0), 0:1], pr[:, :, D1:D2])
                last_stage.then_inc(s.stage_full, 1)
                last.then_inc(s.node_evac, 1)
            dve.wait_ge(s.stage_free, 2 * CHUNKS + 1)
            dve.wait_ge(s.node_evac, 3 * CHUNKS + 1)
            dve.memset(mx[:, :], -BIG).then_inc(s.l2_mx, 1)
            dve.sem_inc(s.l2_maskfree, 2)
            dve.sem_inc(s.l2_hfree, 2)
            with dve.Fori(0, ITER) as i:
                for b in range(2):
                    g = i * 2 + b
                    for u in range(G):
                        last = dve.tensor_scalar(buf_a[:, b, u, :], iota[:, :], step_col(dst_s, g, u), -BIG, ALU.not_equal, ALU.mult)
                    last.then_inc(s.l2_nm, 1)
                for b in range(2):
                    g = i * 2 + b
                    ws = load8(mybir.EngineType.DVE, win_s, g, W - 1)
                    dve.wait_ge(s.l2_mask, g + 1)
                    dve.tensor_reduce(tmp_c[:, b, :], regions(2 * b, P), AX.X, ALU.max).then_inc(s.l2_max, 1)
                    dve.wait_ge(s.l2_max, g + 1)
                    dve.sem_inc(s.l2_maskfree, 1)
                    for u in range(G):
                        m = mx[:, bass.ds(ws[u], 1)]
                        dve.wait_ge(s.l2_mx, g * G + (u + 1))
                        dve.tensor_tensor(m, m, tmp_c[:, b, u:u + 1], ALU.max).then_inc(s.l2_mx, 1)
            dve.wait_ge(s.l2_mx, S + 1)
            sc, mxc = sums[:, :, 0:1].rearrange("p w a -> p (w a)"), sums[:, :, 1:2].rearrange("p w a -> p (w a)")
            link(dve.tensor_tensor(col_a[:, :], mx[:, :], sc, ALU.add))
            link(dve.scalar_tensor_tensor(mxc, col_a[:, :], 0.2, col_a[:, :], ALU.mult, ALU.max))
            dve.sem_inc(s.mx_done, 1)

            dve.memset(acc[:, :, :], 0.0).then_inc(s.l2b_acc, 1)
            dve.sem_inc(s.l2b_hfree, 2)
            dve.sem_inc(s.l2b_accfree, 2)
            h_in = [s.l2b_h0, s.l2b_h1]
            KL2 = 3
            with dve.Fori(0, ITER) as i:
                for b in range(2):
                    g = i * 2 + b
                    for u in range(G):
                        last = dve.tensor_scalar(ob[:, b, u, :], iota[:, :], step_col(dst_s, g, u), None, ALU.is_equal)
                    last.then_inc(s.l2b_o, 1)
                for b in range(2):
                    g = i * 2 + b
                    k = 0

                    def chain(ins):
                        nonlocal k
                        k += 1
                        ins.then_inc(s.l2b_dve, 1)
                        dve.wait_ge(s.l2b_dve, i * (2 * KL2) + (b * KL2 + k))
                    per_edge = ps[:, 2 + b, 0:2 * G].rearrange("p (u k) -> p u k", k=2)
                    score = tmp_c[:, b, :]
                    dve.wait_ge(h_in[b], i * 16 + 16)
                    dve.wait_ge(s.l2b_s, g + 1)
                    chain(dve.tensor_tensor(score, rows[:, b, :, D1:D2].rearrange("p u a -> p (u a)"),
                                            per_edge[:, :, 0:1].rearrange("p u a -> p (u a)"), ALU.add))
                    chain(dve.scalar_tensor_tensor(score, score, 0.2, score, ALU.mult, ALU.max))
                    chain(dve.tensor_tensor(score, score, per_edge[:, :, 1:2].rearrange("p u a -> p (u a)"), ALU.subtract))
                    dve.tensor_scalar(tmp_c[:, 2 + b, :], score, 0.0, None, ALU.min).then_inc(s.l2b_arg, 1)
                    assert k == KL2
                for b in range(2):
                    g = i * 2 + b
                    dve.wait_ge(s.l2b_exp, g + 1)
                    for u in range(G):
                        last = dve.tensor_scalar(buf_a[:, b, u, :], iota[:, :], step_col(dst_s, g, u), ex[:, b, u:u + 1],
                                                 ALU.is_equal, ALU.mult)
                    last.then_inc(s.l2b_ow, 1)
                for b in range(2):
                    g = i * 2 + b
                    ws = load8(mybir.EngineType.DVE, win_s, g, W - 1)
                    dve.wait_ge(s.l2b_out, g + 1)
                    dve.sem_inc(s.l2b_hfree, 1)
                    for u in range(G):
                        add_window(g, u, b, 4, ws, D1, s.l2b_acc)
                    dve.wait_ge(s.l2b_acc, g * G + (G + 1))
                    dve.sem_inc(s.l2b_accfree, 1)
            link(dve.tensor_scalar(col_a[:, :], last_d, 1e-30, None, ALU.max))
            link(dve.reciprocal(col_b[:, :], col_a[:, :]))
            link(dve.tensor_tensor(sums_d, sums_d, bc(col_b[:, :].unsqueeze(2), [P, W, D]), ALU.mult))
            dve.tensor_scalar(scratch, sums_d, 0.0, None, ALU.min).then_inc(s.elu_in, 1)
            link(dve.scalar_tensor_tensor(sums_d, sums_d, 0.0, x_n[:, :, :], ALU.max, ALU.add))
            dve.wait_ge(s.elu_out, 1)
            link(dve.scalar_tensor_tensor(sums_d, scratch, -1.0, sums_d, ALU.add, ALU.add))
            norm(sums_d, 3)
            dinv = mx[:, :]
            dve.tensor_scalar(col_a[:, :], deg[:, :], 1.0, None, ALU.max).then_inc(s.ln_var, 1)
            dve.wait_ge(s.ln_std, 4)
            link(dve.reciprocal(col_b[:, :], col_b[:, :]))
            link(dve.scalar_tensor_tensor(dinv, deg[:, :], 0.0, col_b[:, :], ALU.is_gt, ALU.mult))
            dinv_bc = bc(mx[:, :].unsqueeze(2), [P, W, D])

            link(dve.tensor_tensor(tab_d, x_n[:, :, :], dinv_bc, ALU.mult))
            dve.sem_inc(s.gcn_in0, 1)

            def gcn(got, o, outs, accfree, gfree, order):
                dve.memset(acc[:, :, :], 0.0).then_inc(order, 1)
                dve.sem_inc(accfree, 2)
                dve.sem_inc(gfree, 2)
                with dve.Fori(0, ITER) as i:
                    for b in range(2):
                        g = i * 2 + b
                        for u in range(G):
                            last = dve.tensor_scalar(buf_a[:, b, u, :], iota[:, :], step_col(dst_s, g, u), None, ALU.is_equal)
                        last.then_inc(o, 1)
                    for b in range(2):
                        g = i * 2 + b
                        ws = load8(mybir.EngineType.DVE, win_s, g, W - 1)
                        dve.wait_ge(outs, g + 1)
                        dve.sem_inc(gfree, 1)
                        for u in range(G):
                            add_window(g, u, b, 0, ws, D, order)
                        dve.wait_ge(order, g * G + (G + 1))
                        dve.sem_inc(accfree, 1)

            gcn([s.g0_got0, s.g0_got1], s.g0_o, s.g0_out, s.g0_accfree, s.g0_gfree, s.g0_acc)
            dve.wait_ge(s.gcn_st0, 16)
            link(dve.tensor_tensor(tab_d, sums_d, dinv_bc, ALU.mult))
            dve.sem_inc(s.node_in, 1)
            with dve.Fori(0, CHUNKS) as c:
                dve.wait_ge(s.node_out, c + (3 * CHUNKS + 1))
                for k0, k1 in ((0, 4), (4, 7)):
                    last = dve.tensor_tensor(acc[:, bass.ds(c * WPC + k0, k1 - k0), 0:D], products(4, k0, k1)[:, :, 0:D],
                                             bc(bias3[:, 0:1, :], [P, k1 - k0, D]), ALU.add)
                last.then_inc(s.node_evac, 1)
            dve.wait_ge(s.node_evac, 4 * CHUNKS + 1)
            link(dve.scalar_tensor_tensor(tab_d, sums_d, 0.0, dinv_bc, ALU.max, ALU.mult))
            dve.sem_inc(s.gcn_in1, 1)
            gcn([s.g1_got0, s.g1_got1], s.g1_o, s.g1_out, s.g1_accfree, s.g1_gfree, s.g1_acc)
            dve.wait_ge(s.gcn_st1, 16)
            link(dve.tensor_tensor(tab_d, sums_d, dinv_bc, ALU.mult))
            dve.sem_inc(s.node_in, 1)
            with dve.Fori(0, CHUNKS) as c:
                dve.wait_ge(s.node_out, c + (4 * CHUNKS + 1))
                for k0, k1 in ((0, 4), (4, 7)):
                    last = dve.tensor_tensor(acc[:, bass.ds(c * WPC + k0, k1 - k0), 0:D], products(4, k0, k1)[:, :, 0:D],
                                             bc(bias3[:, 1:2, :], [P, k1 - k0, D]), ALU.add)
                last.then_inc(s.node_evac, 1)
            dve.wait_ge(s.node_evac, 5 * CHUNKS + 1)
            link(dve.tensor_tensor(sums_d, sums_d, x_n[:, :, :], ALU.add))
            norm(sums_d, 5)
            dve.sem_inc(s.result_ready, 1)


_INS = ['x', 'src', 'dst', 'edge_attr_16', 'edge_attr_64', 'L0_gnn_W_edge', 'L0_gnn_b_edge', 'L0_gnn_W_node', 'L0_gnn_b_node',
        'L1_gnn_W_filter', 'L1_gnn_b_filter', 'L1_gnn_gamma_filter', 'L1_gnn_beta_filter',
        'L1_gnn_W_core', 'L1_gnn_b_core', 'L1_gnn_gamma_core', 'L1_gnn_beta_core',
        'L2_gnn_W', 'L2_gnn_a', 'L3_gnn_W1', 'L3_gnn_b1', 'L3_gnn_W2', 'L3_gnn_b2']


def kernel(**inputs):
    import numpy as _np
    import concourse.bacc as _bacc
    from concourse import mybir as _mybir
    from concourse.bass_utils import run_bass_kernel_spmd as _run

    nc = _bacc.Bacc("TRN2", target_bir_lowering=False, num_devices=1)
    arrays, args = {}, []
    for name in _INS:
        a = _np.ascontiguousarray(inputs[name])
        arrays[f"in_{name}_dram"] = a
        args.append(nc.dram_tensor(f"in_{name}_dram", a.shape, _mybir.dt.from_np(a.dtype), kind="ExternalInput").ap())
    out = nc.dram_tensor("out_dram", (N, D), _mybir.dt.float32, kind="ExternalOutput").ap()
    build(nc, *args, out)
    r = _run(nc, [arrays], core_ids=[0])
    return r.results[0]["out_dram"]
```

```python
from collections import namedtuple
from contextlib import ExitStack

import concourse.bass as bass
from concourse import mybir

ALU = mybir.AluOpType
ACT = mybir.ActivationFunctionType
AX = mybir.AxisListType
F32 = mybir.dt.float32
BF16 = mybir.dt.bfloat16
I32 = mybir.dt.int32

P = 128
N = 12500
E = 200000
D = 64
K16 = 16
W = -(-N // P)
NP = W * P
FULL_W = N // P
TAIL_N = N - FULL_W * P
T = -(-E // P)
FULL_T = E // P
HALF = E - FULL_T * P
TB = -(-T // P)
TAIL_T = FULL_T - (TB - 1) * P
G = 8
PAIR = 2 * G
S = -(-(T + W - 1) // P) * P
SB = S // P
ITER = S // PAIR
SPAD = S + 2 * PAIR
CH = S // 4
NOWHERE = 1 << 20
TRASH = NP
SROWS = NP + P
LANES = 4
WPC = 7
CHUNKS = W // WPC
D1 = D + 1
D2 = D + 2
BIG = 2.0 ** 100
EPS = 1e-5
assert CHUNKS * WPC == W and ITER % 2 == 0 and ITER * PAIR == S and CH <= 512


def build(nc, x, src, dst, ea16, ea64, w_edge, b_edge, w_node, b_node,
          w_filter, b_filter, gamma_f, beta_f, w_core, b_core, gamma_c, beta_c,
          w_att, a_att, w1, b1, w2, b2, out):
    with ExitStack() as ctx:
        def sb(name, shape, dt=F32):
            return ctx.enter_context(nc.sbuf_tensor(name, shape, dt))

        def sem(name):
            return ctx.enter_context(nc.semaphore(name))

        def dram(name, shape, dt=F32):
            return nc.dram_tensor(name, shape, dt, kind="Internal").ap()

        lane_tab = [dram(f"lane_tab{k}", (SROWS, D1)) for k in range(LANES)]
        src_tab = dram("src_tab", (NP, 2 * D))
        att_tab = dram("att_tab", (NP, D2))
        gcn_tab = [dram(f"gcn_tab{k}", (NP, D)) for k in range(2)]
        y_stash = dram("y_stash", (2 * ITER, P, G * 2 * D))
        h_stash = dram("h_stash", (2 * ITER, P, G * D2))

        x_n = sb("x_n", [P, W, D])
        acc_w = sb("acc_w", [P, W + G, D1])
        acc = acc_w[:, 0:W, :]
        tab = sb("tab", [P, W, 2 * D])
        aux = sb("aux", [P, W, D1])
        src_s = sb("src_s", [P, SPAD])
        dst_s = sb("dst_s", [P, SPAD])
        gate_s = sb("gate_s", [P, SPAD])
        valid_s = sb("valid_s", [P, SPAD])
        place_s = sb("place_s", [2 * 32 + 1, SPAD], I32)
        win_s, row_s, rel_s = place_s[0:1, :], place_s[32:33, :], place_s[64:65, :]
        buf_a = sb("buf_a", [P, 2, G, 2 * D])
        buf_b = sb("buf_b", [P, 2, G, 2 * D])
        buf_c = sb("buf_c", [P, 2, G, 2 * D])
        buf_d = sb("buf_d", [P, 2, G, 2 * D])
        rows = sb("rows", [P, 2, G, D2])
        sums = sb("sums", [P, W, 2])
        sums_b = sb("sums_b", [P, W, 6], BF16)
        mx = sb("mx", [P, W])
        col_a = sb("col_a", [P, W])
        col_b = sb("col_b", [P, W])
        idx = sb("idx", [P, 2, G], I32)
        idxf = sb("idxf", [P, 2, G])
        srcg = sb("srcg", [P, 2, G])
        dup = sb("dup", [P, 2, G])
        tmp_c = sb("tmp_c", [P, 4, G])
        ex = sb("ex", [P, 2, G])
        target = sb("target", [P, 2, G, 2])
        iota = sb("iota", [P, P])
        ident = sb("ident", [P, P])
        ident_b = sb("ident_b", [P, P], BF16)
        zero_b = sb("zero_b", [P, P], BF16)
        below = sb("below", [P, P])
        ids = sb("ids", [P, TB])
        trash = sb("trash", [P, 1])
        ones = sb("ones", [P, P])
        key = sb("key", [P, TB])
        last_i = sb("last_i", [P, TB], I32)
        t_col = sb("t_col", [P, TB])
        wsm = rows[:, :, :, :].rearrange("p a b c -> p (a b c)")[:, 512:1024]
        wt = sb("wt", [P, 640])
        bias0 = sb("bias0", [P, D])
        bias_d = sb("bias_d", [P, 2 * D])
        bias3 = sb("bias3", [P, 2, D])
        we_bc = sb("we_bc", [P, K16])
        be_c = sb("be_c", [P, 1])
        bn_col = sb("bn_col", [P, 8])
        bn = sb("bn", [P, 2, 2 * D])
        deg = sb("deg", [P, W])

        aux_flat = aux[:, :, :].rearrange("p a b -> p (a b)")
        ob = aux_flat[:, 0:G * P].bitcast(BF16).rearrange("p (b u f) -> p b u f", b=2, u=G)
        ot_b = buf_d[:, 0, :, :].rearrange("p u f -> p (u f)").bitcast(BF16).rearrange("p (b u f) -> p b u f", b=2, u=G)
        sq = aux_flat[:, G * P:3 * G * P].rearrange("p (b u f) -> p b u f", b=2, u=G)
        ea_s = aux_flat[:, 3 * G * P:5 * G * P].rearrange("p (q u f) -> p q u f", q=4, u=G)
        acc_flat = acc_w[:, :, :].rearrange("p a b -> p (a b)")
        stat = acc_flat[:, 0:2 * G * P].rearrange("p (k u f) -> p k u f", k=2, u=G)
        yv = acc_flat[:, 2 * G * P:4 * G * P].rearrange("p (b u f) -> p b u f", b=2, u=G)
        y_buf = tab[:, 0:4 * G, :].rearrange("p (q u) f -> p q u f", q=4)
        z_buf = tab[:, 4 * G:8 * G, :].rearrange("p (q u) f -> p q u f", q=4)
        hot2 = tab[:, 8 * G:10 * G, :].rearrange("p (b u) f -> p b u f", b=2)
        lb_hot, lb_rows = [buf_a, hot2], [buf_c, buf_d]
        l2b_hot, l2b_rows = [buf_a, hot2], [buf_c, buf_b]
        xs = aux_flat[:, 4 * G * P:4 * G * P + WPC * D].rearrange("p (w f) -> p w f", f=D)
        xt = aux_flat[0:D, W * D1 - WPC * P:W * D1]

        ps = ctx.enter_context(nc.psum_tensor("ps", [P, 8, 512], F32))

        def region(k, n):
            return ps[:, k // 4, (k % 4) * P:(k % 4) * P + n]

        ps_flat = ps[:, :, :].rearrange("p a b -> p (a b)")

        def regions(bank, n):
            return ps[:, bank:bank + 2, :].rearrange("p c (k f) -> p (c k) f", f=P)[:, :, 0:n]

        def by_bank(ap):
            return ap.rearrange("p (k c) f -> p c k f", c=2)

        src_t = buf_a[:, :, :, :].rearrange("p a b c -> p (a b) c")[:, 0:TB, :].bitcast(I32)
        dst_t = buf_b[:, :, :, :].rearrange("p a b c -> p (a b) c")[:, 0:TB, :].bitcast(I32)
        src_f = buf_c[:, :, :, :].rearrange("p a b c -> p (a b) c")[:, 0:TB, :]
        dst_f = buf_d[:, :, :, :].rearrange("p a b c -> p (a b) c")[:, 0:TB, :]
        gate_t = aux[:, :, :].rearrange("p a b -> p (a b)")[:, 0:TB * P].rearrange("p (b e) -> p b e", e=P)
        t_row = aux[:, :, :].rearrange("p a b -> p (a b)")[:, TB * P:TB * P + S]
        w_row = aux[:, :, :].rearrange("p a b -> p (a b)")[:, TB * P + S:TB * P + 2 * S]
        scr_i = rows[:, :, :, :].rearrange("p a b c -> p (a b c)").bitcast(I32)
        step_i = acc_flat[:, 0:S].bitcast(I32)
        step_f = acc_flat[:, S:2 * S]
        junk = acc_flat[:, 2 * S:3 * S]
        tab_flat = tab[:, :, :].rearrange("p a b -> p (a b)")
        EB = P * K16
        sel = tab_flat[:, 0:TB * CH].rearrange("p (b s) -> p b s", s=CH)
        x_flat = tab_flat
        tab_d = tab_flat[:, 0:W * D].rearrange("p (w f) -> p w f", f=D)
        scratch = tab_flat[:, W * D:2 * W * D].rearrange("p (w f) -> p w f", f=D)
        stage = buf_a[:, :, :, :].rearrange("p a b c -> p (a b) c")

        NAMES = """consts_made iotas_made tiles_clean tiles_loaded weights_loaded bias_loaded x_clean x_loaded
            ea_loaded0 ea_loaded1 ea_clean dve key_ready keyrow_made tcol_ready trow_made trow_copied sel_made sel_used steps_made gate_lin gate_done
            wt_made wt_copied wa_made fill_ready fill0 fill1 fill2 fill3
            node_in node_xs node_xt node_xtc node_out node_evac stage_full stage_free tab_stored
            l0_src l0_srow l0_og l0_s l0_idxf l0_b l0_bc l0_out l0_outc l0_sfree l0_done l0_turn l0_dve lanes_done lane_in0 lane_in1 lane_in2 lane_in3 lane_again
            l1_idx l1_turn l1_gfree l1_o l1_t l1_tc l1_ys l1_y l1_sq l1_yv l1_s1 l1_s2 l1_yfree l1_ybank e_turn e0 e1 e2 e3 ys0 ys1 l1_got0 l1_got1
            stat_done bn_ready bn_made bn_copied
            lb_y0 lb_y1 lb_y2 lb_y3 lb_z lb_zfree lb_o lb_min bn_rows lb_exp lb_dve lb_msg lb_made lb_out lb_accfree lb_acc 
            ln_var ln_std
            l2_idx l2_turn l2_got0 l2_got1 l2_nm l2_mask l2_max l2_maskfree l2_mx l2_hst0 l2_hst1 l2_hfree 
            mx_done l2b_h0 l2b_h1 l2b_hfree l2b_o l2b_t l2b_tc l2b_s l2b_arg l2b_exp l2b_dve l2b_ow l2b_o32 l2b_out l2b_accfree l2b_acc
            elu_in elu_out gcn_in0 gcn_in1 gcn_st0 gcn_st1
            g0_idx g0_turn g0_got0 g0_got1 g0_o g0_out g0_accfree g0_gfree g0_acc
            g1_idx g1_turn g1_got0 g1_got1 g1_o g1_out g1_accfree g1_gfree g1_acc
            result_ready result_stored""".split()
        s = namedtuple("Semaphores", NAMES)(*[sem(n) for n in NAMES])
        fill = [s.fill0, s.fill1, s.fill2, s.fill3]
        y_in = [s.lb_y0, s.lb_y1, s.lb_y2, s.lb_y3]
        e_in = [s.e0, s.e1, s.e2, s.e3]
        lane_in = [s.lane_in0, s.lane_in1, s.lane_in2, s.lane_in3]

        def bc(ap, shape):
            return ap.to_broadcast(shape)

        def step_slice(t, g):
            return t[:, bass.ds(g * G, G)]

        def step_col(t, g, u):
            return t[:, bass.ds(g * G + u, 1)]

        def load8(engine, table, g, top):
            _, v = nc.values_load_multi_w_load_instructions(
                table[:, bass.ds(g * G, G)], engines=(engine,), min_val=0, max_val=top,
                skip_runtime_bounds_check_because="the table's entries are clamped to it")
            return v

        def load1(engine, table, g, top):
            _, v = nc.values_load_multi_w_load_instructions(
                table[:, bass.ds(g * G, 1)], engines=(engine,), min_val=0, max_val=top,
                skip_runtime_bounds_check_because="the table's entries are clamped to it")
            return v[0]

        def one_hot(engine, to, g):
            return engine.tensor_tensor(to, bc(iota[:, :].unsqueeze(1), [P, G, P]),
                                        bc(step_slice(dst_s, g).unsqueeze(2), [P, G, P]), ALU.is_equal)

        def window(t, w, n, start=0):
            return t[:, bass.ds(w, 1), start:start + n].rearrange("p a b -> p (a b)")

        block = ctx.enter_context(nc.Block())

        WN, WC, WF, WA = 0, D, 4 * D, 7 * D
        TN, TS, TE, TA, T1 = 0, D, 5 * D, 7 * D, 7 * D + D2
        a2 = sb("a2", [D, 2])
        w12 = sb("w12", [D, 2, D])

        @block.sync
        def _(sp):
            sp.wait_ge(s.tiles_clean, 2)
            body = (TB - 1) * P * P
            for tile, arr in ((src_t, src), (dst_t, dst)):
                sp.dma_start(tile[:, 0:TB - 1, :], arr[0:body].rearrange("(b t e) -> t b e", t=P, e=P)).then_inc(s.tiles_loaded, 16)
                sp.dma_start(tile[0:TAIL_T, TB - 1, :],
                             arr[body:FULL_T * P].rearrange("(t e) -> t e", e=P)).then_inc(s.tiles_loaded, 16)
                sp.dma_start(tile[TAIL_T:TAIL_T + 1, TB - 1, P - HALF:P],
                             arr[FULL_T * P:E].rearrange("(a e) -> a e", a=1)).then_inc(s.tiles_loaded, 16)
            sp.dma_start(we_bc[:, :], w_edge.rearrange("k a -> (a k)").partition_broadcast(P)).then_inc(s.weights_loaded, 16)
            sp.dma_start(be_c[:, :], b_edge.partition_broadcast(P)).then_inc(s.weights_loaded, 16)

            def load_ea(b, slot, done):
                view = x_flat[:, slot * EB:(slot + 1) * EB]
                if b < TB - 1:
                    sp.dma_start(view, ea16[b * P * P:(b + 1) * P * P, :].rearrange("(t e) k -> t (e k)", e=P)).then_inc(done, 16)
                else:
                    sp.dma_start(view[0:TAIL_T, :], ea16[b * P * P:FULL_T * P, :].rearrange("(t e) k -> t (e k)", e=P)).then_inc(done, 16)
                    sp.dma_start(view[TAIL_T:TAIL_T + 1, (P - HALF) * K16:EB],
                                 ea16[FULL_T * P:E, :].rearrange("(a e) k -> a (e k)", a=1)).then_inc(done, 16)

            for b in range(6):
                load_ea(b, b, s.ea_loaded0)
            sp.dma_start(wsm[0:D, WN:WN + D], w_node).then_inc(s.weights_loaded, 16)
            sp.dma_start(wsm[0:D, WC:WC + 3 * D], w_core).then_inc(s.weights_loaded, 16)
            sp.dma_start(wsm[0:D, WF:WF + 3 * D], w_filter).then_inc(s.weights_loaded, 16)
            sp.dma_start(wsm[0:D, WA:WA + D], w_att).then_inc(s.weights_loaded, 16)
            with nc.allow_non_contiguous_dma(reason="128 single elements, once"):
                sp.dma_start(a2[:, :], a_att.rearrange("(k d) -> d k", k=2)).then_inc(s.weights_loaded, 16)
            sp.dma_start(w12[:, 0, :], w1).then_inc(s.weights_loaded, 16)
            sp.dma_start(w12[:, 1, :], w2).then_inc(s.weights_loaded, 16)
            sp.dma_start(bias0[:, :], b_node.partition_broadcast(P)).then_inc(s.bias_loaded, 16)
            sp.dma_start(bias_d[:, 0:D], b_core.partition_broadcast(P)).then_inc(s.bias_loaded, 16)
            sp.dma_start(bias_d[:, D:2 * D], b_filter.partition_broadcast(P)).then_inc(s.bias_loaded, 16)
            sp.dma_start(bias3[:, 0, :], b1.partition_broadcast(P)).then_inc(s.bias_loaded, 16)
            sp.dma_start(bias3[:, 1, :], b2.partition_broadcast(P)).then_inc(s.bias_loaded, 16)
            for k, (gam, half) in enumerate(((gamma_c, 0), (gamma_f, 1), (beta_c, 0), (beta_f, 1))):
                sp.dma_start(bn_col[half * D:half * D + D, 2 + k // 2:3 + k // 2], gam.rearrange("(d a) -> d a", a=1)).then_inc(s.bias_loaded, 16)
            sp.wait_ge(s.x_clean, 1)
            sp.dma_start(x_n[:, 0:FULL_W, :], x[0:FULL_W * P, :].rearrange("(w p) f -> p w f", p=P)).then_inc(s.x_loaded, 16)
            sp.dma_start(x_n[0:TAIL_N, FULL_W, :], x[FULL_W * P:N, :]).then_inc(s.x_loaded, 16)
            for part, n in ((1, 6), (2, 1)):
                sp.wait_ge(s.ea_clean, part)
                for b in range(n):
                    load_ea(6 * part + b, b, s.ea_loaded1)

            sp.wait_ge(s.lanes_done, 1)

            def lane_rows(k):
                return lane_tab[k][0:NP, :].rearrange("(w p) f -> p w f", p=P)

            tab_l = tab_flat[:, 0:W * D1].rearrange("p (w f) -> p w f", f=D1)
            for k, to in ((0, acc[:, :, :]), (1, aux[:, :, :]), (2, tab_l)):
                sp.dma_start(to, lane_rows(k)).then_inc(lane_in[k], 16)
            sp.wait_ge(s.lane_again, 1)
            sp.dma_start(aux[:, :, :], lane_rows(3)).then_inc(lane_in[3], 16)

            with sp.Fori(0, CHUNKS) as c:
                sp.wait_ge(s.stage_full, c + 1)
                sp.dma_start(src_tab[bass.ds(c * (WPC * P), WPC * P), :].rearrange("(w p) f -> p w f", p=P),
                             stage[:, 0:WPC, :]).then_inc(s.tab_stored, 16)
                sp.wait_ge(s.tab_stored, c * 16 + 16)
                sp.sem_inc(s.stage_free, 1)

            y_out = [s.ys0, s.ys1]

            def load_edges(g, q):
                starts = load8(mybir.EngineType.SP, row_s, g, E - P)
                for u in range(G):
                    sp.dma_start(ea_s[:, q, u, :], ea64[bass.ds(starts[u], P), :]).then_inc(e_in[q], 16)

            def l1_pair(i, half, first):
                for b in range(2):
                    g = i * 2 + b
                    sp.wait_ge(s.l1_t, g + 1)
                    sp.sem_inc(s.e_turn, 1)
                    load_edges(g + 4, 2 * half + b)
                if not first:
                    for b in range(2):
                        sp.wait_ge(y_out[b], i * 16)
                        sp.sem_inc(s.l1_yfree, 1)
                for b in range(2):
                    g = i * 2 + b
                    sp.wait_ge(s.l1_y, g + 1)
                    sp.dma_start(y_stash[bass.ds(g, 1), :, :].rearrange("a p f -> (a p) f"),
                                 buf_c[:, b, :, :].rearrange("p u f -> p (u f)")).then_inc(y_out[b], 16)

            for q in range(4):
                load_edges(q, q)
            l1_pair(0, 0, True)
            l1_pair(1, 1, False)
            with sp.Fori(1, ITER // 2) as i:
                for half in range(2):
                    l1_pair(i * 2 + half, half, False)
            for b in range(2):
                sp.wait_ge(y_out[b], ITER * 16)
            sp.sem_inc(s.l1_yfree, 2)
            for q in range(4):
                sp.wait_ge(e_in[q], (ITER // 2 + 1) * G * 16)

            with sp.Fori(0, ITER // 2) as i:
                for q in range(4):
                    g = i * 4 + q
                    sp.wait_ge(s.lb_zfree, g + 1)
                    sp.dma_start(y_buf[:, q, :, :].rearrange("p u f -> p (u f)"),
                                 y_stash[bass.ds(g, 1), :, :].rearrange("a p f -> (a p) f")).then_inc(y_in[q], 16)

            with sp.Fori(0, CHUNKS) as c:
                sp.wait_ge(s.stage_full, c + CHUNKS + 1)
                sp.dma_start(att_tab[bass.ds(c * (WPC * P), WPC * P), :].rearrange("(w p) f -> p w f", p=P),
                             stage[:, 0:WPC, 0:D2]).then_inc(s.tab_stored, 16)
                sp.wait_ge(s.tab_stored, c * 16 + (CHUNKS + 1) * 16)
                sp.sem_inc(s.stage_free, 1)
            got, h_out = [s.l2_got0, s.l2_got1], [s.l2_hst0, s.l2_hst1]
            with sp.Fori(0, ITER) as i:
                for b in range(2):
                    sp.wait_ge(got[b], i * (G * 16) + G * 16)
                    sp.dma_start(h_stash[bass.ds(i * 2 + b, 1), :, :].rearrange("a p f -> (a p) f"),
                                 rows[:, b, :, :].rearrange("p u f -> p (u f)")).then_inc(h_out[b], 16)
                    sp.wait_ge(h_out[b], i * 16 + 16)
                    sp.sem_inc(s.e_turn, 1)
                    sp.wait_ge(s.l2_mask, i * 2 + b + 1)
                    sp.sem_inc(s.l2_hfree, 1)
            h_in = [s.l2b_h0, s.l2b_h1]
            with sp.Fori(0, ITER) as i:
                for b in range(2):
                    sp.wait_ge(s.l2b_hfree, i * 2 + b + 1)
                    sp.dma_start(rows[:, b, :, :].rearrange("p u f -> p (u f)"),
                                 h_stash[bass.ds(i * 2 + b, 1), :, :].rearrange("a p f -> (a p) f")).then_inc(h_in[b], 16)

            for k, (ready, stored) in enumerate(((s.gcn_in0, s.gcn_st0), (s.gcn_in1, s.gcn_st1))):
                sp.wait_ge(ready, 1)
                sp.dma_start(gcn_tab[k].rearrange("(w p) f -> p w f", p=P), tab_d).then_inc(stored, 16)

            sp.wait_ge(s.result_ready, 1)
            sp.dma_start(out[0:FULL_W * P, :].rearrange("(w p) f -> p w f", p=P), x_n[:, 0:FULL_W, :]).then_inc(s.result_stored, 16)
            sp.dma_start(out[FULL_W * P:N, :], x_n[0:TAIL_N, FULL_W, :]).then_inc(s.result_stored, 16)
            sp.wait_ge(s.result_stored, 32)

        @block.gpsimd
        def _(pool):
            pool.memset(src_t, 0).then_inc(s.tiles_clean, 1)
            pool.memset(dst_t, NOWHERE).then_inc(s.tiles_clean, 1)
            pool.iota(step_i, [[1, S]], base=0, channel_multiplier=0).then_inc(s.iotas_made, 1)
            pool.iota(scr_i[:, 0:TB], [[P, TB]], base=0, channel_multiplier=1).then_inc(s.iotas_made, 1)
            pool.memset(x_n[:, FULL_W, :], 0.0).then_inc(s.x_clean, 1)

            pool.wait_ge(s.fill_ready, 1)
            per = SROWS * D1 // P
            for k in range(LANES):
                pool.dma_start(lane_tab[k].rearrange("(p r) f -> p (r f)", p=P), tab_flat[:, 0:per]).then_inc(fill[k], 16)
            for k in range(LANES):
                pool.wait_ge(fill[k], 16)
            pool.sem_inc(s.fill_ready, 1)
            with pool.Fori(0, ITER) as i:
                for b in range(2):
                    g = i * 2 + b
                    pool.wait_ge(s.l0_outc, g + 3)
                    pool.sem_inc(s.l0_turn, 1)
                    for u in range(G):
                        k = u % LANES
                        pool.wait_ge(fill[k], i * 64 + (16 + 32 * b + 16 * (u // LANES)))
                        pool.sem_inc(s.l0_done if u == LANES - 1 else s.l0_turn, 1)
                        pool.indirect_dma_start(lane_tab[k][:, :], bass.IndirectOffsetOnAxis(ap=idx[:, b, u:u + 1], axis=0),
                                                rows[:, b, u, 0:D1], None, compute_op=ALU.add).then_inc(fill[k], 16)
            for k in range(LANES):
                pool.wait_ge(fill[k], 16 + 64 * ITER)
            pool.sem_inc(s.lanes_done, 1)

            def gathers(table, n, to, idx_ready, turn, free, got):
                with pool.Fori(0, ITER) as i:
                    for b in range(2):
                        pool.wait_ge(idx_ready, i * 2 + b + 1)
                        pool.sem_inc(turn, 1)
                        pool.wait_ge(free, i * 2 + b + 1)
                        pool.sem_inc(turn, 1)
                        for u in range(G):
                            pool.indirect_dma_start(to[:, b, u, 0:n], None, table[:, :],
                                                    bass.IndirectOffsetOnAxis(ap=idx[:, b, u:u + 1], axis=0)).then_inc(got[b], 16)

            pool.wait_ge(s.tab_stored, CHUNKS * 16)
            gathers(src_tab, 2 * D, buf_b, s.l1_idx, s.l1_turn, s.l1_gfree, [s.l1_got0, s.l1_got1])
            pool.wait_ge(s.bn_rows, 1)
            pool.sem_inc(s.lb_zfree, 4)
            with pool.Fori(0, ITER // 2) as i:
                for q in range(4):
                    g = i * 4 + q
                    z = z_buf[:, q, :, :]
                    pool.wait_ge(y_in[q], i * 16 + 16)
                    pool.sem_inc(s.l1_turn, 1)
                    pool.wait_ge(s.lb_made, g + 1)
                    pool.tensor_tensor(z, y_buf[:, q, :, :], bc(bn[:, 0:1, :], [P, G, 2 * D]), ALU.mult).then_inc(s.lb_z, 1)
                    pool.wait_ge(s.lb_z, g * 2 + 1)
                    pool.sem_inc(s.lb_zfree, 1)
                    pool.tensor_tensor(z, z, bc(bn[:, 1:2, :], [P, G, 2 * D]), ALU.add).then_inc(s.lb_z, 1)
            pool.wait_ge(s.tab_stored, 2 * CHUNKS * 16)
            gathers(att_tab, D2, rows, s.l2_idx, s.l2_turn, s.l2_hfree, [s.l2_got0, s.l2_got1])
            pool.wait_ge(s.gcn_st0, 16)
            gathers(gcn_tab[0], D, rows, s.g0_idx, s.g0_turn, s.g0_gfree, [s.g0_got0, s.g0_got1])
            pool.wait_ge(s.gcn_st1, 16)
            gathers(gcn_tab[1], D, rows, s.g1_idx, s.g1_turn, s.g1_gfree, [s.g1_got0, s.g1_got1])

        @block.scalar
        def _(act):
            act.wait_ge(s.weights_loaded, 16 * 9)
            act.wait_ge(s.gate_lin, 1)
            act.activation(gate_t, gate_t, ACT.Sigmoid, bias=be_c[:, 0:1]).then_inc(s.gate_done, 1)
            act.wait_ge(s.wt_made, 1)
            act.activation(wt[:, 0:7 * D], ps[:, 6, 0:7 * D], ACT.Copy).then_inc(s.wt_copied, 1)
            act.activation(wt[0:D, TA:TA + D], wsm[0:D, WA:WA + D], ACT.Copy).then_inc(s.wt_copied, 1)
            act.activation(xt[0:D, 0:D], ps[0:D, 7, 0:D], ACT.Copy).then_inc(s.wt_copied, 1)
            act.wait_ge(s.wa_made, 1)
            act.activation(wt[0:D, TA + D:TA + D2], ps[0:D, 7, D:D2], ACT.Copy).then_inc(s.wt_copied, 1)

            def node_copies(base, view):
                with act.Fori(0, CHUNKS) as c:
                    act.activation(xs, view[:, bass.ds(c * WPC, WPC), :], ACT.Copy).then_inc(s.node_xs, 1)
                    act.wait_ge(s.node_xt, c + (base + 1))
                    act.activation(xt[:, :], ps[0:D, 0:2, :].rearrange("p a b -> p (a b)")[:, 0:WPC * P], ACT.Copy).then_inc(s.node_xtc, 1)

            act.wait_ge(s.node_in, 1)
            node_copies(0, x_n)

            def l0_gates_copy(g, b):
                act.wait_ge(s.l0_b, g + 1)
                act.activation(buf_d[:, b, :, :], regions(2 * b, P), ACT.Copy).then_inc(s.l0_bc, 1)

            def l0_rows_copy(g, b):
                act.wait_ge(s.l0_out, g + 1)
                act.wait_ge(s.l0_idxf, g + 1)
                act.wait_ge(s.l0_done, g + 1)
                act.activation(idx[:, b, :], idxf[:, b, :], ACT.Copy)
                act.activation(rows[:, b, :, 0:D1], regions(4 + 2 * b, D1), ACT.Copy).then_inc(s.l0_outc, 1)

            l0_gates_copy(0, 0)
            with act.Fori(0, ITER - 1) as i:
                for b in range(2):
                    g = i * 2 + (b + 1)
                    l0_gates_copy(g, 1 - b)
                    l0_rows_copy(g - 1, b)
            l0_gates_copy(2 * ITER - 1, 1)
            l0_rows_copy(2 * ITER - 2, 0)
            l0_rows_copy(2 * ITER - 1, 1)

            def std(n):
                act.wait_ge(s.ln_var, n)
                act.activation(col_b[:, :], col_a[:, :], ACT.Sqrt).then_inc(s.ln_std, 1)

            def indices(ready, got):
                for b in range(2):
                    act.activation(idx[:, b, :], src_s[:, b * G:b * G + G], ACT.Copy).then_inc(ready, 1)

            def next_indices(i, b, ready, got):
                act.wait_ge(got[b], i * (G * 16) + G * 16)
                act.activation(idx[:, b, :], src_s[:, bass.ds(i * PAIR + (PAIR + b * G), G)], ACT.Copy).then_inc(ready, 1)

            std(1)
            act.wait_ge(s.node_in, 3)
            node_copies(CHUNKS, x_n)
            got = [s.l1_got0, s.l1_got1]
            indices(s.l1_idx, got)
            def l1_copies(g, b):
                act.wait_ge(s.l1_t, g + 1)
                act.activation(buf_d[:, b, :, :].rearrange("p u f -> p (u f)"), ps[:, b, :].bitcast(BF16), ACT.Copy)
                act.activation(buf_a[:, b, 0:4, :].rearrange("p u f -> p (u f)"), ps[:, 2 + b, :], ACT.Copy).then_inc(s.l1_tc, 1)

            for b in range(2):
                l1_copies(b, b)
            with act.Fori(0, ITER) as i:
                for b in range(2):
                    l1_copies(i * 2 + (b + 2), b)
                for b in range(2):
                    next_indices(i, b, s.l1_idx, got)
                    act.wait_ge(s.l1_yv, i * 2 + b + 1)
                    act.wait_ge(s.l1_s2, i * 2 + b + 1)
                    act.activation(sq[:, b, :, :], yv[:, b, :, :], ACT.Square).then_inc(s.l1_sq, 1)
            act.wait_ge(s.bn_ready, 1)
            act.activation(bn_col[:, 7:8], bn_col[:, 6:7], ACT.Sqrt).then_inc(s.bn_made, 1)
            act.preload_act_table_set("natural_log_exp_and_others")
            with act.Fori(0, ITER) as i:
                for b in range(2):
                    m = buf_b[:, b, :, :]
                    act.wait_ge(s.lb_min, i * 2 + b + 1)
                    act.activation(m, m, ACT.Exp).then_inc(s.lb_exp, 1)
                    act.wait_ge(s.lb_exp, i * 6 + (3 * b + 1))
                    act.activation(m, m, ACT.Ln, bias=1.0).then_inc(s.lb_exp, 1)
                    act.wait_ge(s.lb_exp, i * 6 + (3 * b + 2))
                    act.activation(m[:, :, D:2 * D], m[:, :, D:2 * D], ACT.Exp, scale=-1.0).then_inc(s.lb_exp, 1)
            std(2)
            act.wait_ge(s.node_in, 5)
            node_copies(2 * CHUNKS, x_n)
            act.wait_ge(s.l1_idx, 2 * ITER + 2)
            got = [s.l2_got0, s.l2_got1]
            indices(s.l2_idx, got)
            with act.Fori(0, ITER) as i:
                for b in range(2):
                    next_indices(i, b, s.l2_idx, got)

            def l2b_copy(g, b):
                act.wait_ge(s.l2b_t, g + 1)
                act.activation(ot_b[:, b, :, :].rearrange("p u f -> p (u f)"), ps[:, b, :].bitcast(BF16), ACT.Copy).then_inc(s.l2b_tc, 1)

            def l2b_exps(i):
                for b in range(2):
                    act.wait_ge(s.l2b_arg, i * 2 + (b + 1))
                    act.activation(ex[:, b, :], tmp_c[:, 2 + b, :], ACT.Exp).then_inc(s.l2b_exp, 1)

            for b in range(2):
                l2b_copy(b, b)
            with act.Fori(0, ITER - 1) as i:
                l2b_exps(i)
                for b in range(2):
                    l2b_copy(i * 2 + (b + 2), b)
            l2b_exps(ITER - 1)
            act.wait_ge(s.elu_in, 1)
            act.activation(scratch, scratch, ACT.Exp).then_inc(s.elu_out, 1)
            std(3)
            std(4)
            act.wait_ge(s.l2_idx, 2 * ITER + 2)
            got = [s.g0_got0, s.g0_got1]
            indices(s.g0_idx, got)
            with act.Fori(0, ITER) as i:
                for b in range(2):
                    next_indices(i, b, s.g0_idx, got)
            act.wait_ge(s.node_in, 6)
            node_copies(3 * CHUNKS, tab_d)
            act.wait_ge(s.g0_idx, 2 * ITER + 2)
            got = [s.g1_got0, s.g1_got1]
            indices(s.g1_idx, got)
            with act.Fori(0, ITER) as i:
                for b in range(2):
                    next_indices(i, b, s.g1_idx, got)
            act.wait_ge(s.node_in, 7)
            node_copies(4 * CHUNKS, tab_d)
            std(5)

        @block.tensor
        def _(pe):
            pe.wait_ge(s.consts_made, 1)
            pe.wait_ge(s.key_ready, 1)
            for b in range(TB):
                last = pe.matmul(region(b, P), bc(key[:, b:b + 1], [P, P]), ident[:, :], start=True, stop=True)
            last.then_inc(s.keyrow_made, 1)
            pe.wait_ge(s.weights_loaded, 16 * 9)
            i64 = ident[0:D, 0:D]
            wps = ps[:, 6, :]
            for at, frm in ((TN, WN), (TS, WC + D), (TS + D, WF + D), (TS + 2 * D, WC), (TS + 3 * D, WF),
                            (TE, WC + 2 * D), (TE + D, WF + 2 * D)):
                pe.matmul(wps[0:D, at:at + D], wsm[0:D, frm:frm + D], i64, start=True, stop=True)
            for at, frm in ((TN, WN), (TS, WC + D), (TS + D, WF + D), (TS + 2 * D, WC), (TS + 3 * D, WF),
                            (TE, WC + 2 * D), (TE + D, WF + 2 * D)):
                pe.matmul(wps[D:P, at:at + D], wsm[0:D, frm:frm + D], i64, start=True, stop=True)
            pe.matmul(ps[0:D, 7, 0:D], wsm[0:D, WA:WA + D], i64, start=True, stop=True).then_inc(s.wt_made, 1)
            pe.wait_ge(s.wt_copied, 3)
            pe.matmul(ps[0:D, 7, D:D2], xt[0:D, 0:D], a2[:, :], start=True, stop=True).then_inc(s.wa_made, 1)
            pe.wait_ge(s.wt_copied, 4)
            pe.wait_ge(s.tcol_ready, 1)
            for b in range(SB):
                last = pe.matmul(region(16 + b, P), bc(t_col[:, b:b + 1], [P, P]), ident[:, :], start=True, stop=True)
            last.then_inc(s.trow_made, 1)
            pe.wait_ge(s.trow_copied, 1)
            pe.wait_ge(s.gate_done, 1)
            with pe.Fori(0, 4) as c:
                pe.wait_ge(s.sel_made, c + 1)
                for k, t in enumerate((src_f, dst_f, gate_t)):
                    for b in range(TB):
                        last = pe.matmul(ps[:, k, 0:CH], t[:, b, :], sel[:, b, :], start=(b == 0), stop=(b == TB - 1))
                last.then_inc(s.sel_used, 1)

            def node_product(base, rhs, n, per_bank):
                with pe.Fori(0, CHUNKS) as c:
                    pe.wait_ge(s.node_xs, c + (base + 1))
                    for k in range(WPC):
                        last = pe.matmul(region(k, P)[0:D, :], xs[:, k, :], ident[:, :], start=True, stop=True)
                    last.then_inc(s.node_xt, 1)
                    pe.wait_ge(s.node_xtc, c + (base + 1))
                    pe.wait_ge(s.node_evac, c + (base + 1))
                    for k in range(WPC):
                        o = ps[:, 2 + k // per_bank, (k % per_bank) * (512 // per_bank):(k % per_bank) * (512 // per_bank) + n]
                        last = pe.matmul(o, xt[:, k * P:k * P + P], rhs, start=True, stop=True)
                    last.then_inc(s.node_out, 1)

            pe.wait_ge(s.node_in, 1)
            pe.sem_inc(s.l0_sfree, 2)
            node_product(0, wt[0:D, TN:TN + D], D, 4)

            pe.wait_ge(s.node_in, 2)
            pe.sem_inc(s.l0_bc, 2)

            def l0_rows(g, b):
                pe.wait_ge(s.l0_src, g + 1)
                pe.wait_ge(s.l0_bc, g + 1)
                for u in range(G):
                    last = pe.matmul(region(8 * b + u, P), bc(srcg[:, b, u:u + 1], [P, P]), ident[:, :], start=True, stop=True)
                last.then_inc(s.l0_srow, 1)

            def l0_gates(g, b):
                pe.wait_ge(s.l0_og, g + 1)
                pe.wait_ge(s.l0_s, g + 1)
                for u in range(G):
                    last = pe.matmul(region(8 * b + u, P), buf_a[:, b, u, :], buf_b[:, b, u, :], start=True, stop=True)
                last.then_inc(s.l0_b, 1)

            def l0_sums(g, b):
                ws = load8(mybir.EngineType.PE, win_s, g, W - 1)
                pe.wait_ge(s.l0_bc, g + 3)
                pe.wait_ge(s.l0_outc, g + 1)
                for u in range(G):
                    o = 16 + 8 * b + u
                    pe.matmul(region(o, D1)[:, D:D1], buf_b[:, b, u, :], step_col(valid_s, g, u), start=True, stop=True)
                    last = pe.matmul(region(o, D), buf_d[:, b, u, :], window(tab, ws[u], D), start=True, stop=True)
                last.then_inc(s.l0_out, 1)
                pe.sem_inc(s.l0_sfree, 1)

            def l0_next(g, b):
                l0_rows(g, b)
                l0_sums(g - 1, 1 - b)
                l0_gates(g, b)

            l0_rows(0, 0)
            l0_gates(0, 0)
            with pe.Fori(0, ITER - 1) as i:
                for b in range(2):
                    l0_next(i * 2 + (b + 1), 1 - b)
            l0_next(2 * ITER - 1, 1)
            l0_sums(2 * ITER - 1, 1)

            pe.wait_ge(s.node_in, 3)
            node_product(CHUNKS, wt[0:D, TS:TS + 4 * D], 4 * D, 2)

            pe.wait_ge(s.node_in, 4)

            def l1_transposes(turn, q, g):
                b = q % 2
                pe.wait_ge(e_in[q], turn * (G * 16) + G * 16)
                pe.wait_ge(s.l1_o, g + 1)
                ob_ps = ps[:, b, :].bitcast(BF16)
                for u in range(G):
                    pe.transpose(ob_ps[:, u * P:u * P + P], ob[:, b, u, :], ident_b[:, :])
                for u in range(G // 2):
                    last = pe.transpose(ps[:, 2 + b, u * P:u * P + P],
                                        ea_s[:, q, 2 * u:2 * u + 2, :].rearrange("p a f -> p (a f)"), ident[:, :])
                last.then_inc(s.l1_t, 1)

            for b in range(2):
                l1_transposes(0, b, b)
            with pe.Fori(0, ITER // 2) as i:
                for half in range(2):
                    for b in range(2):
                        g = i * 4 + (2 * half + b)
                        ws = load8(mybir.EngineType.PE, win_s, g, W - 1)
                        pe.wait_ge(s.l1_tc, g + 1)
                        pe.wait_ge(s.l1_ybank, g + 1)
                        for u in range(G):
                            h = D * (u % 2)
                            o = region(16 + 8 * b + 4 * (u % 2) + u // 2, P)
                            pe.matmul(o, buf_d[:, b, u, :], window(tab, ws[u], P), start=True, stop=False)
                            last = pe.matmul(o, buf_a[h:h + D, b, u // 2, :], wt[h:h + D, TE:TE + 2 * D], start=False, stop=True)
                        last.then_inc(s.l1_ys, 1)
                    for b in range(2):
                        l1_transposes(i + half, 2 * (1 - half) + b, i * 4 + (2 * half + b + 2))
            pe.wait_ge(s.l1_s2, 2 * ITER + 2)
            for k in range(2):
                for u in range(G):
                    last = pe.matmul(ps[:, 4 + k, 0:1], stat[:, k, u, :], ones[:, 0:1], start=(u == 0), stop=(u == G - 1))
            last.then_inc(s.stat_done, 1)
            pe.wait_ge(s.bn_made, 2)
            for k in range(2):
                last = pe.matmul(ps[:, 6, 2 * D * k:2 * D * k + 2 * D], bc(bn_col[:, k:k + 1], [P, P]), ident[:, :], start=True, stop=True)
            last.then_inc(s.bn_copied, 1)

            def add_group(left, right, g, b, bank, n):
                for c in range(2):
                    pe.matmul(ps[:, bank + c, :].rearrange("p (k f) -> p k f", f=P)[:, :, 0:n], zero_b[:, :],
                              bc(ident_b[:, 0:n].unsqueeze(1), [P, 4, n]), start=True, stop=False, skip_group_check=True)
                rel = load8(mybir.EngineType.PE, rel_s, g, (G - 1) * P)
                for u in range(G):
                    last = pe.matmul(ps_flat[:, bass.ds(rel[u] + bank * 512, n)], left[:, b, u, :], right[:, b, u, 0:n],
                                     start=False, stop=True, skip_group_check=True)
                return last

            def aggregate(left, right, n, left_ready, right_ready, free, done):
                with pe.Fori(0, ITER) as i:
                    for b in range(2):
                        g = i * 2 + b
                        pe.wait_ge(left_ready, g + 1)
                        pe.wait_ge(right_ready[b], i * (G * 16) + G * 16)
                        pe.wait_ge(free, g + 1)
                        add_group(left, right, g, b, 2 * b, n).then_inc(done, 1)

            with pe.Fori(0, ITER // 2) as i:
                for q in range(4):
                    g = i * 4 + q
                    pe.wait_ge(s.lb_o, g + 1)
                    pe.wait_ge(s.lb_msg, g + 1)
                    pe.wait_ge(s.lb_accfree, g + 1)
                    add_group(lb_hot[q // 2], lb_rows[q // 2], g, q % 2, 2 * q, D1).then_inc(s.lb_out, 1)

            pe.wait_ge(s.node_in, 5)
            node_product(2 * CHUNKS, wt[0:D, TA:TA + D2], D2, 4)
            got = [s.l2_got0, s.l2_got1]
            with pe.Fori(0, ITER) as i:
                for b in range(2):
                    g = i * 2 + b
                    pe.wait_ge(got[b], i * (G * 16) + G * 16)
                    pe.wait_ge(s.l2_nm, g + 1)
                    pe.wait_ge(s.l2_maskfree, g + 1)
                    for u in range(G):
                        pe.matmul(region(8 * b + u, P), buf_a[:, b, u, :], ident[:, :], start=True, stop=False)
                        last = pe.matmul(region(8 * b + u, P), bc(rows[:, b, u, D1:D2], [P, P]), ident[:, :], start=False, stop=True)
                    last.then_inc(s.l2_mask, 1)
            pe.wait_ge(s.mx_done, 1)

            def l2b_transposes(g, b):
                pe.wait_ge(s.l2b_o, g + 1)
                for u in range(G):
                    last = pe.transpose(ps[:, b, :].bitcast(BF16)[:, u * P:u * P + P], ob[:, b, u, :], ident_b[:, :])
                last.then_inc(s.l2b_t, 1)

            def l2b_targets(g, b):
                ws = load8(mybir.EngineType.PE, win_s, g, W - 1)
                pe.wait_ge(s.l2b_tc, g + 1)
                for u in range(G):
                    last = pe.matmul(ps[:, 2 + b, 6 * u:6 * u + 6], ot_b[:, b, u, :], window(sums_b, ws[u], 6), start=True, stop=True)
                last.then_inc(s.l2b_s, 1)

            def l2b_sums(g, half, b):
                pe.wait_ge(s.l2b_o32, g + 1)
                pe.wait_ge(s.l2b_ow, g + 1)
                pe.wait_ge(s.l2b_accfree, g + 1)
                add_group(l2b_hot[half], l2b_rows[half], g, b, 4 + 2 * b, D1).then_inc(s.l2b_out, 1)

            def l2b_turn(i, half):
                for b in range(2):
                    l2b_transposes(i * 2 + (b + 2), b)
                for b in range(2):
                    l2b_targets(i * 2 + (b + 2), b)
                for b in range(2):
                    l2b_sums(i * 2 + b, half, b)

            for b in range(2):
                l2b_transposes(b, b)
            for b in range(2):
                l2b_targets(b, b)
            with pe.Fori(0, ITER // 2 - 1) as i:
                for half in range(2):
                    l2b_turn(i * 2 + half, half)
            l2b_turn(ITER - 2, 0)
            for b in range(2):
                l2b_sums(2 * ITER - 2 + b, 1, b)
            aggregate(buf_a, rows, D, s.g0_o, [s.g0_got0, s.g0_got1], s.g0_accfree, s.g0_out)
            pe.wait_ge(s.node_in, 6)
            node_product(3 * CHUNKS, w12[:, 0, :], D, 4)
            aggregate(buf_a, rows, D, s.g1_o, [s.g1_got0, s.g1_got1], s.g1_accfree, s.g1_out)
            pe.wait_ge(s.node_in, 7)
            node_product(4 * CHUNKS, w12[:, 1, :], D, 4)

        @block.vector
        def _(dve):
            count = [0]

            def link(ins):
                count[0] += 1
                ins.then_inc(s.dve, 1)
                dve.wait_ge(s.dve, count[0])

            dve.wait_ge(s.iotas_made, 2)
            link(dve.tensor_copy(step_f, step_i))
            link(dve.tensor_copy(ids[:, :], scr_i[:, 0:TB]))
            link(dve.tensor_copy(iota[:, :], step_f[:, 0:P]))
            link(dve.tensor_scalar(ident[:, :], iota[:, :], ids[:, 0:1], None, ALU.is_equal))
            link(dve.tensor_copy(ident_b[:, :], ident[:, :]))
            link(dve.tensor_scalar(below[:, :], iota[:, :], ids[:, 0:1], None, ALU.is_lt))
            link(dve.tensor_scalar(trash[:, :], ids[:, 0:1], float(TRASH), None, ALU.add))
            link(dve.memset(ones[:, :], 1.0))
            link(dve.memset(zero_b[:, :], 0.0))
            for t, v in ((src_s, 0.0), (dst_s, -1.0), (gate_s, 0.0), (valid_s, 0.0)):
                link(dve.memset(t[:, S:SPAD], v))
            link(dve.memset(win_s[:, S:SPAD], 0))
            link(dve.memset(row_s[:, S:SPAD], 0))
            link(dve.memset(rel_s[:, S:SPAD], 0))
            dve.sem_inc(s.consts_made, 1)
            dve.wait_ge(s.tiles_loaded, 96)
            link(dve.tensor_copy(src_f, src_t))
            link(dve.tensor_copy(dst_f, dst_t))
            link(dve.tensor_reduce(last_i[:, :], dst_t, AX.X, ALU.max))
            link(dve.tensor_scalar(last_i[:, :], last_i[:, :], 7, None, ALU.arith_shift_right))
            link(dve.tensor_copy(key[:, :], last_i[:, :]))
            dve.tensor_tensor(key[:, :], key[:, :], ids[:, :], ALU.add).then_inc(s.key_ready, 1)
            dve.wait_ge(s.keyrow_made, 1)
            key_row = ps[:, 0:4, :].rearrange("p a b -> p (a b)")[:, 0:TB * P]
            for c in range(SB):
                link(dve.tensor_scalar(junk, key_row, ids[:, c:c + 1], None, ALU.is_lt, ALU.add, accum_out=t_col[:, c:c + 1]))
            dve.sem_inc(s.tcol_ready, 1)
            dve.wait_ge(s.weights_loaded, 16 * 9)

            def gate_block(b, slot):
                v = x_flat[:, slot * EB:(slot + 1) * EB].rearrange("p (e k) -> p e k", k=K16)
                link(dve.tensor_tensor(v, v, bc(we_bc[:, :].unsqueeze(1), [P, P, K16]), ALU.mult))
                link(dve.tensor_reduce(gate_t[:, b, :], v, AX.X, ALU.add))

            dve.wait_ge(s.ea_loaded0, 16 * 6)
            for b in range(6):
                gate_block(b, b)
            dve.sem_inc(s.ea_clean, 1)
            dve.wait_ge(s.ea_loaded1, 16 * 6)
            for b in range(6):
                gate_block(6 + b, b)
            link(dve.memset(x_flat[:, 0:EB], 0.0))
            dve.sem_inc(s.ea_clean, 1)
            dve.wait_ge(s.ea_loaded1, 16 * 8)
            gate_block(12, 0)
            dve.sem_inc(s.gate_lin, 1)
            dve.wait_ge(s.trow_made, 1)
            trow_ps = ps[:, 4:8, :].rearrange("p a b -> p (a b)")[:, 0:S]
            link(dve.tensor_copy(t_row, trow_ps))
            link(dve.tensor_tensor(w_row, step_f, t_row, ALU.subtract))
            link(dve.tensor_scalar(win_s[:, 0:S], w_row[0:1, :], float(W - 1), None, ALU.min))
            link(dve.tensor_scalar(row_s[:, 0:S], t_row[32:33, :], float(P), float(E - P), ALU.mult, ALU.min))
            link(dve.tensor_scalar(junk, w_row, float(W - 1), float(P), ALU.min, ALU.mult))
            w_grp = junk.rearrange("p (a u) -> p a u", u=G)
            link(dve.tensor_tensor(rel_s[:, 0:S].rearrange("p (a u) -> p a u", u=G), w_grp[64:65],
                                   bc(w_grp[64:65, :, 0:1], [1, S // G, G]), ALU.subtract))
            dve.sem_inc(s.trow_copied, 1)
            dve.sem_inc(s.sel_used, 1)
            with dve.Fori(0, 4) as c:
                at = bass.ds(c * CH, CH)
                for b in range(TB):
                    last = dve.tensor_scalar(sel[:, b, :], t_row[:, at], ids[:, b:b + 1], None, ALU.is_equal)
                last.then_inc(s.sel_made, 1)
                dve.wait_ge(s.sel_used, c + 2)
                dve.tensor_copy(src_s[:, at], ps[:, 0, 0:CH])
                dve.scalar_tensor_tensor(dst_s[:, at], w_row[:, at], -float(P), ps[:, 1, 0:CH], ALU.mult, ALU.add)
                dve.tensor_copy(gate_s[:, at], ps[:, 2, 0:CH]).then_inc(s.steps_made, 1)
                dve.wait_ge(s.steps_made, c + 1)
            link(dve.tensor_scalar(valid_s[:, 0:S], dst_s[:, 0:S], 0.0, None, ALU.is_ge))
            link(dve.scalar_tensor_tensor(valid_s[:, 0:S], dst_s[:, 0:S], float(P), valid_s[:, 0:S], ALU.is_lt, ALU.mult))
            link(dve.memset(tab_flat, 0.0))
            dve.sem_inc(s.fill_ready, 1)
            dve.wait_ge(s.bias_loaded, 16 * 9)
            dve.wait_ge(s.x_loaded, 32)
            dve.wait_ge(s.wt_copied, 4)
            dve.wait_ge(s.fill_ready, 2)
            dve.sem_inc(s.node_in, 1)

            def products(per_bank, k0, k1):
                n = 512 // per_bank
                b0 = 2 + k0 // per_bank
                return ps[:, b0:b0 + 1, 0:(k1 - k0) * n].rearrange("p a (k f) -> p (a k) f", f=n)

            def to_tab0(c):
                for k0, k1 in ((0, 4), (4, 7)):
                    last = dve.tensor_tensor(tab[:, bass.ds(c * WPC + k0, k1 - k0), 0:D], products(4, k0, k1)[:, :, 0:D],
                                             bc(bias0[:, :].unsqueeze(1), [P, k1 - k0, D]), ALU.add)
                last.then_inc(s.node_evac, 1)

            dve.sem_inc(s.node_evac, 1)
            with dve.Fori(0, CHUNKS) as c:
                dve.wait_ge(s.node_out, c + 1)
                to_tab0(c)
            dve.wait_ge(s.node_evac, CHUNKS + 1)
            dve.sem_inc(s.node_in, 1)

            dve.sem_inc(s.l0_outc, 2)
            dve.sem_inc(s.l0_done, 1)
            KL0 = 4
            with dve.Fori(0, ITER) as i:
                for b in range(2):
                    g = i * 2 + b
                    dve.wait_ge(s.l0_sfree, g + 1)
                    dve.tensor_copy(srcg[:, b, :], step_slice(src_s, g)).then_inc(s.l0_src, 1)
                    for u in range(G):
                        last = dve.tensor_scalar(buf_a[:, b, u, :], iota[:, :], step_col(dst_s, g, u), step_col(gate_s, g, u),
                                                 ALU.is_equal, ALU.mult)
                    last.then_inc(s.l0_og, 1)
                    dve.wait_ge(s.l0_srow, g + 1)
                    dve.tensor_tensor(buf_b[:, b, :, :], regions(2 * b, P), bc(srcg[:, b, :].unsqueeze(2), [P, G, P]),
                                      ALU.is_equal).then_inc(s.l0_s, 1)
                    dve.wait_ge(s.l0_s, g + 1)
                    k = 0

                    def chain(ins):
                        nonlocal k
                        k += 1
                        ins.then_inc(s.l0_dve, 1)
                        dve.wait_ge(s.l0_dve, i * (2 * KL0) + (b * KL0 + k))
                    chain(dve.tensor_tensor(buf_c[:, b, :, :], buf_b[:, b, :, :], bc(below[:, :].unsqueeze(1), [P, G, P]), ALU.mult))
                    chain(dve.tensor_reduce(dup[:, b, :], buf_c[:, b, :, :], AX.X, ALU.max))
                    chain(dve.tensor_scalar(tmp_c[:, b, :], srcg[:, b, :], -1.0, trash[:, 0:1], ALU.mult, ALU.add))
                    chain(dve.tensor_tensor(tmp_c[:, b, :], tmp_c[:, b, :], dup[:, b, :], ALU.mult))
                    dve.wait_ge(s.l0_outc, g + 1)
                    dve.tensor_tensor(idxf[:, b, :], tmp_c[:, b, :], srcg[:, b, :], ALU.add).then_inc(s.l0_idxf, 1)
                    dve.wait_ge(s.l0_idxf, g + 1)
                    assert k == KL0

            def norm(t, n):
                link(dve.tensor_reduce(col_a[:, :], t, AX.X, ALU.add))
                link(dve.tensor_scalar(col_a[:, :], col_a[:, :], 1.0 / D, None, ALU.mult))
                link(dve.tensor_tensor(t, t, bc(col_a[:, :].unsqueeze(2), [P, W, D]), ALU.subtract))
                link(dve.tensor_tensor(scratch, t, t, ALU.mult))
                link(dve.tensor_reduce(col_a[:, :], scratch, AX.X, ALU.add))
                dve.tensor_scalar(col_a[:, :], col_a[:, :], 1.0 / D, EPS, ALU.mult, ALU.add).then_inc(s.ln_var, 1)
                dve.wait_ge(s.ln_std, n)
                link(dve.reciprocal(col_b[:, :], col_b[:, :]))
                link(dve.tensor_tensor(x_n[:, :, :], t, bc(col_b[:, :].unsqueeze(2), [P, W, D]), ALU.mult))

            tab_l = tab_flat[:, 0:W * D1].rearrange("p (w f) -> p w f", f=D1)
            dve.wait_ge(lane_in[0], 16)
            dve.wait_ge(lane_in[1], 16)
            link(dve.tensor_tensor(acc[:, :, :], acc[:, :, :], aux[:, :, :], ALU.add))
            dve.sem_inc(s.lane_again, 1)
            dve.wait_ge(lane_in[2], 16)
            link(dve.tensor_tensor(acc[:, :, :], acc[:, :, :], tab_l, ALU.add))
            dve.wait_ge(lane_in[3], 16)
            link(dve.tensor_tensor(acc[:, :, :], acc[:, :, :], aux[:, :, :], ALU.add))
            sums_d = acc[:, :, 0:D]
            last_d = acc[:, :, D:D1].rearrange("p w a -> p (w a)")
            link(dve.tensor_scalar(col_a[:, :], last_d, 1.0, None, ALU.max))
            link(dve.reciprocal(col_b[:, :], col_a[:, :]))
            link(dve.tensor_tensor(sums_d, sums_d, bc(col_b[:, :].unsqueeze(2), [P, W, D]), ALU.mult))
            link(dve.tensor_tensor(sums_d, sums_d, x_n[:, :, :], ALU.add))
            norm(sums_d, 1)
            dve.sem_inc(s.node_in, 1)

            dve.sem_inc(s.stage_free, 1)
            with dve.Fori(0, CHUNKS) as c:
                dve.wait_ge(s.node_out, c + (CHUNKS + 1))
                dve.wait_ge(s.stage_free, c + 1)
                for k0 in range(0, WPC, 2):
                    k1 = min(k0 + 2, WPC)
                    pr = products(2, k0, k1)
                    last_stage = dve.tensor_copy(stage[:, k0:k1, :], pr[:, :, 0:2 * D])
                    last = dve.tensor_tensor(tab[:, bass.ds(c * WPC + k0, k1 - k0), :], pr[:, :, 2 * D:4 * D],
                                             bc(bias_d[:, :].unsqueeze(1), [P, k1 - k0, 2 * D]), ALU.add)
                last_stage.then_inc(s.stage_full, 1)
                last.then_inc(s.node_evac, 1)
            dve.wait_ge(s.node_evac, 2 * CHUNKS + 1)
            dve.wait_ge(s.stage_free, CHUNKS + 1)
            dve.sem_inc(s.node_in, 1)

            link(dve.memset(stat, 0.0))
            dve.sem_inc(s.l1_gfree, 2)
            dve.sem_inc(s.l1_yfree, 2)
            dve.sem_inc(s.l1_ybank, 2)
            dve.sem_inc(s.l1_sq, 2)
            dve.sem_inc(s.l1_s1, 1)
            dve.sem_inc(s.l1_s2, 2)
            got = [s.l1_got0, s.l1_got1]
            for b in range(2):
                one_hot(dve, ob[:, b, :, :], b).then_inc(s.l1_o, 1)
            with dve.Fori(0, ITER) as i:
                for b in range(2):
                    dve.wait_ge(s.l1_t, i * 2 + (b + 1))
                    one_hot(dve, ob[:, b, :, :], i * 2 + (b + 2)).then_inc(s.l1_o, 1)
                for b in range(2):
                    g = i * 2 + b
                    dve.wait_ge(s.l1_yfree, g + 1)
                    dve.wait_ge(s.l1_ys, g + 1)
                    dve.wait_ge(got[b], i * (G * 16) + G * 16)
                    dve.tensor_tensor(by_bank(buf_c[:, b, :, :]), ps[:, 4 + 2 * b:6 + 2 * b, :].rearrange("p c (k f) -> p c k f", f=P),
                                      by_bank(buf_b[:, b, :, :]), ALU.add).then_inc(s.l1_y, 1)
                    dve.wait_ge(s.l1_y, g + 1)
                    dve.sem_inc(s.l1_gfree, 1)
                    dve.sem_inc(s.l1_ybank, 1)
                    dve.wait_ge(s.l1_sq, g + 1)
                    dve.tensor_tensor(yv[:, b, :, :], buf_c[:, b, :, :], bc(step_slice(valid_s, g).unsqueeze(2), [P, G, P]),
                                      ALU.mult).then_inc(s.l1_yv, 1)
                    dve.wait_ge(s.l1_yv, g + 1)
                    dve.wait_ge(s.l1_s1, g + 1)
                    dve.tensor_tensor(stat[:, 0, :, :], stat[:, 0, :, :], yv[:, b, :, :], ALU.add).then_inc(s.l1_s1, 1)
                for b in range(2):
                    g = i * 2 + b
                    dve.wait_ge(s.l1_sq, g + 3)
                    dve.wait_ge(s.l1_s2, g + 2)
                    dve.tensor_tensor(stat[:, 1, :, :], stat[:, 1, :, :], sq[:, b, :, :], ALU.add).then_inc(s.l1_s2, 1)
            dve.wait_ge(s.l1_s1, 2 * ITER + 1)
            dve.wait_ge(s.stat_done, 1)
            scale, shift, gam, bet, mean, var, std = (bn_col[:, k:k + 1] for k in (0, 1, 2, 3, 5, 6, 7))
            link(dve.tensor_scalar(mean, ps[:, 4, 0:1], 1.0 / E, None, ALU.mult))
            link(dve.tensor_scalar(var, ps[:, 5, 0:1], 1.0 / E, None, ALU.mult))
            link(dve.tensor_tensor(scale, mean, mean, ALU.mult))
            link(dve.tensor_tensor(var, var, scale, ALU.subtract))
            dve.tensor_scalar(var, var, 0.0, EPS, ALU.max, ALU.add).then_inc(s.bn_ready, 1)
            dve.wait_ge(s.bn_made, 1)
            link(dve.reciprocal(var, std))
            link(dve.tensor_tensor(scale, var, gam, ALU.mult))
            link(dve.tensor_tensor(mean, mean, scale, ALU.mult))
            dve.tensor_tensor(shift, bet, mean, ALU.subtract).then_inc(s.bn_made, 1)
            dve.wait_ge(s.bn_copied, 1)
            link(dve.tensor_copy(bn[:, :, :].rearrange("p a b -> p (a b)"), ps[:, 6, 0:4 * D]))

            link(dve.tensor_scalar(bn[:, :, D:2 * D], bn[:, :, D:2 * D], -1.0, None, ALU.mult))

            def add_windows(g, bank, w0, n, order):
                a = acc_w[:, bass.ds(w0, G), 0:n]
                dve.wait_ge(order, g + 1)
                return dve.tensor_tensor(a, a, regions(bank, n), ALU.add).then_inc(order, 1)

            dve.wait_ge(s.l1_yfree, 2 * ITER + 2)
            for half in range(2):
                link(dve.memset(lb_rows[half][:, :, :, D:D1], 1.0))
            dve.memset(acc_w[:, :, :], 0.0).then_inc(s.lb_acc, 1)
            dve.sem_inc(s.bn_rows, 1)
            dve.sem_inc(s.lb_accfree, 4)
            dve.sem_inc(s.lb_made, 4)

            def lb_add(g, q):
                w0 = load1(mybir.EngineType.DVE, win_s, g, W - 1)
                dve.wait_ge(s.lb_out, g + 1)
                add_windows(g, 2 * q, w0, D1, s.lb_acc)
                dve.wait_ge(s.lb_acc, g + 2)
                dve.sem_inc(s.lb_accfree, 1)

            def lb_pair(i, half, first):
                for b in range(2):
                    g = i * 2 + b
                    dve.wait_ge(s.lb_z, g * 2 + 2)
                    dve.wait_ge(s.lb_made, g + 3)
                    dve.tensor_scalar(buf_b[:, b, :, :], z_buf[:, 2 * half + b, :, :], 88.0, None, ALU.min).then_inc(s.lb_min, 1)
                if not first:
                    for b in range(2):
                        lb_add(i * 2 + b - 4, 2 * half + b)
                for b in range(2):
                    one_hot(dve, lb_hot[half][:, b, :, :], i * 2 + b).then_inc(s.lb_o, 1)
                for b in range(2):
                    g = i * 2 + b
                    z = z_buf[:, 2 * half + b, :, 0:D]
                    dve.wait_ge(s.lb_exp, g * 3 + 3)
                    dve.tensor_tensor(z, z, buf_b[:, b, :, 0:D], ALU.max).then_inc(s.lb_dve, 1)
                for b in range(2):
                    g = i * 2 + b
                    z = z_buf[:, 2 * half + b, :, 0:D]
                    dve.wait_ge(s.lb_dve, g + 1)
                    dve.tensor_tensor(lb_rows[half][:, b, :, 0:D], z, buf_b[:, b, :, D:2 * D], ALU.mult).then_inc(s.lb_msg, 1)
                for b in range(2):
                    dve.wait_ge(s.lb_msg, i * 2 + b + 1)
                    dve.sem_inc(s.lb_made, 1)

            for half in range(2):
                lb_pair(half, half, True)
            with dve.Fori(1, ITER // 2) as i:
                for half in range(2):
                    lb_pair(i * 2 + half, half, False)
            for q in range(4):
                lb_add(2 * ITER - 4 + q, q)
            link(dve.tensor_copy(deg[:, :], last_d))
            link(dve.scalar_tensor_tensor(sums_d, x_n[:, :, :], 2.0, sums_d, ALU.mult, ALU.add))
            norm(sums_d, 2)
            dve.sem_inc(s.node_in, 1)

            link(dve.memset(stage[:, 0:WPC, D:D1], 1.0))
            with dve.Fori(0, CHUNKS) as c:
                dve.wait_ge(s.node_out, c + (2 * CHUNKS + 1))
                dve.wait_ge(s.stage_free, c + (CHUNKS + 1))
                for k0, k1 in ((0, 4), (4, 7)):
                    pr = products(4, k0, k1)
                    dve.tensor_copy(stage[:, k0:k1, 0:D], pr[:, :, 0:D])
                    last_stage = dve.tensor_copy(stage[:, k0:k1, D1:D2], pr[:, :, D:D1])
                    last = dve.tensor_copy(sums[:, bass.ds(c * WPC + k0, k1 - k0), 0:1], pr[:, :, D1:D2])
                last_stage.then_inc(s.stage_full, 1)
                last.then_inc(s.node_evac, 1)
            dve.wait_ge(s.stage_free, 2 * CHUNKS + 1)
            dve.wait_ge(s.node_evac, 3 * CHUNKS + 1)
            dve.memset(mx[:, :], -BIG).then_inc(s.l2_mx, 1)
            dve.sem_inc(s.l2_maskfree, 2)
            dve.sem_inc(s.l2_hfree, 2)
            with dve.Fori(0, ITER) as i:
                for b in range(2):
                    g = i * 2 + b
                    for u in range(G):
                        last = dve.tensor_scalar(buf_a[:, b, u, :], iota[:, :], step_col(dst_s, g, u), -BIG, ALU.not_equal, ALU.mult)
                    last.then_inc(s.l2_nm, 1)
                for b in range(2):
                    g = i * 2 + b
                    ws = load8(mybir.EngineType.DVE, win_s, g, W - 1)
                    dve.wait_ge(s.l2_mask, g + 1)
                    dve.tensor_reduce(tmp_c[:, b, :], regions(2 * b, P), AX.X, ALU.max).then_inc(s.l2_max, 1)
                    dve.wait_ge(s.l2_max, g + 1)
                    dve.sem_inc(s.l2_maskfree, 1)
                    for u in range(G):
                        m = mx[:, bass.ds(ws[u], 1)]
                        dve.wait_ge(s.l2_mx, g * G + (u + 1))
                        dve.tensor_tensor(m, m, tmp_c[:, b, u:u + 1], ALU.max).then_inc(s.l2_mx, 1)
            dve.wait_ge(s.l2_mx, S + 1)
            sc, mxc = sums[:, :, 0:1].rearrange("p w a -> p (w a)"), sums[:, :, 1:2].rearrange("p w a -> p (w a)")
            link(dve.tensor_tensor(col_a[:, :], mx[:, :], sc, ALU.add))
            link(dve.scalar_tensor_tensor(mxc, col_a[:, :], 0.2, col_a[:, :], ALU.mult, ALU.max))
            rest = col_b[:, :]
            for k, v in enumerate((sc, mxc)):
                for part in range(3):
                    v_b = sums_b[:, :, 2 * part + k:2 * part + k + 1].rearrange("p w a -> p (w a)")
                    link(dve.tensor_copy(v_b, v if part == 0 else rest))
                    if part < 2:
                        link(dve.tensor_tensor(rest, v if part == 0 else rest, v_b, ALU.subtract))
            dve.sem_inc(s.mx_done, 1)

            dve.memset(acc_w[:, :, :], 0.0).then_inc(s.l2b_acc, 1)
            dve.sem_inc(s.l2b_hfree, 2)
            dve.sem_inc(s.l2b_accfree, 2)
            h_in = [s.l2b_h0, s.l2b_h1]
            KL2 = 4

            def l2b_scores(i, b):
                g = i * 2 + b
                k = 0

                def chain(ins):
                    nonlocal k
                    k += 1
                    ins.then_inc(s.l2b_dve, 1)
                    dve.wait_ge(s.l2b_dve, i * (2 * KL2) + (b * KL2 + k))
                per_edge = ps[:, 2 + b, 0:6 * G].rearrange("p (u q k) -> p u k q", k=2, q=3)
                score, st = tmp_c[:, b, :], target[:, b, :, :]
                dve.wait_ge(s.l2b_s, g + 1)
                chain(dve.tensor_reduce(st, per_edge, AX.X, ALU.add))
                dve.wait_ge(h_in[b], i * 16 + 16)
                chain(dve.tensor_tensor(score, rows[:, b, :, D1:D2].rearrange("p u a -> p (u a)"),
                                        st[:, :, 0:1].rearrange("p u a -> p (u a)"), ALU.add))
                chain(dve.scalar_tensor_tensor(score, score, 0.2, score, ALU.mult, ALU.max))
                chain(dve.tensor_tensor(score, score, st[:, :, 1:2].rearrange("p u a -> p (u a)"), ALU.subtract))
                dve.tensor_scalar(tmp_c[:, 2 + b, :], score, 0.0, None, ALU.min).then_inc(s.l2b_arg, 1)
                assert k == KL2

            def l2b_add(g, b):
                w0 = load1(mybir.EngineType.DVE, win_s, g, W - 1)
                dve.wait_ge(s.l2b_out, g + 1)
                add_windows(g, 4 + 2 * b, w0, D1, s.l2b_acc)
                dve.wait_ge(s.l2b_acc, g + 2)
                dve.sem_inc(s.l2b_accfree, 1)

            def l2b_pair(i, half, first, last):
                for b in range(2):
                    l2b_scores(i, b)
                if not last:
                    for b in range(2):
                        dve.wait_ge(s.l2b_t, i * 2 + (b + 1))
                        one_hot(dve, ob[:, b, :, :], i * 2 + (b + 2)).then_inc(s.l2b_o, 1)
                for b in range(2):
                    g = i * 2 + b
                    one_hot(dve, l2b_hot[half][:, b, :, :], g).then_inc(s.l2b_o32, 1)
                    dve.wait_ge(s.l2b_exp, g + 1)
                    dve.tensor_tensor(l2b_rows[half][:, b, :, 0:D1], rows[:, b, :, 0:D1], bc(ex[:, b, :].unsqueeze(2), [P, G, D1]),
                                      ALU.mult).then_inc(s.l2b_ow, 1)
                if not first:
                    for b in range(2):
                        l2b_add(i * 2 + b - 2, b)
                for b in range(2):
                    dve.wait_ge(s.l2b_ow, i * 2 + b + 1)
                    dve.sem_inc(s.l2b_hfree, 1)

            for b in range(2):
                one_hot(dve, ob[:, b, :, :], b).then_inc(s.l2b_o, 1)
            l2b_pair(0, 0, True, False)
            with dve.Fori(0, ITER // 2 - 1) as i:
                for half in (1, 0):
                    l2b_pair(i * 2 + (2 - half), half, False, False)
            l2b_pair(ITER - 1, 1, False, True)
            for b in range(2):
                l2b_add(2 * ITER - 2 + b, b)
            link(dve.tensor_scalar(col_a[:, :], last_d, 1e-30, None, ALU.max))
            link(dve.reciprocal(col_b[:, :], col_a[:, :]))
            link(dve.tensor_tensor(sums_d, sums_d, bc(col_b[:, :].unsqueeze(2), [P, W, D]), ALU.mult))
            dve.tensor_scalar(scratch, sums_d, 0.0, None, ALU.min).then_inc(s.elu_in, 1)
            link(dve.scalar_tensor_tensor(sums_d, sums_d, 0.0, x_n[:, :, :], ALU.max, ALU.add))
            dve.wait_ge(s.elu_out, 1)
            link(dve.scalar_tensor_tensor(sums_d, scratch, -1.0, sums_d, ALU.add, ALU.add))
            norm(sums_d, 3)
            dinv = mx[:, :]
            dve.tensor_scalar(col_a[:, :], deg[:, :], 1.0, None, ALU.max).then_inc(s.ln_var, 1)
            dve.wait_ge(s.ln_std, 4)
            link(dve.reciprocal(col_b[:, :], col_b[:, :]))
            link(dve.scalar_tensor_tensor(dinv, deg[:, :], 0.0, col_b[:, :], ALU.is_gt, ALU.mult))
            dinv_bc = bc(mx[:, :].unsqueeze(2), [P, W, D])

            link(dve.tensor_tensor(tab_d, x_n[:, :, :], dinv_bc, ALU.mult))
            dve.sem_inc(s.gcn_in0, 1)

            def gcn(got, o, outs, accfree, gfree, order):
                dve.memset(acc_w[:, :, :], 0.0).then_inc(order, 1)
                dve.sem_inc(accfree, 2)
                dve.sem_inc(gfree, 2)
                dve.sem_inc(outs, 2)
                with dve.Fori(0, ITER) as i:
                    for b in range(2):
                        g = i * 2 + b
                        dve.wait_ge(outs, g + 1)
                        one_hot(dve, buf_a[:, b, :, :], g).then_inc(o, 1)
                    for b in range(2):
                        g = i * 2 + b
                        w0 = load1(mybir.EngineType.DVE, win_s, g, W - 1)
                        dve.wait_ge(outs, g + 3)
                        dve.sem_inc(gfree, 1)
                        add_windows(g, 2 * b, w0, D, order)
                        dve.wait_ge(order, g + 2)
                        dve.sem_inc(accfree, 1)

            gcn([s.g0_got0, s.g0_got1], s.g0_o, s.g0_out, s.g0_accfree, s.g0_gfree, s.g0_acc)
            dve.wait_ge(s.gcn_st0, 16)
            link(dve.tensor_tensor(tab_d, sums_d, dinv_bc, ALU.mult))
            dve.sem_inc(s.node_in, 1)
            with dve.Fori(0, CHUNKS) as c:
                dve.wait_ge(s.node_out, c + (3 * CHUNKS + 1))
                for k0, k1 in ((0, 4), (4, 7)):
                    last = dve.tensor_tensor(acc[:, bass.ds(c * WPC + k0, k1 - k0), 0:D], products(4, k0, k1)[:, :, 0:D],
                                             bc(bias3[:, 0:1, :], [P, k1 - k0, D]), ALU.add)
                last.then_inc(s.node_evac, 1)
            dve.wait_ge(s.node_evac, 4 * CHUNKS + 1)
            link(dve.scalar_tensor_tensor(tab_d, sums_d, 0.0, dinv_bc, ALU.max, ALU.mult))
            dve.sem_inc(s.gcn_in1, 1)
            gcn([s.g1_got0, s.g1_got1], s.g1_o, s.g1_out, s.g1_accfree, s.g1_gfree, s.g1_acc)
            dve.wait_ge(s.gcn_st1, 16)
            link(dve.tensor_tensor(tab_d, sums_d, dinv_bc, ALU.mult))
            dve.sem_inc(s.node_in, 1)
            with dve.Fori(0, CHUNKS) as c:
                dve.wait_ge(s.node_out, c + (4 * CHUNKS + 1))
                for k0, k1 in ((0, 4), (4, 7)):
                    last = dve.tensor_tensor(acc[:, bass.ds(c * WPC + k0, k1 - k0), 0:D], products(4, k0, k1)[:, :, 0:D],
                                             bc(bias3[:, 1:2, :], [P, k1 - k0, D]), ALU.add)
                last.then_inc(s.node_evac, 1)
            dve.wait_ge(s.node_evac, 5 * CHUNKS + 1)
            link(dve.tensor_tensor(sums_d, sums_d, x_n[:, :, :], ALU.add))
            norm(sums_d, 5)
            dve.sem_inc(s.result_ready, 1)


_INS = ['x', 'src', 'dst', 'edge_attr_16', 'edge_attr_64', 'L0_gnn_W_edge', 'L0_gnn_b_edge', 'L0_gnn_W_node', 'L0_gnn_b_node',
        'L1_gnn_W_filter', 'L1_gnn_b_filter', 'L1_gnn_gamma_filter', 'L1_gnn_beta_filter',
        'L1_gnn_W_core', 'L1_gnn_b_core', 'L1_gnn_gamma_core', 'L1_gnn_beta_core',
        'L2_gnn_W', 'L2_gnn_a', 'L3_gnn_W1', 'L3_gnn_b1', 'L3_gnn_W2', 'L3_gnn_b2']


def kernel(**inputs):
    import numpy as _np
    import concourse.bacc as _bacc
    from concourse import mybir as _mybir
    from concourse.bass_utils import run_bass_kernel_spmd as _run

    nc = _bacc.Bacc("TRN2", target_bir_lowering=False, num_devices=1)
    arrays, args = {}, []
    for name in _INS:
        a = _np.ascontiguousarray(inputs[name])
        arrays[f"in_{name}_dram"] = a
        args.append(nc.dram_tensor(f"in_{name}_dram", a.shape, _mybir.dt.from_np(a.dtype), kind="ExternalInput").ap())
    out = nc.dram_tensor("out_dram", (N, D), _mybir.dt.float32, kind="ExternalOutput").ap()
    build(nc, *args, out)
    r = _run(nc, [arrays], core_ids=[0])
    return r.results[0]["out_dram"]
```

```python
from collections import namedtuple
from contextlib import ExitStack

import concourse.bass as bass
from concourse import mybir

ALU = mybir.AluOpType
ACT = mybir.ActivationFunctionType
AX = mybir.AxisListType
F32 = mybir.dt.float32
BF16 = mybir.dt.bfloat16
I32 = mybir.dt.int32

P = 128
N = 12500
E = 200000
D = 64
K16 = 16
W = -(-N // P)
NP = W * P
FULL_W = N // P
TAIL_N = N - FULL_W * P
T = -(-E // P)
FULL_T = E // P
HALF = E - FULL_T * P
TB = -(-T // P)
TAIL_T = FULL_T - (TB - 1) * P
G = 8
PAIR = 2 * G
S = -(-(T + W - 1) // P) * P
SB = S // P
ITER = S // PAIR
SPAD = S + 2 * PAIR
CHUNKS_S = 4
CH = S // CHUNKS_S
NOWHERE = 1 << 20
TRASH = NP
SROWS = NP + P
LANES = 4
WPC = 7
CHUNKS = W // WPC
OUT_PARTS = ((0, W // 2), (W // 2, W))
D1 = D + 1
D2 = D + 2
ZEROS = 195
BIG = 2.0 ** 100
EPS = 1e-5
assert SB == TB and CHUNKS * WPC == W and CHUNKS % 2 == 0 and ITER % 2 == 0 and ITER * PAIR == S and CH <= 512 and SROWS * D1 // P % ZEROS == 0


def build(nc, x, src, dst, ea16, ea64, w_edge, b_edge, w_node, b_node,
          w_filter, b_filter, gamma_f, beta_f, w_core, b_core, gamma_c, beta_c,
          w_att, a_att, w1, b1, w2, b2, out):
    with ExitStack() as ctx:
        def sb(name, shape, dt=F32):
            return ctx.enter_context(nc.sbuf_tensor(name, shape, dt))

        def sem(name):
            return ctx.enter_context(nc.semaphore(name))

        def dram(name, shape, dt=F32):
            return nc.dram_tensor(name, shape, dt, kind="Internal").ap()

        lane_tab = [dram(f"lane_tab{k}", (SROWS, D1)) for k in range(LANES)]
        src_tab = dram("src_tab", (NP, 2 * D))
        att_tab = dram("att_tab", (NP, D2))
        gcn_tab = [dram(f"gcn_tab{k}", (NP, D)) for k in range(2)]
        y_stash = dram("y_stash", (2 * ITER, P, G * 2 * D))
        h_stash = dram("h_stash", (2 * ITER, P, G * D2))

        x_n = sb("x_n", [P, W, D])
        acc_w = sb("acc_w", [P, W + G, D1])
        acc = acc_w[:, 0:W, :]
        tab = sb("tab", [P, W, 2 * D])
        aux = sb("aux", [P, W, D1])
        src_s = sb("src_s", [P, SPAD])
        dst_s = sb("dst_s", [P, SPAD])
        gate_s = sb("gate_s", [P, SPAD])
        valid_s = sb("valid_s", [P, SPAD])
        place_s = sb("place_s", [2 * 32 + 1, SPAD], I32)
        win_s, row_s, rel_s = place_s[0:1, :], place_s[32:33, :], place_s[64:65, :]
        buf_a = sb("buf_a", [P, 2, G, 2 * D])
        buf_b = sb("buf_b", [P, 2, G, 2 * D])
        buf_c = sb("buf_c", [P, 2, G, 2 * D])
        buf_d = sb("buf_d", [P, 2, G, 2 * D])
        rows = sb("rows", [P, 2, G, D2])
        sums = sb("sums", [P, W, 2])
        sums_b = sb("sums_b", [P, W, 6], BF16)
        mx = sb("mx", [P, W])
        col_a = sb("col_a", [P, W])
        col_b = sb("col_b", [P, W])
        idx = sb("idx", [P, 2, G], I32)
        idxf = sb("idxf", [P, 2, G])
        srcg = sb("srcg", [P, 2, G])
        dup = sb("dup", [P, 2, G])
        tmp_c = sb("tmp_c", [P, 4, G])
        ex = sb("ex", [P, 2, G])
        target = sb("target", [P, 2, G, 2])
        iota = sb("iota", [P, P])
        ident = sb("ident", [P, P])
        ident_b = sb("ident_b", [P, P], BF16)
        zero_b = sb("zero_b", [P, P], BF16)
        below = sb("below", [P, P])
        ids = sb("ids", [P, TB])
        zeros = sb("zeros", [P, ZEROS])
        trash = sb("trash", [P, 1])
        ones = sb("ones", [P, P])
        key = sb("key", [P, TB])
        last_i = sb("last_i", [P, TB], I32)
        t_col = sb("t_col", [P, TB])
        wsm = rows[:, :, :, :].rearrange("p a b c -> p (a b c)")[:, 512:1024]
        wt = sb("wt", [P, 640])
        bias0 = sb("bias0", [P, D])
        bias_d = sb("bias_d", [P, 2 * D])
        bias3 = sb("bias3", [P, 2, D])
        we_bc = sb("we_bc", [P, K16])
        be_c = sb("be_c", [P, 1])
        bn_col = sb("bn_col", [P, 8])
        bn = sb("bn", [P, 2, 2 * D])
        deg = sb("deg", [P, W])

        aux_flat = aux[:, :, :].rearrange("p a b -> p (a b)")
        ob = aux_flat[:, 0:G * P].bitcast(BF16).rearrange("p (b u f) -> p b u f", b=2, u=G)
        ot_b = buf_d[:, 0, :, :].rearrange("p u f -> p (u f)").bitcast(BF16).rearrange("p (b u f) -> p b u f", b=2, u=G)
        sq = aux_flat[:, G * P:3 * G * P].rearrange("p (b u f) -> p b u f", b=2, u=G)
        ea_s = aux_flat[:, 3 * G * P:5 * G * P].rearrange("p (q u f) -> p q u f", q=4, u=G)
        acc_flat = acc_w[:, :, :].rearrange("p a b -> p (a b)")
        stat = acc_flat[:, 0:2 * G * P].rearrange("p (k u f) -> p k u f", k=2, u=G)
        yv = acc_flat[:, 2 * G * P:4 * G * P].rearrange("p (b u f) -> p b u f", b=2, u=G)
        y_buf = tab[:, 0:4 * G, :].rearrange("p (q u) f -> p q u f", q=4)
        z_buf = tab[:, 4 * G:8 * G, :].rearrange("p (q u) f -> p q u f", q=4)
        tab_flat = tab[:, :, :].rearrange("p a b -> p (a b)")
        hot2 = tab[:, 8 * G:10 * G, :].rearrange("p (b u) f -> p b u f", b=2)
        lb_hot, lb_rows = [buf_a, hot2], [buf_c, buf_d]
        h2 = tab_flat[:, 10 * G * 2 * D:10 * G * 2 * D + 2 * G * D2].rearrange("p (b u f) -> p b u f", b=2, u=G)
        ob4 = aux_flat[:, 0:2 * G * P].bitcast(BF16).rearrange("p (q u f) -> p q u f", q=4, u=G)
        l2b_h = [rows, h2]
        l2b_hot, l2b_rows = [buf_a, hot2], [buf_c, buf_b]
        xt_at, xs_at = W * D1 - 2 * WPC * P, W * D1 - 2 * WPC * P - 2 * WPC * D
        xs = [aux_flat[:, xs_at + k * WPC * D:xs_at + (k + 1) * WPC * D].rearrange("p (w f) -> p w f", f=D) for k in range(2)]
        xt = [aux_flat[0:D, xt_at + k * WPC * P:xt_at + (k + 1) * WPC * P] for k in range(2)]

        ps = ctx.enter_context(nc.psum_tensor("ps", [P, 8, 512], F32))

        def region(k, n):
            return ps[:, k // 4, (k % 4) * P:(k % 4) * P + n]

        ps_flat = ps[:, :, :].rearrange("p a b -> p (a b)")

        def regions(bank, n):
            return ps[:, bank:bank + 2, :].rearrange("p c (k f) -> p (c k) f", f=P)[:, :, 0:n]

        def by_bank(ap):
            return ap.rearrange("p (k c) f -> p c k f", c=2)

        src_t = buf_a[:, :, :, :].rearrange("p a b c -> p (a b) c")[:, 0:TB, :].bitcast(I32)
        dst_t = buf_b[:, :, :, :].rearrange("p a b c -> p (a b) c")[:, 0:TB, :].bitcast(I32)
        src_f = buf_c[:, :, :, :].rearrange("p a b c -> p (a b) c")[:, 0:TB, :]
        dst_f = buf_d[:, :, :, :].rearrange("p a b c -> p (a b) c")[:, 0:TB, :]
        gate_t = aux[:, :, :].rearrange("p a b -> p (a b)")[:, 0:TB * P].rearrange("p (b e) -> p b e", e=P)
        t_row = aux[:, :, :].rearrange("p a b -> p (a b)")[:, TB * P:TB * P + S]
        w_row = aux[:, :, :].rearrange("p a b -> p (a b)")[:, TB * P + S:TB * P + 2 * S]
        scr_i = rows[:, :, :, :].rearrange("p a b c -> p (a b c)").bitcast(I32)
        step_i = acc_flat[:, 0:S].bitcast(I32)
        step_f = acc_flat[:, S:2 * S]
        junk = acc_flat[:, 2 * S:3 * S]
        EB = P * K16
        sel = tab_flat[:, 0:TB * CH].rearrange("p (b s) -> p b s", s=CH)
        x_flat = tab_flat
        tab_d = tab_flat[:, 0:W * D].rearrange("p (w f) -> p w f", f=D)
        scratch = tab_flat[:, W * D:2 * W * D].rearrange("p (w f) -> p w f", f=D)
        stage = buf_a[:, :, :, :].rearrange("p a b c -> p (a b) c")

        NAMES = [
            "passed",
            "iotas_made",
            "consts_made",
            "tiles_clean",
            "tiles_loaded",
            "weights_loaded",
            "bias_loaded",
            "x_clean",
            "x_loaded",
            "ea_loaded0",
            "ea_loaded1",
            "ea_loaded2",
            "ea_loaded3",
            "ea_clean",
            "dve_done",
            "key_ready",
            "key_rows",
            "tile_cols",
            "tile_rows",
            "places_made",
            "selected",
            "select_done",
            "steps_made",
            "gate_lin",
            "gate_done",
            "wt_made",
            "wt_copied",
            "wa_made",
            "node_in",
            "node_xs",
            "node_xt",
            "node_xt_copied",
            "node_products",
            "node_evacuated",
            "stage_full",
            "stage_free",
            "tab_stored",
            "norm_var",
            "norm_std",
            "zeros_made",
            "lane_done0",
            "lane_done1",
            "lane_done2",
            "lane_done3",
            "l0_sources",
            "l0_source_rows",
            "l0_gated_hot",
            "l0_same",
            "l0_rows_known",
            "l0_gates",
            "l0_gates_copied",
            "l0_sums",
            "l0_sums_copied",
            "l0_slot_free",
            "l0_landed",
            "l0_chain",
            "lanes_done",
            "lane_in0",
            "lane_in1",
            "lane_in2",
            "lane_in3",
            "lane_again",
            "l1_indices",
            "l1_rows_used",
            "l1_got0",
            "l1_got1",
            "l1_hot",
            "l1_transposed",
            "l1_trans_copied",
            "l1_products",
            "l1_bank_free",
            "l1_made",
            "l1_stored",
            "l1_masked",
            "l1_squared",
            "l1_added",
            "l1_sq_added",
            "edges_in0",
            "edges_in1",
            "edges_in2",
            "edges_in3",
            "y_stored0",
            "y_stored1",
            "stat_done",
            "bn_var",
            "bn_made",
            "bn_spread",
            "bn_ready",
            "l1b_y_in0",
            "l1b_y_in1",
            "l1b_y_in2",
            "l1b_y_in3",
            "l1b_y_used",
            "l1b_normed",
            "l1b_clamped",
            "l1b_act",
            "l1b_softplus",
            "l1b_hot",
            "l1b_messages",
            "l1b_slot_free",
            "l1b_sums",
            "l1b_bank_free",
            "l1b_added",
            "l2_indices",
            "l2_got0",
            "l2_got1",
            "l2_not_hot",
            "l2_scores",
            "l2_max",
            "l2_bank_free",
            "l2_max_kept",
            "h_stored0",
            "h_stored1",
            "l2_rows_used",
            "max_done",
            "l2b_h_in0",
            "l2b_h_in1",
            "l2b_h_in2",
            "l2b_h_in3",
            "l2b_rows_used",
            "l2b_hot",
            "l2b_transposed",
            "l2b_trans_copied",
            "l2b_hot_copied",
            "l2b_targets",
            "l2b_chain",
            "l2b_args",
            "l2b_weights",
            "l2b_weighted",
            "l2b_sums",
            "l2b_bank_free",
            "l2b_added",
            "elu_in",
            "elu_out",
            "gcn_in0",
            "gcn_in1",
            "gcn_stored0",
            "gcn_stored1",
            "g0_indices",
            "g1_indices",
            "g0_got0",
            "g0_got1",
            "g1_got0",
            "g1_got1",
            "g0_hot",
            "g1_hot",
            "g0_sums",
            "g1_sums",
            "g0_bank_free",
            "g1_bank_free",
            "g0_rows_used",
            "g1_rows_used",
            "g0_added",
            "g1_added",
            "result_ready",
            "result_stored",
        ]
        s = namedtuple("Semaphores", NAMES)(*[sem(n) for n in NAMES])
        fill = [s.lane_done0, s.lane_done1, s.lane_done2, s.lane_done3]
        y_in = [s.l1b_y_in0, s.l1b_y_in1, s.l1b_y_in2, s.l1b_y_in3]
        h_in = [s.l2b_h_in0, s.l2b_h_in1, s.l2b_h_in2, s.l2b_h_in3]
        e_in = [s.edges_in0, s.edges_in1, s.edges_in2, s.edges_in3]
        lane_in = [s.lane_in0, s.lane_in1, s.lane_in2, s.lane_in3]

        def bc(ap, shape):
            return ap.to_broadcast(shape)

        def step_slice(t, g):
            return t[:, bass.ds(g * G, G)]

        def step_col(t, g, u):
            return t[:, bass.ds(g * G + u, 1)]

        def load8(engine, table, g, top):
            _, v = nc.values_load_multi_w_load_instructions(
                table[:, bass.ds(g * G, G)], engines=(engine,), min_val=0, max_val=top,
                skip_runtime_bounds_check_because="the table's entries are clamped to it")
            return v

        def load1(engine, table, g, top):
            _, v = nc.values_load_multi_w_load_instructions(
                table[:, bass.ds(g * G, 1)], engines=(engine,), min_val=0, max_val=top,
                skip_runtime_bounds_check_because="the table's entries are clamped to it")
            return v[0]

        def one_hot(engine, to, g):
            return engine.tensor_tensor(to, bc(iota[:, :].unsqueeze(1), [P, G, P]),
                                        bc(step_slice(dst_s, g).unsqueeze(2), [P, G, P]), ALU.is_equal)

        def window(t, w, n, start=0):
            return t[:, bass.ds(w, 1), start:start + n].rearrange("p a b -> p (a b)")

        def blocks_of(c):
            first, last = max(c * CH - (W - 1), 0), c * CH + CH - 1
            return range(first // P, last // P + 1)

        block = ctx.enter_context(nc.Block())

        WN, WC, WF, WA = 0, D, 4 * D, 7 * D
        TN, TS, TE, TA = 0, D, 5 * D, 7 * D
        a2 = sb("a2", [D, 2])
        w12 = sb("w12", [D, 2, D])

        @block.sync
        def _(sp):
            sp.wait_ge(s.tiles_clean, 2)
            body = (TB - 1) * P * P
            for tile, arr in ((src_t, src), (dst_t, dst)):
                sp.dma_start(tile[:, 0:TB - 1, :], arr[0:body].rearrange("(b t e) -> t b e", t=P, e=P)).then_inc(s.tiles_loaded, 16)
                sp.dma_start(tile[0:TAIL_T, TB - 1, :],
                             arr[body:FULL_T * P].rearrange("(t e) -> t e", e=P)).then_inc(s.tiles_loaded, 16)
                sp.dma_start(tile[TAIL_T:TAIL_T + 1, TB - 1, P - HALF:P],
                             arr[FULL_T * P:E].rearrange("(a e) -> a e", a=1)).then_inc(s.tiles_loaded, 16)
            sp.dma_start(we_bc[:, :], w_edge.rearrange("k a -> (a k)").partition_broadcast(P)).then_inc(s.weights_loaded, 16)
            sp.dma_start(be_c[:, :], b_edge.partition_broadcast(P)).then_inc(s.weights_loaded, 16)

            def load_ea(b, slot, done):
                view = x_flat[:, slot * EB:(slot + 1) * EB]
                if b < TB - 1:
                    sp.dma_start(view, ea16[b * P * P:(b + 1) * P * P, :].rearrange("(t e) k -> t (e k)", e=P)).then_inc(done, 16)
                else:
                    sp.dma_start(view[0:TAIL_T, :], ea16[b * P * P:FULL_T * P, :].rearrange("(t e) k -> t (e k)", e=P)).then_inc(done, 16)
                    sp.dma_start(view[TAIL_T:TAIL_T + 1, (P - HALF) * K16:EB],
                                 ea16[FULL_T * P:E, :].rearrange("(a e) k -> a (e k)", a=1)).then_inc(done, 16)

            for b in range(6):
                load_ea(b, b, s.ea_loaded0)
            sp.dma_start(wsm[0:D, WN:WN + D], w_node).then_inc(s.weights_loaded, 16)
            sp.dma_start(wsm[0:D, WC:WC + 3 * D], w_core).then_inc(s.weights_loaded, 16)
            sp.dma_start(wsm[0:D, WF:WF + 3 * D], w_filter).then_inc(s.weights_loaded, 16)
            sp.dma_start(wsm[0:D, WA:WA + D], w_att).then_inc(s.weights_loaded, 16)
            with nc.allow_non_contiguous_dma(reason="128 single elements, once"):
                sp.dma_start(a2[:, :], a_att.rearrange("(k d) -> d k", k=2)).then_inc(s.weights_loaded, 16)
            sp.dma_start(w12[:, 0, :], w1).then_inc(s.weights_loaded, 16)
            sp.dma_start(w12[:, 1, :], w2).then_inc(s.weights_loaded, 16)
            sp.dma_start(bias0[:, :], b_node.partition_broadcast(P)).then_inc(s.bias_loaded, 16)
            sp.dma_start(bias_d[:, 0:D], b_core.partition_broadcast(P)).then_inc(s.bias_loaded, 16)
            sp.dma_start(bias_d[:, D:2 * D], b_filter.partition_broadcast(P)).then_inc(s.bias_loaded, 16)
            sp.dma_start(bias3[:, 0, :], b1.partition_broadcast(P)).then_inc(s.bias_loaded, 16)
            sp.dma_start(bias3[:, 1, :], b2.partition_broadcast(P)).then_inc(s.bias_loaded, 16)
            for k, (gam, half) in enumerate(((gamma_c, 0), (gamma_f, 1), (beta_c, 0), (beta_f, 1))):
                sp.dma_start(bn_col[half * D:half * D + D, 2 + k // 2:3 + k // 2], gam.rearrange("(d a) -> d a", a=1)).then_inc(s.bias_loaded, 16)
            sp.wait_ge(s.x_clean, 1)
            sp.dma_start(x_n[:, 0:FULL_W, :], x[0:FULL_W * P, :].rearrange("(w p) f -> p w f", p=P)).then_inc(s.x_loaded, 16)
            sp.dma_start(x_n[0:TAIL_N, FULL_W, :], x[FULL_W * P:N, :]).then_inc(s.x_loaded, 16)
            for half in range(2):
                sp.wait_ge(s.ea_clean, half + 1)
                for b in range(3):
                    load_ea(6 + 3 * half + b, 3 * half + b, (s.ea_loaded1, s.ea_loaded2)[half])
            sp.wait_ge(s.ea_clean, 3)
            load_ea(12, 0, s.ea_loaded3)

            sp.wait_ge(s.lanes_done, 1)

            def lane_rows(k):
                return lane_tab[k][0:NP, :].rearrange("(p w) f -> p w f", p=P)

            tab_l = tab_flat[:, 0:W * D1].rearrange("p (w f) -> p w f", f=D1)
            for k, to in ((0, acc[:, :, :]), (1, aux[:, :, :]), (2, tab_l)):
                sp.dma_start(to, lane_rows(k)).then_inc(lane_in[k], 16)
            sp.wait_ge(s.lane_again, 1)
            sp.dma_start(aux[:, :, :], lane_rows(3)).then_inc(lane_in[3], 16)

            def store_tab(table, n, base):
                with sp.Fori(0, CHUNKS // 2) as i:
                    for k in range(2):
                        c = i * 2 + k
                        sp.wait_ge(s.stage_full, c + (base + 1))
                        sp.dma_start(table.rearrange("(p w) f -> p w f", p=P)[:, bass.ds(c * WPC, WPC), :],
                                     stage[:, WPC * k:WPC * (k + 1), 0:n]).then_inc(s.tab_stored, 16)
                        sp.wait_ge(s.tab_stored, c * 16 + (base + 1) * 16)
                        sp.sem_inc(s.stage_free, 1)

            store_tab(src_tab, 2 * D, 0)

            y_out = [s.y_stored0, s.y_stored1]

            def load_edges(g, q):
                starts = load8(mybir.EngineType.SP, row_s, g, E - P)
                for u in range(G):
                    sp.dma_start(ea_s[:, q, u, :], ea64[bass.ds(starts[u], P), :]).then_inc(e_in[q], 16)

            def l1_pair(i, half, first):
                for b in range(2):
                    g = i * 2 + b
                    sp.wait_ge(s.l1_transposed, g + 1)
                    sp.sem_inc(s.passed, 1)
                    load_edges(g + 4, 2 * half + b)
                if not first:
                    for b in range(2):
                        sp.wait_ge(y_out[b], i * 16)
                        sp.sem_inc(s.l1_stored, 1)
                for b in range(2):
                    g = i * 2 + b
                    sp.wait_ge(s.l1_made, g + 1)
                    sp.dma_start(y_stash[bass.ds(g, 1), :, :].rearrange("a p f -> (a p) f"),
                                 buf_c[:, b, :, :].rearrange("p u f -> p (u f)")).then_inc(y_out[b], 16)

            for q in range(4):
                load_edges(q, q)
            l1_pair(0, 0, True)
            l1_pair(1, 1, False)
            with sp.Fori(1, ITER // 2) as i:
                for half in range(2):
                    l1_pair(i * 2 + half, half, False)
            for b in range(2):
                sp.wait_ge(y_out[b], ITER * 16)
            sp.sem_inc(s.l1_stored, 2)
            for q in range(4):
                sp.wait_ge(e_in[q], (ITER // 2 + 1) * G * 16)

            with sp.Fori(0, ITER // 2) as i:
                for q in range(4):
                    g = i * 4 + q
                    sp.wait_ge(s.l1b_y_used, g + 1)
                    sp.dma_start(y_buf[:, q, :, :].rearrange("p u f -> p (u f)"),
                                 y_stash[bass.ds(g, 1), :, :].rearrange("a p f -> (a p) f")).then_inc(y_in[q], 16)

            store_tab(att_tab, D2, CHUNKS)
            got, h_out = [s.l2_got0, s.l2_got1], [s.h_stored0, s.h_stored1]
            with sp.Fori(0, ITER) as i:
                for b in range(2):
                    sp.wait_ge(got[b], i * (G * 16) + G * 16)
                    sp.dma_start(h_stash[bass.ds(i * 2 + b, 1), :, :].rearrange("a p f -> (a p) f"),
                                 rows[:, b, :, :].rearrange("p u f -> p (u f)")).then_inc(h_out[b], 16)
                    sp.wait_ge(h_out[b], i * 16 + 16)
                    sp.sem_inc(s.passed, 1)
                    sp.wait_ge(s.l2_scores, i * 2 + b + 1)
                    sp.sem_inc(s.l2_rows_used, 1)
            with sp.Fori(0, ITER // 2) as i:
                for q in range(4):
                    g = i * 4 + q
                    sp.wait_ge(s.l2b_rows_used, g + 1)
                    sp.dma_start(l2b_h[q // 2][:, q % 2, :, :].rearrange("p u f -> p (u f)"),
                                 h_stash[bass.ds(g, 1), :, :].rearrange("a p f -> (a p) f")).then_inc(h_in[q], 16)

            for k, (ready, stored) in enumerate(((s.gcn_in0, s.gcn_stored0), (s.gcn_in1, s.gcn_stored1))):
                sp.wait_ge(ready, 1)
                sp.dma_start(gcn_tab[k].rearrange("(p w) f -> p w f", p=P), tab_d).then_inc(stored, 16)

            for k, (start, end) in enumerate(OUT_PARTS):
                full = min(end, FULL_W)
                sp.wait_ge(s.result_ready, k + 1)
                sp.dma_start(out[start * P:full * P, :].rearrange("(w p) f -> p w f", p=P), x_n[:, start:full, :]).then_inc(s.result_stored, 16)
            sp.dma_start(out[FULL_W * P:N, :], x_n[0:TAIL_N, FULL_W, :]).then_inc(s.result_stored, 16)
            sp.wait_ge(s.result_stored, 16 * len(OUT_PARTS) + 16)

        @block.gpsimd
        def _(pool):
            pool.memset(zeros[:, :], 0.0).then_inc(s.zeros_made, 1)
            pool.memset(src_t, 0).then_inc(s.tiles_clean, 1)
            pool.memset(dst_t, NOWHERE).then_inc(s.tiles_clean, 1)
            pool.iota(step_i, [[1, S]], base=0, channel_multiplier=0).then_inc(s.iotas_made, 1)
            pool.iota(scr_i[:, 0:TB], [[P, TB]], base=0, channel_multiplier=1).then_inc(s.iotas_made, 1)
            pool.memset(x_n[:, FULL_W, :], 0.0).then_inc(s.x_clean, 1)

            pool.wait_ge(s.zeros_made, 1)
            runs = SROWS * D1 // P // ZEROS
            for k in range(LANES):
                pool.dma_start(lane_tab[k].rearrange("(p r) f -> p (r f)", p=P).rearrange("p (a z) -> p a z", z=ZEROS),
                               bc(zeros[:, :].unsqueeze(1), [P, runs, ZEROS])).then_inc(fill[k], 16)
            with pool.Fori(0, ITER) as i:
                for b in range(2):
                    g = i * 2 + b
                    pool.wait_ge(s.l0_sums_copied, g + 3)
                    pool.sem_inc(s.passed, 1)
                    for u in range(G):
                        k = u % LANES
                        pool.wait_ge(fill[k], i * 64 + (16 + 32 * b + 16 * (u // LANES)))
                        pool.sem_inc(s.l0_landed if u == LANES - 1 else s.passed, 1)
                        pool.indirect_dma_start(lane_tab[k][:, :], bass.IndirectOffsetOnAxis(ap=idx[:, b, u:u + 1], axis=0),
                                                rows[:, b, u, 0:D1], None, compute_op=ALU.add).then_inc(fill[k], 16)
            for k in range(LANES):
                pool.wait_ge(fill[k], 16 + 64 * ITER)
            pool.sem_inc(s.lanes_done, 1)

            def gathers(table, n, to, idx_ready, turn, free, got):
                with pool.Fori(0, ITER) as i:
                    for b in range(2):
                        pool.wait_ge(idx_ready, i * 2 + b + 1)
                        pool.sem_inc(turn, 1)
                        pool.wait_ge(free, i * 2 + b + 1)
                        pool.sem_inc(turn, 1)
                        for u in range(G):
                            pool.indirect_dma_start(to[:, b, u, 0:n], None, table[:, :],
                                                    bass.IndirectOffsetOnAxis(ap=idx[:, b, u:u + 1], axis=0)).then_inc(got[b], 16)

            pool.wait_ge(s.tab_stored, CHUNKS * 16)
            gathers(src_tab, 2 * D, buf_b, s.l1_indices, s.passed, s.l1_rows_used, [s.l1_got0, s.l1_got1])
            pool.wait_ge(s.bn_ready, 1)
            pool.sem_inc(s.l1b_y_used, 4)
            with pool.Fori(0, ITER // 2) as i:
                for q in range(4):
                    g = i * 4 + q
                    z = z_buf[:, q, :, :]
                    pool.wait_ge(y_in[q], i * 16 + 16)
                    pool.sem_inc(s.passed, 1)
                    pool.wait_ge(s.l1b_slot_free, g + 1)
                    pool.tensor_tensor(z, y_buf[:, q, :, :], bc(bn[:, 0:1, :], [P, G, 2 * D]), ALU.mult).then_inc(s.l1b_normed, 1)
                    pool.wait_ge(s.l1b_normed, g * 2 + 1)
                    pool.sem_inc(s.l1b_y_used, 1)
                    pool.tensor_tensor(z, z, bc(bn[:, 1:2, :], [P, G, 2 * D]), ALU.add).then_inc(s.l1b_normed, 1)
            pool.wait_ge(s.tab_stored, 2 * CHUNKS * 16)
            gathers(att_tab, D2, rows, s.l2_indices, s.passed, s.l2_rows_used, [s.l2_got0, s.l2_got1])
            pool.wait_ge(s.gcn_stored0, 16)
            gathers(gcn_tab[0], D, rows, s.g0_indices, s.passed, s.g0_rows_used, [s.g0_got0, s.g0_got1])
            pool.wait_ge(s.gcn_stored1, 16)
            gathers(gcn_tab[1], D, rows, s.g1_indices, s.passed, s.g1_rows_used, [s.g1_got0, s.g1_got1])

        @block.scalar
        def _(act):
            act.wait_ge(s.weights_loaded, 16 * 9)
            act.wait_ge(s.gate_lin, 1)
            act.activation(gate_t, gate_t, ACT.Sigmoid, bias=be_c[:, 0:1]).then_inc(s.gate_done, 1)
            act.wait_ge(s.wt_made, 1)
            act.activation(wt[:, 0:7 * D], ps[:, 6, 0:7 * D], ACT.Copy).then_inc(s.wt_copied, 1)
            act.activation(wt[0:D, TA:TA + D], wsm[0:D, WA:WA + D], ACT.Copy).then_inc(s.wt_copied, 1)
            act.activation(xt[1][0:D, 0:D], ps[0:D, 7, 0:D], ACT.Copy).then_inc(s.wt_copied, 1)
            act.wait_ge(s.wa_made, 1)
            act.activation(wt[0:D, TA + D:TA + D2], ps[0:D, 7, D:D2], ACT.Copy).then_inc(s.wt_copied, 1)

            def node_copies(base, view):
                def x_copy(c, k):
                    act.activation(xs[k], view[:, bass.ds(c * WPC, WPC), :], ACT.Copy).then_inc(s.node_xs, 1)

                def xt_copy(c, k):
                    act.wait_ge(s.node_xt, c + (base + 1))
                    act.wait_ge(s.node_products, c + (base + 1))
                    act.activation(xt[k], ps[0:D, 2 * k:2 * k + 2, :].rearrange("p a b -> p (a b)")[:, 0:WPC * P],
                                   ACT.Copy).then_inc(s.node_xt_copied, 1)

                for k in range(2):
                    x_copy(k, k)
                with act.Fori(0, CHUNKS // 2 - 1) as i:
                    for k in range(2):
                        xt_copy(i * 2 + k, k)
                        x_copy(i * 2 + (k + 2), k)
                for k in range(2):
                    xt_copy(CHUNKS - 2 + k, k)

            act.wait_ge(s.node_in, 1)
            node_copies(0, x_n)

            def l0_gates_copy(g, b):
                act.wait_ge(s.l0_gates, g + 1)
                act.activation(buf_d[:, b, :, :], regions(2 * b, P), ACT.Copy).then_inc(s.l0_gates_copied, 1)

            def l0_rows_copy(g, b):
                act.wait_ge(s.l0_sums, g + 1)
                act.wait_ge(s.l0_rows_known, g + 1)
                act.wait_ge(s.l0_landed, g + 1)
                act.activation(idx[:, b, :], idxf[:, b, :], ACT.Copy)
                act.activation(rows[:, b, :, 0:D1], regions(4 + 2 * b, D1), ACT.Copy).then_inc(s.l0_sums_copied, 1)

            l0_gates_copy(0, 0)
            with act.Fori(0, ITER - 1) as i:
                for b in range(2):
                    g = i * 2 + (b + 1)
                    l0_gates_copy(g, 1 - b)
                    l0_rows_copy(g - 1, b)
            l0_gates_copy(2 * ITER - 1, 1)
            l0_rows_copy(2 * ITER - 2, 0)
            l0_rows_copy(2 * ITER - 1, 1)

            def std(n):
                act.wait_ge(s.norm_var, n)
                act.activation(col_b[:, :], col_a[:, :], ACT.Sqrt).then_inc(s.norm_std, 1)

            def indices(ready, got):
                for b in range(2):
                    act.activation(idx[:, b, :], src_s[:, b * G:b * G + G], ACT.Copy).then_inc(ready, 1)

            def next_indices(i, b, ready, got):
                act.wait_ge(got[b], i * (G * 16) + G * 16)
                act.activation(idx[:, b, :], src_s[:, bass.ds(i * PAIR + (PAIR + b * G), G)], ACT.Copy).then_inc(ready, 1)

            std(1)
            act.wait_ge(s.node_in, 3)
            node_copies(CHUNKS, x_n)
            got = [s.l1_got0, s.l1_got1]
            indices(s.l1_indices, got)
            def l1_copies(g, b):
                act.wait_ge(s.l1_transposed, g + 1)
                act.activation(buf_d[:, b, :, :].rearrange("p u f -> p (u f)"), ps[:, b, :].bitcast(BF16), ACT.Copy)
                act.activation(buf_a[:, b, 0:4, :].rearrange("p u f -> p (u f)"), ps[:, 2 + b, :], ACT.Copy).then_inc(s.l1_trans_copied, 1)

            for b in range(2):
                l1_copies(b, b)
            with act.Fori(0, ITER) as i:
                for b in range(2):
                    l1_copies(i * 2 + (b + 2), b)
                for b in range(2):
                    next_indices(i, b, s.l1_indices, got)
                    act.wait_ge(s.l1_masked, i * 2 + b + 1)
                    act.wait_ge(s.l1_sq_added, i * 2 + b + 1)
                    act.activation(sq[:, b, :, :], yv[:, b, :, :], ACT.Square).then_inc(s.l1_squared, 1)
            act.wait_ge(s.bn_var, 1)
            act.activation(bn_col[:, 7:8], bn_col[:, 6:7], ACT.Sqrt).then_inc(s.bn_made, 1)
            act.preload_act_table_set("natural_log_exp_and_others")
            with act.Fori(0, ITER) as i:
                for b in range(2):
                    m = buf_b[:, b, :, :]
                    act.wait_ge(s.l1b_clamped, i * 2 + b + 1)
                    act.activation(m, m, ACT.Exp).then_inc(s.l1b_act, 1)
                    act.wait_ge(s.l1b_act, i * 6 + (3 * b + 1))
                    act.activation(m, m, ACT.Ln, bias=1.0).then_inc(s.l1b_act, 1)
                    act.wait_ge(s.l1b_act, i * 6 + (3 * b + 2))
                    act.activation(m[:, :, D:2 * D], m[:, :, D:2 * D], ACT.Exp, scale=-1.0).then_inc(s.l1b_act, 1)
            std(2)
            act.wait_ge(s.node_in, 5)
            node_copies(2 * CHUNKS, x_n)
            act.wait_ge(s.l1_indices, 2 * ITER + 2)
            got = [s.l2_got0, s.l2_got1]
            indices(s.l2_indices, got)
            with act.Fori(0, ITER) as i:
                for b in range(2):
                    next_indices(i, b, s.l2_indices, got)

            def l2b_copies(i, half):
                for b in range(2):
                    act.wait_ge(s.l2b_transposed, i * 2 + (b + 1))
                    act.activation(ot_b[:, b, :, :].rearrange("p u f -> p (u f)"), ps[:, b, :].bitcast(BF16), ACT.Copy).then_inc(s.l2b_trans_copied, 1)

            def l2b_hots(i, half, later):
                for b in range(2):
                    if later:
                        act.wait_ge(s.l2b_sums, i * 2 + (b - 1))
                    act.activation(l2b_hot[half][:, b, :, :], ob4[:, 2 * half + b, :, :], ACT.Copy).then_inc(s.l2b_hot_copied, 1)

            def l2b_turn(i, half, later):
                act.wait_ge(s.l2b_args, i + 1)
                act.activation(ex[:, :, :], tmp_c[:, 2:4, :], ACT.Exp).then_inc(s.l2b_weights, 1)
                l2b_copies(i + 1, 1 - half)
                l2b_hots(i + 1, 1 - half, later)

            act.preload_act_table_set("natural_log_exp_and_others")
            l2b_copies(0, 0)
            l2b_hots(0, 0, False)
            l2b_turn(0, 0, False)
            with act.Fori(0, ITER // 2 - 1) as i:
                for half in (1, 0):
                    l2b_turn(i * 2 + (2 - half), half, True)
            act.wait_ge(s.l2b_args, ITER)
            act.activation(ex[:, :, :], tmp_c[:, 2:4, :], ACT.Exp).then_inc(s.l2b_weights, 1)
            act.wait_ge(s.elu_in, 1)
            act.activation(scratch, scratch, ACT.Exp).then_inc(s.elu_out, 1)
            std(3)
            std(4)
            act.wait_ge(s.l2_indices, 2 * ITER + 2)
            got = [s.g0_got0, s.g0_got1]
            indices(s.g0_indices, got)
            with act.Fori(0, ITER) as i:
                for b in range(2):
                    next_indices(i, b, s.g0_indices, got)
            act.wait_ge(s.node_in, 6)
            node_copies(3 * CHUNKS, tab_d)
            act.wait_ge(s.g0_indices, 2 * ITER + 2)
            got = [s.g1_got0, s.g1_got1]
            indices(s.g1_indices, got)
            with act.Fori(0, ITER) as i:
                for b in range(2):
                    next_indices(i, b, s.g1_indices, got)
            act.wait_ge(s.node_in, 7)
            node_copies(4 * CHUNKS, tab_d)
            std(5)

        @block.tensor
        def _(pe):
            pe.wait_ge(s.consts_made, 1)
            pe.wait_ge(s.key_ready, 1)
            for b in range(TB):
                last = pe.matmul(region(b, P), bc(key[:, b:b + 1], [P, P]), ident[:, :], start=True, stop=True)
            last.then_inc(s.key_rows, 1)
            pe.wait_ge(s.weights_loaded, 16 * 9)
            i64 = ident[0:D, 0:D]
            wps = ps[:, 6, :]
            for at, frm in ((TN, WN), (TS, WC + D), (TS + D, WF + D), (TS + 2 * D, WC), (TS + 3 * D, WF),
                            (TE, WC + 2 * D), (TE + D, WF + 2 * D)):
                pe.matmul(wps[0:D, at:at + D], wsm[0:D, frm:frm + D], i64, start=True, stop=True)
            for at, frm in ((TN, WN), (TS, WC + D), (TS + D, WF + D), (TS + 2 * D, WC), (TS + 3 * D, WF),
                            (TE, WC + 2 * D), (TE + D, WF + 2 * D)):
                pe.matmul(wps[D:P, at:at + D], wsm[0:D, frm:frm + D], i64, start=True, stop=True)
            pe.matmul(ps[0:D, 7, 0:D], wsm[0:D, WA:WA + D], i64, start=True, stop=True).then_inc(s.wt_made, 1)
            pe.wait_ge(s.wt_copied, 3)
            pe.matmul(ps[0:D, 7, D:D2], xt[1][0:D, 0:D], a2[:, :], start=True, stop=True).then_inc(s.wa_made, 1)
            pe.wait_ge(s.wt_copied, 4)
            pe.wait_ge(s.tile_cols, 1)
            for b in range(SB):
                last = pe.matmul(region(16 + b, P), bc(t_col[:, b:b + 1], [P, P]), ident[:, :], start=True, stop=True)
            last.then_inc(s.tile_rows, 1)
            pe.wait_ge(s.places_made, 1)
            pe.wait_ge(s.gate_done, 1)
            for c in range(CHUNKS_S):
                blocks = blocks_of(c)
                pe.wait_ge(s.selected, c + 1)
                for k, t in enumerate((src_f, dst_f, gate_t)):
                    for n, b in enumerate(blocks):
                        last = pe.matmul(ps[:, k, 0:CH], t[:, b, :], sel[:, n, :], start=(n == 0), stop=(n == len(blocks) - 1))
                last.then_inc(s.select_done, 1)

            pe.sem_inc(s.node_products, 2)

            def node_product(base, rhs, n, per_bank):
                def transposes(c, k):
                    pe.wait_ge(s.node_xs, c + (base + 1))
                    for w in range(WPC):
                        last = pe.matmul(region(8 * k + w, P)[0:D, :], xs[k][:, w, :], ident[:, :], start=True, stop=True)
                    last.then_inc(s.node_xt, 1)

                def products(c, k):
                    pe.wait_ge(s.node_xt_copied, c + (base + 1))
                    pe.wait_ge(s.node_evacuated, c + (base + (1 if per_bank == 4 else 2)))
                    bank = 4 + (2 * k if per_bank == 4 else 0)
                    for w in range(WPC):
                        at = (w % per_bank) * (512 // per_bank)
                        last = pe.matmul(ps[:, bank + w // per_bank, at:at + n], xt[k][:, w * P:w * P + P], rhs, start=True, stop=True)
                    last.then_inc(s.node_products, 1)

                transposes(0, 0)
                with pe.Fori(0, CHUNKS // 2 - 1) as i:
                    for k in range(2):
                        transposes(i * 2 + (k + 1), 1 - k)
                        products(i * 2 + k, k)
                transposes(CHUNKS - 1, 1)
                for k in range(2):
                    products(CHUNKS - 2 + k, k)

            pe.wait_ge(s.node_in, 1)
            pe.sem_inc(s.l0_slot_free, 2)
            node_product(0, wt[0:D, TN:TN + D], D, 4)

            pe.wait_ge(s.node_in, 2)
            pe.sem_inc(s.l0_gates_copied, 2)

            def l0_rows(g, b):
                pe.wait_ge(s.l0_sources, g + 1)
                pe.wait_ge(s.l0_gates_copied, g + 1)
                for u in range(G):
                    last = pe.matmul(region(8 * b + u, P), bc(srcg[:, b, u:u + 1], [P, P]), ident[:, :], start=True, stop=True)
                last.then_inc(s.l0_source_rows, 1)

            def l0_gates(g, b):
                pe.wait_ge(s.l0_gated_hot, g + 1)
                pe.wait_ge(s.l0_same, g + 1)
                for u in range(G):
                    last = pe.matmul(region(8 * b + u, P), buf_a[:, b, u, :], buf_b[:, b, u, :], start=True, stop=True)
                last.then_inc(s.l0_gates, 1)

            def l0_sums(g, b):
                ws = load8(mybir.EngineType.PE, win_s, g, W - 1)
                pe.wait_ge(s.l0_gates_copied, g + 3)
                pe.wait_ge(s.l0_sums_copied, g + 1)
                for u in range(G):
                    o = 16 + 8 * b + u
                    pe.matmul(region(o, D1)[:, D:D1], buf_b[:, b, u, :], step_col(valid_s, g, u), start=True, stop=True)
                    last = pe.matmul(region(o, D), buf_d[:, b, u, :], window(tab, ws[u], D), start=True, stop=True)
                last.then_inc(s.l0_sums, 1)
                pe.sem_inc(s.l0_slot_free, 1)

            def l0_next(g, b):
                l0_rows(g, b)
                l0_sums(g - 1, 1 - b)
                l0_gates(g, b)

            l0_rows(0, 0)
            l0_gates(0, 0)
            with pe.Fori(0, ITER - 1) as i:
                for b in range(2):
                    l0_next(i * 2 + (b + 1), 1 - b)
            l0_next(2 * ITER - 1, 1)
            l0_sums(2 * ITER - 1, 1)

            pe.wait_ge(s.node_in, 3)
            node_product(CHUNKS, wt[0:D, TS:TS + 4 * D], 4 * D, 2)

            pe.wait_ge(s.node_in, 4)

            def l1_transposes(turn, q, g):
                b = q % 2
                pe.wait_ge(e_in[q], turn * (G * 16) + G * 16)
                pe.wait_ge(s.l1_hot, g + 1)
                ob_ps = ps[:, b, :].bitcast(BF16)
                for u in range(G):
                    pe.transpose(ob_ps[:, u * P:u * P + P], ob[:, b, u, :], ident_b[:, :])
                for u in range(G // 2):
                    last = pe.transpose(ps[:, 2 + b, u * P:u * P + P],
                                        ea_s[:, q, 2 * u:2 * u + 2, :].rearrange("p a f -> p (a f)"), ident[:, :])
                last.then_inc(s.l1_transposed, 1)

            for b in range(2):
                l1_transposes(0, b, b)
            with pe.Fori(0, ITER // 2) as i:
                for half in range(2):
                    for b in range(2):
                        g = i * 4 + (2 * half + b)
                        ws = load8(mybir.EngineType.PE, win_s, g, W - 1)
                        pe.wait_ge(s.l1_trans_copied, g + 1)
                        pe.wait_ge(s.l1_bank_free, g + 1)
                        for u in range(G):
                            h = D * (u % 2)
                            o = region(16 + 8 * b + 4 * (u % 2) + u // 2, P)
                            pe.matmul(o, buf_d[:, b, u, :], window(tab, ws[u], P), start=True, stop=False)
                            last = pe.matmul(o, buf_a[h:h + D, b, u // 2, :], wt[h:h + D, TE:TE + 2 * D], start=False, stop=True)
                        last.then_inc(s.l1_products, 1)
                    for b in range(2):
                        l1_transposes(i + half, 2 * (1 - half) + b, i * 4 + (2 * half + b + 2))
            pe.wait_ge(s.l1_sq_added, 2 * ITER + 2)
            for k in range(2):
                for u in range(G):
                    last = pe.matmul(ps[:, 4 + k, 0:1], stat[:, k, u, :], ones[:, 0:1], start=(u == 0), stop=(u == G - 1))
            last.then_inc(s.stat_done, 1)
            pe.wait_ge(s.bn_made, 2)
            for k in range(2):
                last = pe.matmul(ps[:, 6, 2 * D * k:2 * D * k + 2 * D], bc(bn_col[:, k:k + 1], [P, P]), ident[:, :], start=True, stop=True)
            last.then_inc(s.bn_spread, 1)

            def add_group(left, right, g, b, bank, n):
                for c in range(2):
                    pe.matmul(ps[:, bank + c, :].rearrange("p (k f) -> p k f", f=P)[:, :, 0:n], zero_b[:, :],
                              bc(ident_b[:, 0:n].unsqueeze(1), [P, 4, n]), start=True, stop=False, skip_group_check=True)
                rel = load8(mybir.EngineType.PE, rel_s, g, (G - 1) * P)
                for u in range(G):
                    last = pe.matmul(ps_flat[:, bass.ds(rel[u] + bank * 512, n)], left[:, b, u, :], right[:, b, u, 0:n],
                                     start=False, stop=True, skip_group_check=True)
                return last

            def aggregate(left, right, n, left_ready, right_ready, free, done):
                with pe.Fori(0, ITER) as i:
                    for b in range(2):
                        g = i * 2 + b
                        pe.wait_ge(left_ready, g + 1)
                        pe.wait_ge(right_ready[b], i * (G * 16) + G * 16)
                        pe.wait_ge(free, g + 1)
                        add_group(left, right, g, b, 2 * b, n).then_inc(done, 1)

            with pe.Fori(0, ITER // 2) as i:
                for q in range(4):
                    g = i * 4 + q
                    pe.wait_ge(s.l1b_hot, g + 1)
                    pe.wait_ge(s.l1b_messages, g + 1)
                    pe.wait_ge(s.l1b_bank_free, g + 1)
                    add_group(lb_hot[q // 2], lb_rows[q // 2], g, q % 2, 2 * q, D1).then_inc(s.l1b_sums, 1)

            pe.wait_ge(s.node_in, 5)
            node_product(2 * CHUNKS, wt[0:D, TA:TA + D2], D2, 4)
            got = [s.l2_got0, s.l2_got1]
            with pe.Fori(0, ITER) as i:
                for b in range(2):
                    g = i * 2 + b
                    pe.wait_ge(got[b], i * (G * 16) + G * 16)
                    pe.wait_ge(s.l2_not_hot, g + 1)
                    pe.wait_ge(s.l2_bank_free, g + 1)
                    for u in range(G):
                        pe.matmul(region(8 * b + u, P), buf_a[:, b, u, :], ident[:, :], start=True, stop=False)
                        last = pe.matmul(region(8 * b + u, P), bc(rows[:, b, u, D1:D2], [P, P]), ident[:, :], start=False, stop=True)
                    last.then_inc(s.l2_scores, 1)
            pe.wait_ge(s.max_done, 1)

            def l2b_transposes(g, q):
                pe.wait_ge(s.l2b_hot, g + 1)
                for u in range(G):
                    last = pe.transpose(ps[:, q % 2, :].bitcast(BF16)[:, u * P:u * P + P], ob4[:, q, u, :], ident_b[:, :])
                last.then_inc(s.l2b_transposed, 1)

            def l2b_targets(g, b):
                ws = load8(mybir.EngineType.PE, win_s, g, W - 1)
                pe.wait_ge(s.l2b_trans_copied, g + 1)
                for u in range(G):
                    last = pe.matmul(ps[:, 2, 6 * (b * G + u):6 * (b * G + u) + 6], ot_b[:, b, u, :], window(sums_b, ws[u], 6), start=True, stop=True)
                last.then_inc(s.l2b_targets, 1)

            def l2b_sums(g, half, b):
                pe.wait_ge(s.l2b_hot_copied, g + 1)
                pe.wait_ge(s.l2b_weighted, g + 1)
                pe.wait_ge(s.l2b_bank_free, g + 1)
                add_group(l2b_hot[half], l2b_rows[half], g, b, 4 + 2 * b, D1).then_inc(s.l2b_sums, 1)

            def l2b_turn(i, half):
                for b in range(2):
                    l2b_transposes(i * 2 + (b + 2), 2 * (1 - half) + b)
                l2b_sums(i * 2, half, 0)
                for b in range(2):
                    l2b_targets(i * 2 + (b + 2), b)
                l2b_sums(i * 2 + 1, half, 1)

            for b in range(2):
                l2b_transposes(b, b)
            for b in range(2):
                l2b_targets(b, b)
            with pe.Fori(0, ITER // 2 - 1) as i:
                for half in range(2):
                    l2b_turn(i * 2 + half, half)
            l2b_turn(ITER - 2, 0)
            for b in range(2):
                l2b_sums(2 * ITER - 2 + b, 1, b)
            aggregate(buf_a, rows, D, s.g0_hot, [s.g0_got0, s.g0_got1], s.g0_bank_free, s.g0_sums)
            pe.wait_ge(s.node_in, 6)
            node_product(3 * CHUNKS, w12[:, 0, :], D, 4)
            aggregate(buf_a, rows, D, s.g1_hot, [s.g1_got0, s.g1_got1], s.g1_bank_free, s.g1_sums)
            pe.wait_ge(s.node_in, 7)
            node_product(4 * CHUNKS, w12[:, 1, :], D, 4)

        @block.vector
        def _(dve):
            count = [0]

            def link(ins):
                count[0] += 1
                ins.then_inc(s.dve_done, 1)
                dve.wait_ge(s.dve_done, count[0])

            dve.wait_ge(s.iotas_made, 2)
            link(dve.tensor_copy(step_f, step_i))
            link(dve.tensor_copy(ids[:, :], scr_i[:, 0:TB]))
            link(dve.tensor_copy(iota[:, :], step_f[:, 0:P]))
            link(dve.tensor_scalar(ident[:, :], iota[:, :], ids[:, 0:1], None, ALU.is_equal))
            link(dve.tensor_copy(ident_b[:, :], ident[:, :]))
            link(dve.tensor_scalar(below[:, :], iota[:, :], ids[:, 0:1], None, ALU.is_lt))
            link(dve.tensor_scalar(trash[:, :], ids[:, 0:1], float(TRASH), None, ALU.add))
            link(dve.memset(ones[:, :], 1.0))
            link(dve.memset(zero_b[:, :], 0.0))
            for t, v in ((src_s, 0.0), (dst_s, -1.0), (gate_s, 0.0), (valid_s, 0.0)):
                link(dve.memset(t[:, S:SPAD], v))
            link(dve.memset(win_s[:, S:SPAD], 0))
            link(dve.memset(row_s[:, S:SPAD], 0))
            link(dve.memset(rel_s[:, S:SPAD], 0))
            dve.sem_inc(s.consts_made, 1)
            dve.wait_ge(s.tiles_loaded, 96)
            link(dve.tensor_copy(src_f, src_t))
            link(dve.tensor_scalar(src_t, src_t, P.bit_length() - 1, None, ALU.arith_shift_right))
            window_f = junk.rearrange("p (b e) -> p b e", e=P)
            link(dve.tensor_copy(window_f, src_t))
            link(dve.tensor_scalar(src_f, src_f, float(W), None, ALU.mult))
            link(dve.scalar_tensor_tensor(src_f, window_f, float(1 - P * W), src_f, ALU.mult, ALU.add))
            link(dve.tensor_copy(dst_f, dst_t))
            link(dve.tensor_reduce(last_i[:, :], dst_t, AX.X, ALU.max))
            link(dve.tensor_scalar(last_i[:, :], last_i[:, :], 7, None, ALU.arith_shift_right))
            link(dve.tensor_copy(key[:, :], last_i[:, :]))
            dve.tensor_tensor(key[:, :], key[:, :], ids[:, :], ALU.add).then_inc(s.key_ready, 1)
            dve.wait_ge(s.key_rows, 1)
            key_row = ps[:, 0:4, :].rearrange("p a b -> p (a b)")[:, 0:TB * P]
            for c in range(SB):
                link(dve.tensor_scalar(junk, key_row, ids[:, c:c + 1], None, ALU.is_lt, ALU.add, accum_out=t_col[:, c:c + 1]))
            dve.sem_inc(s.tile_cols, 1)
            dve.wait_ge(s.weights_loaded, 16 * 9)

            def gate_block(b, slot):
                v = x_flat[:, slot * EB:(slot + 1) * EB].rearrange("p (e k) -> p e k", k=K16)
                link(dve.tensor_tensor(v, v, bc(we_bc[:, :].unsqueeze(1), [P, P, K16]), ALU.mult))
                link(dve.tensor_reduce(gate_t[:, b, :], v, AX.X, ALU.add))

            dve.wait_ge(s.ea_loaded0, 16 * 6)
            for b in range(6):
                gate_block(b, b)
                if b % 3 == 2:
                    dve.sem_inc(s.ea_clean, 1)
            dve.wait_ge(s.ea_loaded1, 16 * 3)
            for b in range(3):
                gate_block(6 + b, b)
            link(dve.memset(x_flat[:, 0:EB], 0.0))
            dve.sem_inc(s.ea_clean, 1)
            dve.wait_ge(s.ea_loaded2, 16 * 3)
            for b in range(3, 6):
                gate_block(6 + b, b)
            dve.wait_ge(s.ea_loaded3, 16 * 2)
            gate_block(12, 0)
            dve.sem_inc(s.gate_lin, 1)
            dve.wait_ge(s.tile_rows, 1)
            trow_ps = ps[:, 4:8, :].rearrange("p a b -> p (a b)")[:, 0:S]
            link(dve.tensor_copy(t_row, trow_ps))
            link(dve.tensor_tensor(w_row, step_f, t_row, ALU.subtract))
            link(dve.tensor_scalar(win_s[:, 0:S], w_row[0:1, :], float(W - 1), None, ALU.min))
            link(dve.tensor_scalar(row_s[:, 0:S], t_row[32:33, :], float(P), float(E - P), ALU.mult, ALU.min))
            link(dve.tensor_scalar(junk, w_row, float(W - 1), float(P), ALU.min, ALU.mult))
            w_grp = junk.rearrange("p (a u) -> p a u", u=G)
            link(dve.tensor_tensor(rel_s[:, 0:S].rearrange("p (a u) -> p a u", u=G), w_grp[64:65],
                                   bc(w_grp[64:65, :, 0:1], [1, S // G, G]), ALU.subtract))
            dve.sem_inc(s.places_made, 1)
            dve.sem_inc(s.select_done, 1)
            for c in range(CHUNKS_S):
                at = slice(c * CH, (c + 1) * CH)
                for n, b in enumerate(blocks_of(c)):
                    last = dve.tensor_scalar(sel[:, n, :], t_row[:, at], ids[:, b:b + 1], None, ALU.is_equal)
                last.then_inc(s.selected, 1)
                dve.wait_ge(s.select_done, c + 2)
                dve.tensor_copy(src_s[:, at], ps[:, 0, 0:CH])
                dve.scalar_tensor_tensor(dst_s[:, at], w_row[:, at], -float(P), ps[:, 1, 0:CH], ALU.mult, ALU.add)
                dve.tensor_copy(gate_s[:, at], ps[:, 2, 0:CH]).then_inc(s.steps_made, 1)
                dve.wait_ge(s.steps_made, c + 1)
            link(dve.tensor_scalar(valid_s[:, 0:S], dst_s[:, 0:S], 0.0, None, ALU.is_ge))
            link(dve.scalar_tensor_tensor(valid_s[:, 0:S], dst_s[:, 0:S], float(P), valid_s[:, 0:S], ALU.is_lt, ALU.mult))
            dve.wait_ge(s.bias_loaded, 16 * 9)
            dve.wait_ge(s.x_loaded, 32)
            dve.wait_ge(s.wt_copied, 4)
            dve.sem_inc(s.node_in, 1)

            def products(per_bank, k0, k1, k):
                n = 512 // per_bank
                b0 = 4 + (2 * k if per_bank == 4 else 0) + k0 // per_bank
                return ps[:, b0:b0 + 1, 0:(k1 - k0) * n].rearrange("p a (w f) -> p (a w) f", f=n)

            def chunks(base, evacuate):
                with dve.Fori(0, CHUNKS // 2) as i:
                    for k in range(2):
                        dve.wait_ge(s.node_products, i * 2 + (base + k + 3))
                        evacuate(i * 2 + k, k)
                dve.wait_ge(s.node_evacuated, base + CHUNKS + 2)

            def to_tab0(c, k):
                for k0, k1 in ((0, 4), (4, 7)):
                    last = dve.tensor_tensor(tab[:, bass.ds(c * WPC + k0, k1 - k0), 0:D], products(4, k0, k1, k)[:, :, 0:D],
                                             bc(bias0[:, :].unsqueeze(1), [P, k1 - k0, D]), ALU.add)
                last.then_inc(s.node_evacuated, 1)

            dve.sem_inc(s.node_evacuated, 2)
            chunks(0, to_tab0)
            dve.sem_inc(s.node_in, 1)

            dve.sem_inc(s.l0_sums_copied, 2)
            dve.sem_inc(s.l0_landed, 1)
            KL0 = 4
            with dve.Fori(0, ITER) as i:
                for b in range(2):
                    g = i * 2 + b
                    dve.wait_ge(s.l0_slot_free, g + 1)
                    dve.tensor_copy(srcg[:, b, :], step_slice(src_s, g)).then_inc(s.l0_sources, 1)
                    for u in range(G):
                        last = dve.tensor_scalar(buf_a[:, b, u, :], iota[:, :], step_col(dst_s, g, u), step_col(gate_s, g, u),
                                                 ALU.is_equal, ALU.mult)
                    last.then_inc(s.l0_gated_hot, 1)
                    dve.wait_ge(s.l0_source_rows, g + 1)
                    dve.tensor_tensor(buf_b[:, b, :, :], regions(2 * b, P), bc(srcg[:, b, :].unsqueeze(2), [P, G, P]),
                                      ALU.is_equal).then_inc(s.l0_same, 1)
                    dve.wait_ge(s.l0_same, g + 1)
                    k = 0

                    def chain(ins):
                        nonlocal k
                        k += 1
                        ins.then_inc(s.l0_chain, 1)
                        dve.wait_ge(s.l0_chain, i * (2 * KL0) + (b * KL0 + k))
                    chain(dve.tensor_tensor(buf_c[:, b, :, :], buf_b[:, b, :, :], bc(below[:, :].unsqueeze(1), [P, G, P]), ALU.mult))
                    chain(dve.tensor_reduce(dup[:, b, :], buf_c[:, b, :, :], AX.X, ALU.max))
                    chain(dve.tensor_scalar(tmp_c[:, b, :], srcg[:, b, :], -1.0, trash[:, 0:1], ALU.mult, ALU.add))
                    chain(dve.tensor_tensor(tmp_c[:, b, :], tmp_c[:, b, :], dup[:, b, :], ALU.mult))
                    dve.wait_ge(s.l0_sums_copied, g + 1)
                    dve.tensor_tensor(idxf[:, b, :], tmp_c[:, b, :], srcg[:, b, :], ALU.add).then_inc(s.l0_rows_known, 1)
                    dve.wait_ge(s.l0_rows_known, g + 1)
                    assert k == KL0

            def norm(t, n, ready=None):
                link(dve.tensor_reduce(col_a[:, :], t, AX.X, ALU.add))
                link(dve.tensor_scalar(col_a[:, :], col_a[:, :], 1.0 / D, None, ALU.mult))
                link(dve.tensor_tensor(t, t, bc(col_a[:, :].unsqueeze(2), [P, W, D]), ALU.subtract))
                link(dve.tensor_tensor(scratch, t, t, ALU.mult))
                link(dve.tensor_reduce(col_a[:, :], scratch, AX.X, ALU.add))
                dve.tensor_scalar(col_a[:, :], col_a[:, :], 1.0 / D, EPS, ALU.mult, ALU.add).then_inc(s.norm_var, 1)
                dve.wait_ge(s.norm_std, n)
                link(dve.reciprocal(col_b[:, :], col_b[:, :]))
                if ready is None:
                    link(dve.tensor_tensor(x_n[:, :, :], t, bc(col_b[:, :].unsqueeze(2), [P, W, D]), ALU.mult))
                else:
                    for start, end in OUT_PARTS:
                        dve.tensor_tensor(x_n[:, start:end, :], t[:, start:end, :],
                                          bc(col_b[:, start:end].unsqueeze(2), [P, end - start, D]), ALU.mult).then_inc(ready, 1)

            tab_l = tab_flat[:, 0:W * D1].rearrange("p (w f) -> p w f", f=D1)
            dve.wait_ge(lane_in[0], 16)
            dve.wait_ge(lane_in[1], 16)
            link(dve.tensor_tensor(acc[:, :, :], acc[:, :, :], aux[:, :, :], ALU.add))
            dve.sem_inc(s.lane_again, 1)
            dve.wait_ge(lane_in[2], 16)
            link(dve.tensor_tensor(acc[:, :, :], acc[:, :, :], tab_l, ALU.add))
            dve.wait_ge(lane_in[3], 16)
            link(dve.tensor_tensor(acc[:, :, :], acc[:, :, :], aux[:, :, :], ALU.add))
            sums_d = acc[:, :, 0:D]
            last_d = acc[:, :, D:D1].rearrange("p w a -> p (w a)")
            link(dve.tensor_scalar(col_a[:, :], last_d, 1.0, None, ALU.max))
            link(dve.reciprocal(col_b[:, :], col_a[:, :]))
            link(dve.tensor_tensor(sums_d, sums_d, bc(col_b[:, :].unsqueeze(2), [P, W, D]), ALU.mult))
            link(dve.tensor_tensor(sums_d, sums_d, x_n[:, :, :], ALU.add))
            norm(sums_d, 1)
            dve.sem_inc(s.node_in, 1)

            dve.sem_inc(s.stage_free, 2)

            def to_src_tab(c, k):
                dve.wait_ge(s.stage_free, c + 1)
                for k0 in range(0, WPC, 2):
                    k1 = min(k0 + 2, WPC)
                    pr = products(2, k0, k1, k)
                    last_stage = dve.tensor_copy(stage[:, WPC * k + k0:WPC * k + k1, :], pr[:, :, 0:2 * D])
                    last = dve.tensor_tensor(tab[:, bass.ds(c * WPC + k0, k1 - k0), :], pr[:, :, 2 * D:4 * D],
                                             bc(bias_d[:, :].unsqueeze(1), [P, k1 - k0, 2 * D]), ALU.add)
                last_stage.then_inc(s.stage_full, 1)
                last.then_inc(s.node_evacuated, 1)

            chunks(CHUNKS, to_src_tab)
            dve.wait_ge(s.stage_free, CHUNKS + 2)
            dve.sem_inc(s.node_in, 1)

            link(dve.memset(stat, 0.0))
            dve.sem_inc(s.l1_rows_used, 2)
            dve.sem_inc(s.l1_stored, 2)
            dve.sem_inc(s.l1_bank_free, 2)
            dve.sem_inc(s.l1_squared, 2)
            dve.sem_inc(s.l1_added, 1)
            dve.sem_inc(s.l1_sq_added, 2)
            got = [s.l1_got0, s.l1_got1]
            for b in range(2):
                one_hot(dve, ob[:, b, :, :], b).then_inc(s.l1_hot, 1)
            with dve.Fori(0, ITER) as i:
                for b in range(2):
                    dve.wait_ge(s.l1_transposed, i * 2 + (b + 1))
                    one_hot(dve, ob[:, b, :, :], i * 2 + (b + 2)).then_inc(s.l1_hot, 1)
                for b in range(2):
                    g = i * 2 + b
                    dve.wait_ge(s.l1_stored, g + 1)
                    dve.wait_ge(s.l1_products, g + 1)
                    dve.wait_ge(got[b], i * (G * 16) + G * 16)
                    dve.tensor_tensor(by_bank(buf_c[:, b, :, :]), ps[:, 4 + 2 * b:6 + 2 * b, :].rearrange("p c (k f) -> p c k f", f=P),
                                      by_bank(buf_b[:, b, :, :]), ALU.add).then_inc(s.l1_made, 1)
                    dve.wait_ge(s.l1_made, g + 1)
                    dve.sem_inc(s.l1_rows_used, 1)
                    dve.sem_inc(s.l1_bank_free, 1)
                    dve.wait_ge(s.l1_squared, g + 1)
                    dve.tensor_tensor(yv[:, b, :, :], buf_c[:, b, :, :], bc(step_slice(valid_s, g).unsqueeze(2), [P, G, P]),
                                      ALU.mult).then_inc(s.l1_masked, 1)
                    dve.wait_ge(s.l1_masked, g + 1)
                    dve.wait_ge(s.l1_added, g + 1)
                    dve.tensor_tensor(stat[:, 0, :, :], stat[:, 0, :, :], yv[:, b, :, :], ALU.add).then_inc(s.l1_added, 1)
                for b in range(2):
                    g = i * 2 + b
                    dve.wait_ge(s.l1_squared, g + 3)
                    dve.wait_ge(s.l1_sq_added, g + 2)
                    dve.tensor_tensor(stat[:, 1, :, :], stat[:, 1, :, :], sq[:, b, :, :], ALU.add).then_inc(s.l1_sq_added, 1)
            dve.wait_ge(s.l1_added, 2 * ITER + 1)
            dve.wait_ge(s.stat_done, 1)
            scale, shift, gam, bet, mean, var, std = (bn_col[:, k:k + 1] for k in (0, 1, 2, 3, 5, 6, 7))
            link(dve.tensor_scalar(mean, ps[:, 4, 0:1], 1.0 / E, None, ALU.mult))
            link(dve.tensor_scalar(var, ps[:, 5, 0:1], 1.0 / E, None, ALU.mult))
            link(dve.tensor_tensor(scale, mean, mean, ALU.mult))
            link(dve.tensor_tensor(var, var, scale, ALU.subtract))
            dve.tensor_scalar(var, var, 0.0, EPS, ALU.max, ALU.add).then_inc(s.bn_var, 1)
            dve.wait_ge(s.bn_made, 1)
            link(dve.reciprocal(var, std))
            link(dve.tensor_tensor(scale, var, gam, ALU.mult))
            link(dve.tensor_tensor(mean, mean, scale, ALU.mult))
            dve.tensor_tensor(shift, bet, mean, ALU.subtract).then_inc(s.bn_made, 1)
            dve.wait_ge(s.bn_spread, 1)
            link(dve.tensor_copy(bn[:, :, :].rearrange("p a b -> p (a b)"), ps[:, 6, 0:4 * D]))

            link(dve.tensor_scalar(bn[:, :, D:2 * D], bn[:, :, D:2 * D], -1.0, None, ALU.mult))

            def add_windows(g, bank, w0, n, order):
                a = acc_w[:, bass.ds(w0, G), 0:n]
                dve.wait_ge(order, g + 1)
                return dve.tensor_tensor(a, a, regions(bank, n), ALU.add).then_inc(order, 1)

            dve.wait_ge(s.l1_stored, 2 * ITER + 2)
            for half in range(2):
                link(dve.memset(lb_rows[half][:, :, :, D:D1], 1.0))
            dve.memset(acc_w[:, :, :], 0.0).then_inc(s.l1b_added, 1)
            dve.sem_inc(s.bn_ready, 1)
            dve.sem_inc(s.l1b_bank_free, 4)
            dve.sem_inc(s.l1b_slot_free, 4)

            def lb_add(g, q):
                w0 = load1(mybir.EngineType.DVE, win_s, g, W - 1)
                dve.wait_ge(s.l1b_sums, g + 1)
                add_windows(g, 2 * q, w0, D1, s.l1b_added)
                dve.wait_ge(s.l1b_added, g + 2)
                dve.sem_inc(s.l1b_bank_free, 1)

            def lb_pair(i, half, first):
                for b in range(2):
                    g = i * 2 + b
                    dve.wait_ge(s.l1b_normed, g * 2 + 2)
                    dve.wait_ge(s.l1b_slot_free, g + 3)
                    dve.tensor_scalar(buf_b[:, b, :, :], z_buf[:, 2 * half + b, :, :], 88.0, None, ALU.min).then_inc(s.l1b_clamped, 1)
                if not first:
                    for b in range(2):
                        lb_add(i * 2 + b - 4, 2 * half + b)
                for b in range(2):
                    one_hot(dve, lb_hot[half][:, b, :, :], i * 2 + b).then_inc(s.l1b_hot, 1)
                for b in range(2):
                    g = i * 2 + b
                    z = z_buf[:, 2 * half + b, :, 0:D]
                    dve.wait_ge(s.l1b_act, g * 3 + 3)
                    dve.tensor_tensor(z, z, buf_b[:, b, :, 0:D], ALU.max).then_inc(s.l1b_softplus, 1)
                for b in range(2):
                    g = i * 2 + b
                    z = z_buf[:, 2 * half + b, :, 0:D]
                    dve.wait_ge(s.l1b_softplus, g + 1)
                    dve.tensor_tensor(lb_rows[half][:, b, :, 0:D], z, buf_b[:, b, :, D:2 * D], ALU.mult).then_inc(s.l1b_messages, 1)
                for b in range(2):
                    dve.wait_ge(s.l1b_messages, i * 2 + b + 1)
                    dve.sem_inc(s.l1b_slot_free, 1)

            for half in range(2):
                lb_pair(half, half, True)
            with dve.Fori(1, ITER // 2) as i:
                for half in range(2):
                    lb_pair(i * 2 + half, half, False)
            for q in range(4):
                lb_add(2 * ITER - 4 + q, q)
            link(dve.tensor_copy(deg[:, :], last_d))
            link(dve.scalar_tensor_tensor(sums_d, x_n[:, :, :], 2.0, sums_d, ALU.mult, ALU.add))
            norm(sums_d, 2)
            dve.sem_inc(s.node_in, 1)

            link(dve.memset(stage[:, 0:2 * WPC, D:D1], 1.0))

            def to_att_tab(c, k):
                dve.wait_ge(s.stage_free, c + (CHUNKS + 1))
                for k0, k1 in ((0, 4), (4, 7)):
                    pr = products(4, k0, k1, k)
                    to = stage[:, WPC * k + k0:WPC * k + k1, :]
                    dve.tensor_copy(to[:, :, 0:D], pr[:, :, 0:D])
                    last_stage = dve.tensor_copy(to[:, :, D1:D2], pr[:, :, D:D1])
                    last = dve.tensor_copy(sums[:, bass.ds(c * WPC + k0, k1 - k0), 0:1], pr[:, :, D1:D2])
                last_stage.then_inc(s.stage_full, 1)
                last.then_inc(s.node_evacuated, 1)

            chunks(2 * CHUNKS, to_att_tab)
            dve.wait_ge(s.stage_free, 2 * CHUNKS + 2)
            dve.memset(mx[:, :], -BIG).then_inc(s.l2_max_kept, 1)
            dve.sem_inc(s.l2_bank_free, 2)
            dve.sem_inc(s.l2_rows_used, 2)
            with dve.Fori(0, ITER) as i:
                for b in range(2):
                    g = i * 2 + b
                    for u in range(G):
                        last = dve.tensor_scalar(buf_a[:, b, u, :], iota[:, :], step_col(dst_s, g, u), -BIG, ALU.not_equal, ALU.mult)
                    last.then_inc(s.l2_not_hot, 1)
                for b in range(2):
                    g = i * 2 + b
                    ws = load8(mybir.EngineType.DVE, win_s, g, W - 1)
                    dve.wait_ge(s.l2_scores, g + 1)
                    dve.tensor_reduce(tmp_c[:, b, :], regions(2 * b, P), AX.X, ALU.max).then_inc(s.l2_max, 1)
                    dve.wait_ge(s.l2_max, g + 1)
                    dve.sem_inc(s.l2_bank_free, 1)
                    for u in range(G):
                        m = mx[:, bass.ds(ws[u], 1)]
                        dve.wait_ge(s.l2_max_kept, g * G + (u + 1))
                        dve.tensor_tensor(m, m, tmp_c[:, b, u:u + 1], ALU.max).then_inc(s.l2_max_kept, 1)
            dve.wait_ge(s.l2_max_kept, S + 1)
            sc, mxc = sums[:, :, 0:1].rearrange("p w a -> p (w a)"), sums[:, :, 1:2].rearrange("p w a -> p (w a)")
            link(dve.tensor_tensor(col_a[:, :], mx[:, :], sc, ALU.add))
            link(dve.scalar_tensor_tensor(mxc, col_a[:, :], 0.2, col_a[:, :], ALU.mult, ALU.max))
            rest = col_b[:, :]
            for k, v in enumerate((sc, mxc)):
                for part in range(3):
                    v_b = sums_b[:, :, 2 * part + k:2 * part + k + 1].rearrange("p w a -> p (w a)")
                    link(dve.tensor_copy(v_b, v if part == 0 else rest))
                    if part < 2:
                        link(dve.tensor_tensor(rest, v if part == 0 else rest, v_b, ALU.subtract))
            dve.sem_inc(s.max_done, 1)

            dve.memset(acc_w[:, :, :], 0.0).then_inc(s.l2b_added, 1)
            dve.sem_inc(s.l2b_rows_used, 4)
            dve.sem_inc(s.l2b_sums, 2)
            dve.sem_inc(s.l2b_bank_free, 2)
            KL2 = 4

            def l2b_scores(i, half, turn):
                k = 0

                def chain(ins):
                    nonlocal k
                    k += 1
                    ins.then_inc(s.l2b_chain, 1)
                    dve.wait_ge(s.l2b_chain, i * KL2 + k)
                per_edge = ps[:, 2, 0:6 * PAIR].rearrange("p (v q k) -> p v k q", k=2, q=3)
                score = tmp_c[:, 0:2, :].rearrange("p b u -> p (b u)")
                st = target[:, :, :, :].rearrange("p b u k -> p (b u) k")
                dve.wait_ge(s.l2b_targets, i * 2 + 2)
                chain(dve.tensor_reduce(st, per_edge, AX.X, ALU.add))
                for b in range(2):
                    dve.wait_ge(h_in[2 * half + b], turn * 16 + 16)
                chain(dve.tensor_tensor(score, l2b_h[half][:, :, :, D1:D2].rearrange("p b u a -> p (b u a)"),
                                        st[:, :, 0:1].rearrange("p v a -> p (v a)"), ALU.add))
                chain(dve.scalar_tensor_tensor(score, score, 0.2, score, ALU.mult, ALU.max))
                chain(dve.tensor_tensor(score, score, st[:, :, 1:2].rearrange("p v a -> p (v a)"), ALU.subtract))
                dve.tensor_scalar(tmp_c[:, 2:4, :].rearrange("p b u -> p (b u)"), score, 0.0, None, ALU.min).then_inc(s.l2b_args, 1)
                assert k == KL2

            def l2b_add(g, b):
                w0 = load1(mybir.EngineType.DVE, win_s, g, W - 1)
                dve.wait_ge(s.l2b_sums, g + 3)
                add_windows(g, 4 + 2 * b, w0, D1, s.l2b_added)
                dve.wait_ge(s.l2b_added, g + 2)
                dve.sem_inc(s.l2b_bank_free, 1)

            def l2b_pair(i, half, turn, first, last):
                l2b_scores(i, half, turn)
                if not last:
                    if not first:
                        dve.wait_ge(s.l2b_hot_copied, i * 2)
                    for b in range(2):
                        one_hot(dve, ob4[:, 2 * (1 - half) + b, :, :], i * 2 + (b + 2)).then_inc(s.l2b_hot, 1)
                if not first:
                    l2b_add(i * 2 - 2, 0)
                dve.wait_ge(s.l2b_weights, i + 1)
                for b in range(2):
                    dve.tensor_tensor(l2b_rows[half][:, b, :, 0:D1], l2b_h[half][:, b, :, 0:D1],
                                      bc(ex[:, b, :].unsqueeze(2), [P, G, D1]), ALU.mult).then_inc(s.l2b_weighted, 1)
                if not first:
                    l2b_add(i * 2 - 1, 1)
                for b in range(2):
                    dve.wait_ge(s.l2b_weighted, i * 2 + b + 1)
                    dve.sem_inc(s.l2b_rows_used, 1)

            for b in range(2):
                one_hot(dve, ob4[:, b, :, :], b).then_inc(s.l2b_hot, 1)
            l2b_pair(0, 0, 0, True, False)
            with dve.Fori(0, ITER // 2 - 1) as i:
                for half in (1, 0):
                    l2b_pair(i * 2 + (2 - half), half, i + (1 - half), False, False)
            l2b_pair(ITER - 1, 1, ITER // 2 - 1, False, True)
            for b in range(2):
                l2b_add(2 * ITER - 2 + b, b)
            link(dve.tensor_scalar(col_a[:, :], last_d, 1e-30, None, ALU.max))
            link(dve.reciprocal(col_b[:, :], col_a[:, :]))
            link(dve.tensor_tensor(sums_d, sums_d, bc(col_b[:, :].unsqueeze(2), [P, W, D]), ALU.mult))
            dve.tensor_scalar(scratch, sums_d, 0.0, None, ALU.min).then_inc(s.elu_in, 1)
            link(dve.scalar_tensor_tensor(sums_d, sums_d, 0.0, x_n[:, :, :], ALU.max, ALU.add))
            dve.wait_ge(s.elu_out, 1)
            link(dve.scalar_tensor_tensor(sums_d, scratch, -1.0, sums_d, ALU.add, ALU.add))
            norm(sums_d, 3)
            dinv = mx[:, :]
            dve.tensor_scalar(col_a[:, :], deg[:, :], 1.0, None, ALU.max).then_inc(s.norm_var, 1)
            dve.wait_ge(s.norm_std, 4)
            link(dve.reciprocal(col_b[:, :], col_b[:, :]))
            link(dve.scalar_tensor_tensor(dinv, deg[:, :], 0.0, col_b[:, :], ALU.is_gt, ALU.mult))
            dinv_bc = bc(mx[:, :].unsqueeze(2), [P, W, D])

            link(dve.tensor_tensor(tab_d, x_n[:, :, :], dinv_bc, ALU.mult))
            dve.sem_inc(s.gcn_in0, 1)

            def to_acc(c, k, conv):
                for k0, k1 in ((0, 4), (4, 7)):
                    last = dve.tensor_tensor(acc[:, bass.ds(c * WPC + k0, k1 - k0), 0:D], products(4, k0, k1, k)[:, :, 0:D],
                                             bc(bias3[:, conv:conv + 1, :], [P, k1 - k0, D]), ALU.add)
                last.then_inc(s.node_evacuated, 1)

            def gcn(got, o, outs, accfree, gfree, order):
                dve.memset(acc_w[:, :, :], 0.0).then_inc(order, 1)
                dve.sem_inc(accfree, 2)
                dve.sem_inc(gfree, 2)
                dve.sem_inc(outs, 2)
                with dve.Fori(0, ITER) as i:
                    for b in range(2):
                        g = i * 2 + b
                        dve.wait_ge(outs, g + 1)
                        one_hot(dve, buf_a[:, b, :, :], g).then_inc(o, 1)
                    for b in range(2):
                        g = i * 2 + b
                        w0 = load1(mybir.EngineType.DVE, win_s, g, W - 1)
                        dve.wait_ge(outs, g + 3)
                        dve.sem_inc(gfree, 1)
                        add_windows(g, 2 * b, w0, D, order)
                        dve.wait_ge(order, g + 2)
                        dve.sem_inc(accfree, 1)

            gcn([s.g0_got0, s.g0_got1], s.g0_hot, s.g0_sums, s.g0_bank_free, s.g0_rows_used, s.g0_added)
            dve.wait_ge(s.gcn_stored0, 16)
            link(dve.tensor_tensor(tab_d, sums_d, dinv_bc, ALU.mult))
            dve.sem_inc(s.node_in, 1)
            chunks(3 * CHUNKS, lambda c, k: to_acc(c, k, 0))
            link(dve.scalar_tensor_tensor(tab_d, sums_d, 0.0, dinv_bc, ALU.max, ALU.mult))
            dve.sem_inc(s.gcn_in1, 1)
            gcn([s.g1_got0, s.g1_got1], s.g1_hot, s.g1_sums, s.g1_bank_free, s.g1_rows_used, s.g1_added)
            dve.wait_ge(s.gcn_stored1, 16)
            link(dve.tensor_tensor(tab_d, sums_d, dinv_bc, ALU.mult))
            dve.sem_inc(s.node_in, 1)
            chunks(4 * CHUNKS, lambda c, k: to_acc(c, k, 1))
            link(dve.tensor_tensor(sums_d, sums_d, x_n[:, :, :], ALU.add))
            norm(sums_d, 5, s.result_ready)


_INS = ['x', 'src', 'dst', 'edge_attr_16', 'edge_attr_64', 'L0_gnn_W_edge', 'L0_gnn_b_edge', 'L0_gnn_W_node', 'L0_gnn_b_node',
        'L1_gnn_W_filter', 'L1_gnn_b_filter', 'L1_gnn_gamma_filter', 'L1_gnn_beta_filter',
        'L1_gnn_W_core', 'L1_gnn_b_core', 'L1_gnn_gamma_core', 'L1_gnn_beta_core',
        'L2_gnn_W', 'L2_gnn_a', 'L3_gnn_W1', 'L3_gnn_b1', 'L3_gnn_W2', 'L3_gnn_b2']


def kernel(**inputs):
    import numpy as _np
    import concourse.bacc as _bacc
    from concourse import mybir as _mybir
    from concourse.bass_utils import run_bass_kernel_spmd as _run

    nc = _bacc.Bacc("TRN2", target_bir_lowering=False, num_devices=1)
    arrays, args = {}, []
    for name in _INS:
        a = _np.ascontiguousarray(inputs[name])
        arrays[f"in_{name}_dram"] = a
        args.append(nc.dram_tensor(f"in_{name}_dram", a.shape, _mybir.dt.from_np(a.dtype), kind="ExternalInput").ap())
    out = nc.dram_tensor("out_dram", (N, D), _mybir.dt.float32, kind="ExternalOutput").ap()
    build(nc, *args, out)
    r = _run(nc, [arrays], core_ids=[0])
    return r.results[0]["out_dram"]
```
